# Optimizing a Trainium2 kernel written in Bass

```python
import numpy as np
import jax
import jax.numpy as jnp

def _softmax(x, axis=-1):
    return jax.nn.softmax(x, axis=axis)

def _gelu(x):
    return jax.nn.gelu(x, approximate=True)

def _silu(x):
    return jax.nn.silu(x)

def _sigmoid(x):
    return jax.nn.sigmoid(x)

def _layernorm(x, axis=-1, eps=1e-05):
    m = jnp.mean(x, axis=axis, keepdims=True)
    v = jnp.var(x, axis=axis, keepdims=True)
    return (x - m) / jnp.sqrt(v + eps)

def _scatter_add(tgt, idx, src, axis=0):
    return tgt.at[idx].add(src)

def _segment_sum(src, seg, n):
    return jax.ops.segment_sum(src, seg, n)
kernel_name = 'mk_flamingo_gated_d1_seqx_r4_3dceea'

def setup_inputs(seed: int=0):
    np.random.seed(seed)
    _w = jnp.asarray

    def _rec_inputs():
        import jax
        import jax.numpy as jnp
        _rk = jax.random.key(seed)
        x = 7.22e-05 + 1 * jax.random.normal(jax.random.fold_in(_rk, 1), (2, 1024, 256), jnp.float32)
        _lenS = 1024 - jax.random.randint(jax.random.fold_in(_rk, 7), (2,), 0, max(1, 1024 // 4) + 1, jnp.int32)
        _lenS2 = 64 - jax.random.randint(jax.random.fold_in(_rk, 8), (2,), 0, max(1, 64 // 4) + 1, jnp.int32)
        _ctx_1024P = jax.random.normal(jax.random.fold_in(_rk, 11), (2, 16, 256), jnp.float32)
        _ctx_1024c = jax.random.dirichlet(jax.random.fold_in(_rk, 511), 0.3 * jnp.ones((16,), jnp.float32), (2, 64))
        _ctx_1024t = jnp.einsum('bsk,bkd->bsd', _ctx_1024c, _ctx_1024P)
        _ctx_1024t = _ctx_1024t * jax.lax.rsqrt(jnp.mean(jnp.square(_ctx_1024t)) + 1e-12) * 0.953939
        ctx_1024 = 4.13588e-05 + 0.999923 * (_ctx_1024t + 0.3 * jax.random.normal(jax.random.fold_in(_rk, 611), (2, 64, 256), jnp.float32))
        _g = jax.random.normal(jax.random.fold_in(_rk, 9001), (2, 1), jnp.float32)
        _g = jnp.sign(_g) * jnp.maximum(jnp.abs(_g), 1.0) + (_g == 0) * 1.0
        g_xattn = _g[0]
        g_ffn = _g[1]
        return (x, ctx_1024, g_xattn, g_ffn)
    x, ctx_1024, g_xattn, g_ffn = _rec_inputs()

    def _L0_xattn_setup():
        import jax, jax.numpy as jnp
        import numpy as np
        B, S, D, H, DH = (4, 512, 256, 16, 64)
        key = jax.random.key(seed)
        ks = jax.random.split(key, 8)
        scale = 1.0 / np.sqrt(D)
        return {'inputs_q': jax.random.normal(ks[0], (B, S, D), jnp.float32), 'inputs_kv': jax.random.normal(ks[1], (B, S, D), jnp.float32), 'Wq': jax.random.normal(ks[2], (D, H, DH), jnp.float32) * scale, 'bq': jnp.zeros((H, DH), jnp.float32), 'Wk': jax.random.normal(ks[3], (D, H, DH), jnp.float32) * scale, 'bk': jnp.zeros((H, DH), jnp.float32), 'Wv': jax.random.normal(ks[4], (D, H, DH), jnp.float32) * scale, 'bv': jnp.zeros((H, DH), jnp.float32), 'Wo': jax.random.normal(ks[5], (H, DH, D), jnp.float32) * (1.0 / np.sqrt(H * DH)), 'bo': jnp.zeros((D,), jnp.float32)}
    _L0_xattn_all = _L0_xattn_setup()
    _L0_xattn_in = {k: v for k, v in _L0_xattn_all.items() if k in ('Wq', 'bq', 'Wk', 'bk', 'Wv', 'bv', 'Wo', 'bo')}
    del _L0_xattn_all

    def _L0_ffn_setup():
        import jax, jax.numpy as jnp
        import numpy as np
        TOP_K = 2
        ROUTE_SCALE = 1.0
        EPS = 1e-20
        B, S, D = (2, 128, 256)
        E = 8
        F = 192
        FS = 192 * 1
        key = jax.random.key(seed)
        ks = jax.random.split(key, 9)
        s = 0.02
        return {'hidden_states': jax.random.normal(ks[0], (B, S, D), dtype=jnp.float32), 'W_gate_router': jax.random.normal(ks[1], (D, E), dtype=jnp.float32) * s, 'expert_bias': jnp.zeros((E,), dtype=jnp.float32), 'Wg': jax.random.normal(ks[2], (E, D, F), dtype=jnp.float32) * s, 'Wu': jax.random.normal(ks[3], (E, D, F), dtype=jnp.float32) * s, 'Wd': jax.random.normal(ks[4], (E, F, D), dtype=jnp.float32) * s, 'Wg_s': jax.random.normal(ks[5], (D, FS), dtype=jnp.float32) * s, 'Wu_s': jax.random.normal(ks[6], (D, FS), dtype=jnp.float32) * s, 'Wd_s': jax.random.normal(ks[7], (FS, D), dtype=jnp.float32) * s}
    _L0_ffn_all = _L0_ffn_setup()
    _L0_ffn_in = {k: v for k, v in _L0_ffn_all.items() if k in ('W_gate_router', 'expert_bias', 'Wg', 'Wu', 'Wd', 'Wg_s', 'Wu_s', 'Wd_s')}
    del _L0_ffn_all
    return {'x': x, 'ctx_1024': ctx_1024, 'g_xattn': g_xattn, 'g_ffn': g_ffn, 'L0_xattn_Wq': _L0_xattn_in['Wq'], 'L0_xattn_bq': _L0_xattn_in['bq'], 'L0_xattn_Wk': _L0_xattn_in['Wk'], 'L0_xattn_bk': _L0_xattn_in['bk'], 'L0_xattn_Wv': _L0_xattn_in['Wv'], 'L0_xattn_bv': _L0_xattn_in['bv'], 'L0_xattn_Wo': _L0_xattn_in['Wo'], 'L0_xattn_bo': _L0_xattn_in['bo'], 'L0_ffn_W_gate_router': _L0_ffn_in['W_gate_router'], 'L0_ffn_expert_bias': _L0_ffn_in['expert_bias'], 'L0_ffn_Wg': _L0_ffn_in['Wg'], 'L0_ffn_Wu': _L0_ffn_in['Wu'], 'L0_ffn_Wd': _L0_ffn_in['Wd'], 'L0_ffn_Wg_s': _L0_ffn_in['Wg_s'], 'L0_ffn_Wu_s': _L0_ffn_in['Wu_s'], 'L0_ffn_Wd_s': _L0_ffn_in['Wd_s']}

def reference(x, ctx_1024, g_xattn, g_ffn, L0_xattn_Wq, L0_xattn_bq, L0_xattn_Wk, L0_xattn_bk, L0_xattn_Wv, L0_xattn_bv, L0_xattn_Wo, L0_xattn_bo, L0_ffn_W_gate_router, L0_ffn_expert_bias, L0_ffn_Wg, L0_ffn_Wu, L0_ffn_Wd, L0_ffn_Wg_s, L0_ffn_Wu_s, L0_ffn_Wd_s):
    import jax
    import jax.numpy as jnp

    def _L0_xattn_ref(inputs_q, inputs_kv, Wq, bq, Wk, bk, Wv, bv, Wo, bo):
        import jax, jax.numpy as jnp
        import numpy as np
        B, S, D, H, DH = (4, 512, 256, 16, 64)
        q = jnp.einsum('bsd,dhf->bshf', inputs_q, Wq) + bq
        k = jnp.einsum('bsd,dhf->bshf', inputs_kv, Wk) + bk
        v = jnp.einsum('bsd,dhf->bshf', inputs_kv, Wv) + bv
        q = q / jnp.sqrt(jnp.asarray(DH, q.dtype))
        scores = jnp.einsum('bqhf,bkhf->bhqk', q, k)
        probs = jax.nn.softmax(scores, axis=-1)
        x = jnp.einsum('bhqk,bkhf->bqhf', probs, v)
        out = jnp.einsum('bqhf,hfd->bqd', x, Wo) + bo
        return out

    def _L0_ffn_ref(hidden_states, W_gate_router, expert_bias, Wg, Wu, Wd, Wg_s, Wu_s, Wd_s):
        import jax, jax.numpy as jnp
        import numpy as np
        TOP_K = 2
        ROUTE_SCALE = 1.0
        EPS = 1e-20
        B, S, D = (2, 128, 256)
        E = 8
        F = 192
        FS = 192 * 1
        b, s, d = hidden_states.shape
        x = hidden_states.reshape(-1, d)
        T = x.shape[0]
        logits = x @ W_gate_router
        scores = jax.nn.sigmoid(logits.astype(jnp.float32))
        _, sel = jax.lax.top_k(scores + expert_bias, TOP_K)
        top_scores = jnp.take_along_axis(scores, sel, axis=1)
        top_scores = top_scores / (top_scores.sum(-1, keepdims=True) + EPS)
        top_scores = top_scores * ROUTE_SCALE
        shared = jax.nn.silu(x @ Wg_s) * (x @ Wu_s) @ Wd_s
        tok = jnp.repeat(jnp.arange(T), TOP_K)
        exp = sel.reshape(-1)
        w = top_scores.reshape(-1)
        xr = x[tok]
        h = jax.nn.silu(jnp.einsum('nd,edf->enf', xr, Wg)) * jnp.einsum('nd,edf->enf', xr, Wu)
        out_all = jnp.einsum('enf,efd->end', h, Wd)
        routed = out_all[exp, jnp.arange(exp.shape[0])]
        routed = (routed.astype(jnp.float32) * w[:, None]).astype(hidden_states.dtype)
        out = shared.at[tok].add(routed)
        return out.reshape(b, s, d)
    x = x + jnp.tanh(g_xattn[0]) * _L0_xattn_ref(_layernorm(x, axis=-1), ctx_1024, L0_xattn_Wq, L0_xattn_bq, L0_xattn_Wk, L0_xattn_bk, L0_xattn_Wv, L0_xattn_bv, L0_xattn_Wo, L0_xattn_bo)
    x = x + jnp.tanh(g_ffn[0]) * _L0_ffn_ref(_layernorm(x, axis=-1), L0_ffn_W_gate_router, L0_ffn_expert_bias, L0_ffn_Wg, L0_ffn_Wu, L0_ffn_Wd, L0_ffn_Wg_s, L0_ffn_Wu_s, L0_ffn_Wd_s)
    return x

_drawn_inputs = setup_inputs


def setup_inputs(seed=0):
    import zlib

    import numpy as np

    out = dict(_drawn_inputs(seed))
    spreads = {'L0_xattn_bq': (0.0, 0.422),
     'L0_xattn_bk': (0.0, 0.8),
     'L0_xattn_bv': (0.0, 0.1),
     'L0_xattn_bo': (0.0, 0.1),
     'L0_ffn_expert_bias': (0.0, 0.8)}
    factors = {'L0_ffn_W_gate_router': 8.0,
     'L0_ffn_Wg': 6.401,
     'L0_ffn_Wu': 6.343,
     'L0_ffn_Wd': 6.35,
     'L0_ffn_Wg_s': 4.548,
     'L0_ffn_Wu_s': 4.49,
     'L0_ffn_Wd_s': 4.486}
    for name, (base, spread) in spreads.items():
        noise = np.random.default_rng([zlib.crc32(name.encode()), seed]).standard_normal(out[name].shape)
        drawn = base * np.exp(spread * noise) if base else spread * noise
        out[name] = jnp.asarray(drawn.astype(out[name].dtype))
    for name, factor in factors.items():
        out[name] = (out[name] * factor).astype(out[name].dtype)
    return out
```

```python
from contextlib import ExitStack

import concourse.bass as bass
from concourse import mybir

F32 = mybir.dt.float32
F32R = mybir.dt.float32r
I32 = mybir.dt.int32
ALU = mybir.AluOpType
ACT = mybir.ActivationFunctionType
AX_X = mybir.AxisListType.X

P = 128
B, SEQ, D = 2, 1024, 256
KV = 64
H, DH = 16, 64
HP = H // 2
HK = H * KV
KC = D // P
E, F = 8, 192
FH = F // 2
TOKENS = B * SEQ
T = TOKENS // P
TB = SEQ // P
TOPK = 2
SLOT_TILES = (TOKENS * TOPK + E * (P - 1)) // P
Q = SLOT_TILES + 1
RING = 4
LN_EPS = 1e-5
ROUTE_EPS = 1e-20
FAR = 8192.0
BIG = 3.0e38


def flamingo_layer(nc, x, ctx_kv, g_xattn, g_ffn, Wq, bq, Wk, bk, Wv, bv, Wo, bo,
                   W_router, expert_bias, Wg, Wu, Wd, Wg_s, Wu_s, Wd_s, out):
    stack = ExitStack()
    with stack:
        def sb(name, shape, dt=F32):
            return stack.enter_context(nc.sbuf_tensor(name, shape, dt))

        def sem(name):
            return stack.enter_context(nc.semaphore(name))

        x_sb = sb("x_sb", [P, T, D])
        A_hi = sb("A_hi", [P, B, KC, HK], F32R)
        A_lo = sb("A_lo", [P, B, KC, HK], F32R)
        B_hi = sb("B_hi", [P, B, HP, D], F32R)
        B_lo = sb("B_lo", [P, B, HP, D], F32R)
        score_bias = sb("score_bias", [P, B, HK], F32R)
        pick_rows = sb("pick_rows", [P, P], F32R)
        Wsh_hi = sb("Wsh_hi", [P, KC, 2 * F + E], F32R)
        Wsh_lo = sb("Wsh_lo", [P, KC, 2 * F + E], F32R)
        Wds_hi = sb("Wds_hi", [FH, 2, D], F32R)
        Wds_lo = sb("Wds_lo", [FH, 2, D], F32R)

        ident = sb("ident", [P, P])
        bo_row = sb("bo_row", [P, D])
        gates = sb("gates", [P, 2])
        tgate = sb("tgate", [P, 2])
        half_tgf = sb("half_tgf", [P, 1])
        minus_half = sb("minus_half", [P, T])
        stats1 = sb("stats1", [P, T, 6])
        mv1 = sb("mv1", [P, T, 2])
        ve1 = sb("ve1", [P, T])
        rstd1 = sb("rstd1", [P, T])
        shift1 = sb("shift1", [P, T])
        xn = [sb(f"xn{q}", [P, D]) for q in range(2)]
        xnT_hi = [sb(f"xnT_hi{q}", [P, KC, P], F32R) for q in range(2)]
        xnT_lo = [sb(f"xnT_lo{q}", [P, KC, P], F32R) for q in range(2)]
        prob = [sb(f"prob{q}", [P, HK]) for q in range(2)]
        row_max = sb("row_max", [P, H])
        row_sum = sb("row_sum", [P, H])
        row_inv = sb("row_inv", [P, H])
        pT_hi = sb("pT_hi", [P, HP, P], F32R)
        pT_lo = sb("pT_lo", [P, HP, P], F32R)
        stats2 = sb("stats2", [P, 6])
        mv2 = sb("mv2", [P, 2])
        ve2 = sb("ve2", [P, 1])
        neg_mean2 = sb("neg_mean2", [P, 1])
        eps_col = sb("eps_col", [P, 1])
        minus_one = sb("minus_one", [P, 1])
        carrier = sb("carrier", [P, 1])
        rstd2 = sb("rstd2", [P, 1])
        shift2 = sb("shift2", [P, 1])
        xn2 = [sb(f"xn2_{q}", [P, D]) for q in range(2)]
        xn2T_hi = [sb(f"xn2T_hi{q}", [P, KC, P], F32R) for q in range(2)]
        xn2T_lo = [sb(f"xn2T_lo{q}", [P, KC, P], F32R) for q in range(2)]
        tanh_g = sb("tanh_g", [P, F])
        gate_act = sb("gate_act", [P, F])
        hid = sb("hid", [P, F])
        hT_hi = sb("hT_hi", [FH, 2, P], F32R)
        hT_lo = sb("hT_lo", [FH, 2, P], F32R)
        iota_e = sb("iota_e", [P, E])
        iota_e8 = sb("iota_e8", [P, E])
        iota_q = sb("iota_q", [P, Q])
        iota_p = sb("iota_p", [P, P])
        pair_row = sb("pair_row", [P, TOPK * T])
        upper_f = sb("upper_f", [P, P])
        upper = sb("upper", [P, P], F32R)
        ones_r = sb("ones_r", [P, P], F32R)
        not_after = sb("not_after", [P, E, E])
        expert_b = sb("expert_b", [P, E])
        score = sb("score", [P, T, E])
        choice = sb("choice", [P, T, E])
        best = sb("best", [P, T])
        cand = sb("cand", [P, T, E])
        first_e = sb("first_e", [P, T])
        hot = [sb(f"hot{k}", [P, T, E]) for k in range(TOPK)]
        mask = sb("mask", [P, T, E], F32R)
        mask_sum = sb("mask_sum", [P, E])
        picked = [sb(f"picked{k}", [P, T]) for k in range(TOPK)]
        weight = [sb(f"weight{k}", [P, T]) for k in range(TOPK)]
        den = sb("den", [P, T])
        count_i = sb("count_i", [P, E], I32)
        tiles_f = sb("tiles_f", [P, E])
        end_prod = sb("end_prod", [P, E, E])
        end_f = sb("end_f", [P, E])
        start_f = sb("start_f", [P, E])
        slot = sb("slot", [P, TOPK, T])
        slot_i = sb("slot_i", [P, TOPK * T], I32)
        slot_p = sb("slot_p", [P, TOPK * T])
        slot_q = sb("slot_q", [P, TOPK * T])
        part_i = sb("part_i", [P, TOPK * T], I32)
        table = sb("table", [P, Q])
        pad_far = sb("pad_far", [P, Q])
        src_i = sb("src_i", [P, Q], I32)
        dst_i = sb("dst_i", [P, Q], I32)
        zero_i = sb("zero_i", [P, 1], I32)
        tile_cmp = sb("tile_cmp", [1, Q, E])
        tile_e = sb("tile_e", [1, Q])
        tile_row = sb("tile_row", [1, Q], I32)
        gat_idx = [sb(f"gat_idx{k}", [P, 1], I32) for k in range(RING)]
        sct_idx = [sb(f"sct_idx{k}", [P, 1], I32) for k in range(RING)]
        xg = [sb(f"xg{k}", [P, D]) for k in range(RING)]
        y_sb = [sb(f"y_sb{k}", [P, D]) for k in range(RING)]
        exp_neg = sb("exp_neg", [P, T, E])

        fold = ExitStack()

        def fb(name, shape, dt=F32):
            return fold.enter_context(nc.sbuf_tensor(name, shape, dt))

        Wk_sb = fb("Wk_sb", [P, KC, H * DH])
        Wq_sb = fb("Wq_sb", [P, KC, H * DH])
        Wv_sb = fb("Wv_sb", [P, KC, H * DH])
        Wo_sb = fb("Wo_sb", [P, HP, D])
        WqT = fb("WqT", [P, HP, D])
        ctx_sb = fb("ctx_sb", [P, D])
        ctxT = fb("ctxT", [P, KC, P])
        bias_rows = fb("bias_rows", [3 * HP, P])
        bias_cols = fb("bias_cols", [P, 3 * HP])
        kT = fb("kT", [P, HP, P])
        vT = fb("vT", [P, HP, P])
        raw_sh = fb("raw_sh", [P, KC, 2 * F + E])
        raw_ds = fb("raw_ds", [FH, 2, D])
        fold.close()
        W_hi = sb("W_hi", [P, E * KC, 2 * F], F32R)
        W_lo = sb("W_lo", [P, E * KC, 2 * F], F32R)
        raw_buf = [sb(f"raw_buf{q}", [P, 4 * D]) for q in range(2)]
        raw_w = [r[:, 0:KC * 2 * F].rearrange("p (k f) -> p k f", k=KC) for r in raw_buf]
        raw_d = [r[0:FH, :].rearrange("p (n d) -> p n d", d=D) for r in raw_buf]
        Wd_hi = A_hi[0:FH, :, :, :].rearrange("p b k (c d) -> p (b k c) d", d=D)
        Wd_lo = A_lo[0:FH, :, :, :].rearrange("p b k (c d) -> p (b k c) d", d=D)

        routed_in = [r[:, :].rearrange("p (t d) -> p t d", d=D) for r in raw_buf]
        onehot_p = B_hi[:, :, :, :].rearrange("p b c d -> p (b c d)").rearrange("p (n s) -> p n s", s=P)
        onehot_q = B_lo[:, :, :, :].rearrange("p b c d -> p (b c d)")[:, 0:TOPK * T * Q].rearrange("p (n s) -> p n s", s=Q)
        bank = [stack.enter_context(nc.psum_tensor(f"bank{i}", [P, 512], F32)) for i in range(2, 8)]
        scores_ps = stack.enter_context(nc.psum_tensor("scores_ps", [P, HK], F32))
        pT_ps = bank[0:2]
        att_ps, xT_ps, h_ps, hy_ps = bank[2], bank[3], bank[4], bank[5]

        rank_ps = bank[4][:, 0:T * E].rearrange("p (t e) -> p t e", e=E)
        count_ps = bank[5][:, 0:E]
        table_ps = bank[3][:, 0:Q]
        gT_ps = [bank[3], bank[2]]
        eh_ps = [bank[4], scores_ps[:, 0:512]]
        ehT_ps = [bank[5], scores_ps[:, 512:1024]]
        ey_ps = [bank[0], bank[1]]

        xn2_dram = nc.dram_tensor("xn2_dram", [TOKENS, D], F32, kind="Internal").ap()
        routed_dram = nc.dram_tensor("routed_dram", [TOPK * TOKENS, D], F32, kind="Internal").ap()

        ld_kv = sem("ld_kv")
        ld_q = sem("ld_q")
        ld_x = [sem("ld_x0"), sem("ld_x1")]
        ld_vo = sem("ld_vo")
        ld_misc = sem("ld_misc")
        ld_sh = sem("ld_sh")
        ld_d = [sem("ld_d0"), sem("ld_d1")]
        pool_held = sem("pool_held")
        const_route = sem("const_route")
        route_step = sem("route_step")
        mask_done = sem("mask_done")
        rank_ps_done = sem("rank_ps_done")
        onehot_done = sem("onehot_done")
        table_ps_done = sem("table_ps_done")
        src_done = sem("src_done")
        dst_done = sem("dst_done")
        tile_row_done = sem("tile_row_done")
        wd_hi_done = sem("wd_hi_done")
        wd_lo_done = sem("wd_lo_done")
        gat_idx_done = sem("gat_idx_done")
        sct_idx_done = sem("sct_idx_done")
        gathered = [sem(f"gathered{k}") for k in range(RING)]
        scattered = [sem(f"scattered{k}") for k in range(RING)]
        gT_done = sem("gT_done")
        gT_hi_done = sem("gT_hi_done")
        gT_lo_done = sem("gT_lo_done")
        eh_done = sem("eh_done")
        esilu_done = sem("esilu_done")
        ehid_done = sem("ehid_done")
        ehT_done = sem("ehT_done")
        ehT_hi_done = sem("ehT_hi_done")
        ehT_lo_done = sem("ehT_lo_done")
        ey_done = sem("ey_done")
        ycopy_done = sem("ycopy_done")
        routed_loaded = [sem("routed_loaded0"), sem("routed_loaded1")]
        add_step = sem("add_step")
        const_step = sem("const_step")
        const_pick = sem("const_pick")
        gates_done = sem("gates_done")
        ctxT_ps = sem("ctxT_ps")
        ctxT_done = sem("ctxT_done")
        kv_ps = sem("kv_ps")
        kv_done = sem("kv_done")
        wqT_ps = sem("wqT_ps")
        wqT_done = sem("wqT_done")
        A_ps = sem("A_ps")
        A_hi_done = sem("A_hi_done")
        A_done = sem("A_done")
        sbias_ps = sem("sbias_ps")
        sbias_hi = sem("sbias_hi")
        sbias_done = sem("sbias_done")
        B_ps = sem("B_ps")
        B_hi_done = sem("B_hi_done")
        B_done = sem("B_done")
        wsh_hi_done = sem("wsh_hi_done")
        wsh_done = sem("wsh_done")
        stats1_done = sem("stats1_done")
        mv1_done = sem("mv1_done")
        ln1_step = sem("ln1_step")
        xn_done = sem("xn_done")
        xb_done = sem("xb_done")
        xT_done = sem("xT_done")
        xT_hi_done = sem("xT_hi_done")
        xT_lo_done = sem("xT_lo_done")
        scores_done = sem("scores_done")
        max_done = sem("max_done")
        sub_done = sem("sub_done")
        exp_done = sem("exp_done")
        sum_done = sem("sum_done")
        inv_done = sem("inv_done")
        norm_done = sem("norm_done")
        pT_done = sem("pT_done")
        pT_hi_done = sem("pT_hi_done")
        pT_lo_done = sem("pT_lo_done")
        att_done = sem("att_done")
        x2_done = sem("x2_done")
        stats2_done = sem("stats2_done")
        mv2_done = sem("mv2_done")
        ln2_step = sem("ln2_step")
        xn2_done = sem("xn2_done")
        xn2_stored = [sem("xn2_stored0"), sem("xn2_stored1")]
        x2T_done = sem("x2T_done")
        x2T_hi_done = sem("x2T_hi_done")
        x2T_lo_done = sem("x2T_lo_done")
        h_done = sem("h_done")
        logit_done = sem("logit_done")
        tanh_done = sem("tanh_done")
        gact_done = sem("gact_done")
        hid_done = sem("hid_done")
        hT_done = sem("hT_done")
        hT_hi_done = sem("hT_hi_done")
        hT_lo_done = sem("hT_lo_done")
        y_done = sem("y_done")
        yadd_done = sem("yadd_done")
        raw_loaded = [sem("raw_loaded0"), sem("raw_loaded1")]
        w_hi_done = sem("w_hi_done")
        w_lo_done = sem("w_lo_done")
        out_stored = sem("out_stored")

        NG = 2
        GC = HP // NG

        def token_loop(eng, step):
            for t in range(-3, 4):
                step(t, t % 2, None)
            with eng.Fori(0, E // 2) as i:
                for k in range(2):
                    step(4 + 2 * i + k, k, i)
            for t in range(4 + E, T + 2):
                step(t, t % 2, None)

        def expert_loop(eng, step):
            turns = (SLOT_TILES - 3 - 2 * RING) // RING
            for j in range(-3, 2 * RING):
                step(j, j % RING, None)
            with eng.Fori(0, turns) as i:
                for k in range(RING):
                    step(RING * (i + 2) + k, k, i)
            for j in range(RING * (turns + 2), SLOT_TILES + 2):
                step(j, j % RING, None)

        def in_tiles(j):
            return not isinstance(j, int) or 0 <= j < SLOT_TILES

        def scatter_wait(eng, d, kd, k, i):
            if i is None:
                after(eng, scattered[kd], 16 * (d // RING))
            else:
                eng.wait_ge(scattered[kd], 16 * (i + (1 if k == 0 else 2)))

        def inside(t):
            return not isinstance(t, int) or 0 <= t < T

        def after(eng, s, n):
            if not isinstance(n, int) or n > 0:
                eng.wait_ge(s, n)

        def store(sp, c):
            b, t = c // (TB // 2), 2 * c % TB
            sp.dma_start(out[b, t * P:(t + 2) * P, :].rearrange("(t p) d -> p t d", p=P),
                         x_sb[:, 2 * c:2 * c + 2, :]).then_inc(out_stored, 16)

        block = stack.enter_context(nc.Block())

        @block.sync
        def _(sp):
            sp.dma_start(ctx_sb[:, :], ctx_kv.rearrange("b s d -> (b s) d")).then_inc(ld_kv, 16)
            for j, b_in in enumerate((bq, bk, bv)):
                sp.dma_start(bias_rows[j * HP:(j + 1) * HP, :],
                             b_in.rearrange("(c p) f -> c (p f)", p=2)).then_inc(ld_kv, 16)
            sp.dma_start(Wk_sb[:, :, :], Wk.rearrange("(k p) h f -> p k (h f)", p=P)).then_inc(ld_kv, 16)
            sp.dma_start(Wq_sb[:, :, :], Wq.rearrange("(k p) h f -> p k (h f)", p=P)).then_inc(ld_q, 16)
            sp.dma_start(x_sb[:, 0:TB, :], x[0].rearrange("(t p) d -> p t d", p=P)).then_inc(ld_x[0], 16)
            sp.dma_start(Wv_sb[:, :, :], Wv.rearrange("(k p) h f -> p k (h f)", p=P)).then_inc(ld_vo, 16)
            sp.dma_start(Wo_sb[:, :, :], Wo.rearrange("(c p) f d -> (p f) c d", p=2)).then_inc(ld_vo, 16)
            sp.dma_start(raw_sh[:, :, 0:F], Wg_s.rearrange("(k p) f -> p k f", p=P)).then_inc(ld_sh, 16)
            sp.dma_start(raw_sh[:, :, F:2 * F], Wu_s.rearrange("(k p) f -> p k f", p=P)).then_inc(ld_sh, 16)
            sp.dma_start(raw_sh[:, :, 2 * F:], W_router.rearrange("(k p) e -> p k e", p=P)).then_inc(ld_sh, 16)
            sp.dma_start(raw_ds[:, :, :], Wd_s.rearrange("(k p) d -> p k d", p=FH)).then_inc(ld_sh, 16)
            sp.dma_start(x_sb[:, TB:T, :], x[1].rearrange("(t p) d -> p t d", p=P)).then_inc(ld_x[1], 16)

            sp.wait_ge(B_done, 2 * HP)
            sp.wait_ge(wsh_done, 2)

            def step(t, q, i):
                if i is not None:
                    e = 2 * i + q
                    sp.wait_ge(xb_done, t + 1)
                    for half, W in enumerate((Wg, Wu)):
                        sp.dma_start(raw_w[q][:, :, half * F:(half + 1) * F],
                                     W[bass.ds(e, 1), :, :].rearrange("o (k p) f -> p (o k) f", p=P)).then_inc(raw_loaded[q], 16)
                if isinstance(t, int) and T - 4 <= t < T:
                    n = t - (T - 4)
                    if n < 2:
                        sp.wait_ge(w_lo_done, E)
                    else:
                        sp.wait_ge(wd_lo_done, n - 1)
                    sp.dma_start(raw_d[n % 2][:, :, :],
                                 Wd[2 * n:2 * n + 2].rearrange("e (k p) d -> p (e k) d", p=FH)).then_inc(ld_d[n % 2], 16)
                w = t - 1
                if inside(w):
                    sp.wait_ge(xn2_done, w + 1)
                    sp.dma_start(xn2_dram[bass.ds(w * P, P), :], xn2[1 - q][:, :]).then_inc(xn2_stored[1 - q], 16)

            token_loop(sp, step)
            for k in range(RING):
                sp.wait_ge(scattered[k], 16 * len(range(k, SLOT_TILES, RING)))
            for c in range(T // 2):
                if c >= 2:
                    sp.wait_ge(add_step, 4 * (c - 1))
                for k in range(TOPK):
                    row = k * TOKENS + c * 2 * P
                    sp.dma_start(routed_in[c % 2][:, 2 * k:2 * k + 2, :],
                                 routed_dram[row:row + 2 * P, :].rearrange("(t p) d -> p t d", p=P)).then_inc(routed_loaded[c % 2], 16)
                if c >= 1:
                    sp.wait_ge(add_step, 4 * c)
                    store(sp, c - 1)
            sp.wait_ge(add_step, 4 * (T // 2))
            store(sp, T // 2 - 1)
            sp.wait_ge(out_stored, 16 * (T // 2))

        @block.gpsimd
        def _(pool):
            pool.dma_start(gates[:, 0:1], g_xattn.partition_broadcast(P)).then_inc(ld_misc, 16)
            pool.dma_start(gates[:, 1:2], g_ffn.partition_broadcast(P)).then_inc(ld_misc, 16)
            pool.dma_start(bo_row[:, :], bo.partition_broadcast(P)).then_inc(ld_misc, 16)
            nc.gpsimd.memset(ident[:, :], 0.0).then_inc(const_step, 1)
            nc.gpsimd.memset(minus_half[:, :], -0.5).then_inc(const_step, 1)
            nc.gpsimd.memset(eps_col[:, :], LN_EPS).then_inc(const_step, 1)
            nc.gpsimd.memset(minus_one[:, :], -1.0).then_inc(const_step, 1)
            nc.gpsimd.memset(pick_rows[:, :].bitcast(F32), 0.0).then_inc(const_pick, 1)
            pool.wait_ge(const_step, 4)
            nc.gpsimd.affine_select(out=ident[:, :], in_=ident[:, :], compare_op=ALU.not_equal, fill=1.0,
                                    base=0, pattern=[[-1, P]], channel_multiplier=1).then_inc(const_step, 1)
            pool.wait_ge(const_step, 5)
            nc.gpsimd.memset(score_bias[64:P, :, :].bitcast(F32), 0.0).then_inc(const_pick, 1)
            pool.wait_ge(const_pick, 2)
            nc.gpsimd.memset(pick_rows[0:1, :].bitcast(F32), 1.0).then_inc(const_pick, 1)
            pool.wait_ge(const_pick, 3)
            nc.gpsimd.memset(pick_rows[32:33, :].bitcast(F32), 1.0).then_inc(const_pick, 1)

            pool.wait_ge(const_pick, 4)
            pool.dma_start(expert_b[:, :], expert_bias.partition_broadcast(P)).then_inc(ld_misc, 16)
            nc.gpsimd.iota(iota_e[:, :], [[1, E]], base=0, channel_multiplier=0,
                           allow_small_or_imprecise_dtypes=True).then_inc(const_route, 1)
            nc.gpsimd.iota(iota_e8[:, :], [[1, E]], base=-E, channel_multiplier=0,
                           allow_small_or_imprecise_dtypes=True).then_inc(const_route, 1)
            nc.gpsimd.iota(iota_q[:, :], [[1, Q]], base=0, channel_multiplier=0,
                           allow_small_or_imprecise_dtypes=True).then_inc(const_route, 1)
            nc.gpsimd.iota(iota_p[:, :], [[1, P]], base=0, channel_multiplier=0,
                           allow_small_or_imprecise_dtypes=True).then_inc(const_route, 1)
            nc.gpsimd.iota(pair_row[:, :], [[TOKENS, TOPK], [P, T]], base=1, channel_multiplier=1,
                           allow_small_or_imprecise_dtypes=True).then_inc(const_route, 1)
            nc.gpsimd.iota(not_after[:, :, :], [[-1, E], [1, E]], base=0, channel_multiplier=0,
                           allow_small_or_imprecise_dtypes=True).then_inc(const_route, 1)
            nc.gpsimd.memset(zero_i[:, :], 0).then_inc(const_route, 1)
            nc.gpsimd.memset(ones_r[:, :].bitcast(F32), 1.0).then_inc(const_route, 1)
            nc.gpsimd.memset(upper_f[:, :], 1.0).then_inc(const_route, 1)
            pool.wait_ge(const_route, 9)
            nc.gpsimd.affine_select(out=upper_f[:, :], in_=upper_f[:, :], compare_op=ALU.is_gt, fill=0.0,
                                    base=0, pattern=[[1, P]], channel_multiplier=-1).then_inc(const_route, 1)

            pool.wait_ge(mv1_done, T)
            nc.gpsimd.tensor_scalar(ve1[:, :], mv1[:, :, 1], LN_EPS, None, ALU.add).then_inc(ln1_step, 1)
            pool.wait_ge(ln1_step, 1)
            nc.gpsimd.tensor_tensor(rstd1[:, :], ve1[:, :], minus_half[:, :], ALU.pow).then_inc(ln1_step, 1)
            pool.wait_ge(ln1_step, 2)
            nc.gpsimd.tensor_tensor(shift1[:, :], mv1[:, :, 0], rstd1[:, :], ALU.mult).then_inc(ln1_step, 1)
            pool.wait_ge(ln1_step, 3)
            nc.gpsimd.tensor_scalar(shift1[:, :], shift1[:, :], -1.0, None, ALU.mult).then_inc(ln1_step, 1)
            pool.wait_ge(ln1_step, 4)
            pool.wait_ge(ld_misc, 64)

            def step(t, q, i):
                w, m, u = t - 1, t + 1, t + 1
                if inside(w):
                    pool.wait_ge(mv2_done, w + 1)
                    after(pool, xn2_done, w)
                    nc.gpsimd.tensor_tensor(ve2[:, :], mv2[:, 1:2], eps_col[:, :], ALU.add).then_inc(ln2_step, 1)
                    nc.gpsimd.tensor_tensor(neg_mean2[:, :], mv2[:, 0:1], minus_one[:, :], ALU.mult).then_inc(ln2_step, 1)
                    pool.wait_ge(ln2_step, 4 * w + 1)
                    nc.gpsimd.tensor_tensor(rstd2[:, :], ve2[:, :], minus_half[:, 0:1], ALU.pow).then_inc(ln2_step, 1)
                    pool.wait_ge(ln2_step, 4 * w + 3)
                    nc.gpsimd.tensor_tensor(shift2[:, :], neg_mean2[:, :], rstd2[:, :], ALU.mult).then_inc(ln2_step, 1)
                if inside(u):
                    pool.wait_ge(xn_done, u + 1)
                    nc.gpsimd.tensor_tensor(x_sb[:, bass.ds(u, 1), :], x_sb[:, bass.ds(u, 1), :], bo_row[:, :],
                                            ALU.add).then_inc(xb_done, 1)
                if inside(m):
                    pool.wait_ge(inv_done, m + 1)
                    pr = prob[1 - q][:, :].rearrange("p (h k) -> p h k", k=KV)
                    nc.gpsimd.tensor_tensor(pr, pr, row_inv[:, :].unsqueeze(2).to_broadcast([P, H, KV]),
                                            ALU.mult).then_inc(norm_done, 1)
                if i is not None:
                    e = 2 * i + q
                    pool.wait_ge(w_hi_done, e + 1)
                    nc.gpsimd.tensor_tensor(W_lo[:, bass.ds(KC * e, KC), :], raw_w[q],
                                            W_hi[:, bass.ds(KC * e, KC), :].bitcast(F32), ALU.subtract).then_inc(w_lo_done, 1)
                if isinstance(t, int) and T - 2 <= t < T + 2:
                    n = t - (T - 2)
                    part = slice(4 * n, 4 * n + 4)
                    pool.wait_ge(wd_hi_done, n + 1)
                    nc.gpsimd.tensor_tensor(Wd_lo[:, part, :], raw_d[n % 2][:, :, :],
                                            Wd_hi[:, part, :].bitcast(F32), ALU.subtract).then_inc(wd_lo_done, 1)

            token_loop(pool, step)

            def hold():
                pool.sem_inc(pool_held, 1)

            for q in range(2):
                pool.wait_ge(xn2_stored[q], 16 * (T // 2))

            def expert_step(j, k, i):
                n, s = j + 3, j - 2
                kn, ks = (k + 3) % RING, (k - 2) % RING
                if in_tiles(n):
                    after(pool, gT_done, j)
                    pool.wait_ge(gat_idx_done, n + 1)
                    hold()
                    nc.gpsimd.indirect_dma_start(xg[kn][:, :], None, xn2_dram[:, :],
                                                 bass.IndirectOffsetOnAxis(ap=gat_idx[kn][:, 0:1], axis=0)).then_inc(gathered[kn], 16)
                if in_tiles(s):
                    pool.wait_ge(sct_idx_done, s + 1)
                    pool.wait_ge(ycopy_done, s + 1)
                    hold()
                    nc.gpsimd.indirect_dma_start(routed_dram[:, :], bass.IndirectOffsetOnAxis(ap=sct_idx[ks][:, 0:1], axis=0),
                                                 y_sb[ks][:, :], None, bounds_check=TOPK * TOKENS - 1,
                                                 oob_is_err=False).then_inc(scattered[ks], 16)

            expert_loop(pool, expert_step)

        @block.scalar
        def _(act):
            act.wait_ge(ld_misc, 64)
            nc.scalar.activation(tgate[:, :], gates[:, :], ACT.Tanh).then_inc(gates_done, 1)
            act.wait_ge(gates_done, 1)
            nc.scalar.activation(bo_row[:, :], bo_row[:, :], ACT.Copy, scale=tgate[:, 0:1]).then_inc(gates_done, 1)
            nc.scalar.activation(half_tgf[:, :], tgate[:, 1:2], ACT.Copy, scale=0.5).then_inc(gates_done, 1)
            for j in range(HP // 2):
                act.wait_ge(wqT_ps, j + 1)
                nc.scalar.activation(WqT[:, 2 * j:2 * j + 2, :], bank[j][:, :].rearrange("p (c d) -> p c d", c=2),
                                     ACT.Copy).then_inc(wqT_done, 1)
            j = 0
            for kc in range(KC):
                for g in range(NG):
                    for p in range(2):
                        act.wait_ge(A_ps, j + 1)
                        nc.scalar.activation(A_out(A_hi, kc, g, p), A_in(fold_bank(bank, scores_ps, j)),
                                             ACT.Copy).then_inc(A_hi_done, 1)
                        j += 1
            j = 0
            for g in range(NG):
                for p in range(2):
                    act.wait_ge(sbias_ps, j + 1)
                    nc.scalar.activation(S_out(score_bias, g, p, 0), S_in(fold_bank(bank, scores_ps, j), 0),
                                         ACT.Copy).then_inc(sbias_hi, 1)
                    j += 1
            for j in range(2 * HP):
                c, p = j // 2, j % 2
                act.wait_ge(B_ps, j + 1)
                nc.scalar.activation(B_hi[64 * p:64 * p + 64, :, c, :],
                                     fold_bank(bank, scores_ps, j)[64 * p:64 * p + 64, :].rearrange("p (b d) -> p b d", b=B),
                                     ACT.Copy, scale=tgate[64 * p:64 * p + 64, 0:1]).then_inc(B_hi_done, 1)
            act.wait_ge(ld_sh, 64)
            nc.scalar.activation(Wsh_hi[:, :, :], raw_sh[:, :, :], ACT.Copy).then_inc(wsh_hi_done, 1)
            nc.scalar.activation(Wds_hi[:, :, :], raw_ds[:, :, :], ACT.Copy).then_inc(wsh_hi_done, 1)

            act.wait_ge(const_route, 10)
            nc.scalar.activation(upper[:, :], upper_f[:, :], ACT.Copy).then_inc(mask_done, 1)
            act.wait_ge(ln1_step, 4)

            def step(t, q, i):
                u, v, m, w, n = t + 2, t - 2, t + 1, t - 1, t + 3
                if inside(t):
                    for h in range(2):
                        act.wait_ge(pT_done, 2 * t + h + 1)
                        if h == 0:
                            after(act, att_done, t)
                        nc.scalar.activation(pT_hi[:, 4 * h:4 * h + 4, :],
                                             pT_ps[h][:, :].rearrange("p (c s) -> p c s", c=4),
                                             ACT.Copy).then_inc(pT_hi_done, 1)
                if inside(u):
                    act.wait_ge(xT_done, u + 1)
                    after(act, scores_done, u - 1)
                    nc.scalar.activation(xnT_hi[q][:, :, :], xT_ps[:, 0:D].rearrange("p (k s) -> p k s", k=KC),
                                         ACT.Copy).then_inc(xT_hi_done, 1)
                if inside(n):
                    after(act, xT_done, n - 1)
                    nc.scalar.activation(xn[1 - q][:, :], x_sb[:, bass.ds(n, 1), :], ACT.Identity,
                                         scale=rstd1[:, bass.ds(n, 1)], bias=shift1[:, bass.ds(n, 1)]).then_inc(xn_done, 1)
                if inside(w):
                    after(act, x2T_done, w - 1)
                    if isinstance(w, int):
                        after(act, xn2_stored[1 - q], 16 * (w // 2))
                    else:
                        act.wait_ge(xn2_stored[1 - q], 8 * (w - (1 - q)))
                    act.wait_ge(ln2_step, 4 * w + 4)
                    nc.scalar.activation(xn2[1 - q][:, :], x_sb[:, bass.ds(w, 1), :], ACT.Identity,
                                         scale=rstd2[:, 0:1], bias=shift2[:, 0:1]).then_inc(xn2_done, 1)
                if inside(v):
                    act.wait_ge(h_done, v + 1)
                    nc.scalar.activation(exp_neg[:, bass.ds(v, 1), :], h_ps[:, 2 * F:2 * F + E], ACT.Exp,
                                         scale=-1.0).then_inc(logit_done, 1)
                    after(act, gact_done, v)
                    nc.scalar.activation(tanh_g[:, :], h_ps[:, 0:F], ACT.Tanh, scale=0.5).then_inc(tanh_done, 1)
                if inside(m):
                    act.wait_ge(sub_done, m + 1)
                    nc.scalar.activation(prob[1 - q][:, :], prob[1 - q][:, :], ACT.Exp).then_inc(exp_done, 1)
                if inside(v):
                    act.wait_ge(hT_done, v + 1)
                    after(act, y_done, v)
                    nc.scalar.activation(hT_hi[:, :, :], hy_ps[0:FH, 0:2 * P].rearrange("p (k s) -> p k s", k=2),
                                         ACT.Copy).then_inc(hT_hi_done, 1)
                if inside(w):
                    act.wait_ge(x2T_done, w + 1)
                    after(act, h_done, w - 1)
                    nc.scalar.activation(xn2T_hi[1 - q][:, :, :], xT_ps[:, 0:D].rearrange("p (k s) -> p k s", k=KC),
                                         ACT.Copy).then_inc(x2T_hi_done, 1)
                if i is not None:
                    act.wait_ge(raw_loaded[q], 32 * (i + 1))
                    nc.scalar.activation(W_hi[:, bass.ds(KC * (2 * i + q), KC), :], raw_w[q], ACT.Copy).then_inc(w_hi_done, 1)
                if isinstance(t, int) and T - 2 <= t < T + 2:
                    n = t - (T - 2)
                    part = slice(4 * n, 4 * n + 4)
                    act.wait_ge(ld_d[n % 2], 16 * (n // 2 + 1))
                    act.wait_ge(scores_done, T)
                    nc.scalar.activation(Wd_hi[:, part, :], raw_d[n % 2][:, :, :], ACT.Copy).then_inc(wd_hi_done, 1)

            token_loop(act, step)

            def expert_step(j, k, i):
                n, d = j + 1, j - 1
                if in_tiles(n):
                    act.wait_ge(gT_done, n + 1)
                    after(act, eh_done, n - 1)
                    nc.scalar.activation(xnT_hi[(k + 1) % 2][:, :, :],
                                         gT_ps[(k + 1) % 2][:, 0:D].rearrange("p (k s) -> p k s", k=KC),
                                         ACT.Copy).then_inc(gT_hi_done, 1)
                if in_tiles(d):
                    act.wait_ge(ehT_done, d + 1)
                    after(act, ey_done, d)
                    nc.scalar.activation(hT_hi[:, :, :], ehT_ps[(k + 1) % 2][0:FH, 0:2 * P].rearrange("p (k s) -> p k s", k=2),
                                         ACT.Copy).then_inc(ehT_hi_done, 1)
                if in_tiles(j):
                    act.wait_ge(eh_done, j + 1)
                    after(act, ehid_done, j)
                    nc.scalar.activation(gate_act[:, :], eh_ps[k % 2][:, 0:F], ACT.Silu).then_inc(esilu_done, 1)

            expert_loop(act, expert_step)

        @block.vector
        def _(dve):
            dve.wait_ge(ctxT_ps, 1)
            nc.vector.tensor_copy(ctxT[:, :, :], bank[0][:, 0:KC * P].rearrange("p (k s) -> p k s", k=KC)).then_inc(ctxT_done, 1)
            nc.vector.tensor_copy(bias_cols[:, :], bank[0][:, 256:256 + 3 * HP]).then_inc(ctxT_done, 1)
            dve.wait_ge(ctxT_done, 2)
            for c in range(HP):
                dve.wait_ge(kv_ps, c // GC + 1)
                nc.vector.tensor_scalar(kT[:, c, :], bank[4 + c // GC][:, (c % GC) * P:(c % GC + 1) * P],
                                        bias_cols[:, HP + c:HP + c + 1], DH ** -0.5, ALU.add, ALU.mult).then_inc(kv_done, 1)
            j = 0
            for kc in range(KC):
                for g in range(NG):
                    for p in range(2):
                        dve.wait_ge(A_hi_done, j + 1)
                        nc.vector.tensor_tensor(A_out(A_lo, kc, g, p), A_in(fold_bank(bank, scores_ps, j)),
                                                A_out(A_hi, kc, g, p).bitcast(F32), ALU.subtract).then_inc(A_done, 1)
                        j += 1
            j = 0
            for g in range(NG):
                for p in range(2):
                    dve.wait_ge(sbias_hi, j + 1)
                    nc.vector.tensor_tensor(S_out(score_bias, g, p, 32), S_in(fold_bank(bank, scores_ps, j), 32),
                                            S_out(score_bias, g, p, 32).bitcast(F32), ALU.subtract).then_inc(sbias_done, 1)
                    j += 1
            for t in range(T):
                if t % TB == 0:
                    dve.wait_ge(ld_x[t // TB], 16)
                nc.vector.bn_stats(stats1[:, t, :], x_sb[:, t, :]).then_inc(stats1_done, 1)
            for t in range(T):
                dve.wait_ge(stats1_done, t + 1)
                nc.vector.bn_aggr(mv1[:, t, :], stats1[:, t, :]).then_inc(mv1_done, 1)
            for c in range(HP):
                dve.wait_ge(kv_ps, NG + c // GC + 1)
                nc.vector.tensor_scalar(vT[:, c, :], bank[4 + c // GC][:, (c % GC) * P:(c % GC + 1) * P],
                                        bias_cols[:, 2 * HP + c:2 * HP + c + 1], None, ALU.add).then_inc(kv_done, 1)
            for j in range(2 * HP):
                c, p = j // 2, j % 2
                rows = slice(64 * p, 64 * p + 64)
                dve.wait_ge(B_hi_done, j + 1)
                nc.vector.scalar_tensor_tensor(out=B_lo[rows, :, c, :],
                                               in0=fold_bank(bank, scores_ps, j)[rows, :].rearrange("p (b d) -> p b d", b=B),
                                               scalar=tgate[rows, 0:1], in1=B_hi[rows, :, c, :].bitcast(F32),
                                               op0=ALU.mult, op1=ALU.subtract).then_inc(B_done, 1)
            dve.wait_ge(wsh_hi_done, 1)
            nc.vector.tensor_tensor(Wsh_lo[:, :, :], raw_sh[:, :, :], Wsh_hi[:, :, :].bitcast(F32),
                                    ALU.subtract).then_inc(wsh_done, 1)
            dve.wait_ge(wsh_hi_done, 2)
            nc.vector.tensor_tensor(Wds_lo[:, :, :], raw_ds[:, :, :], Wds_hi[:, :, :].bitcast(F32),
                                    ALU.subtract).then_inc(wsh_done, 1)

            def step(t, q, i):
                u, v, m, w = t + 2, t - 2, t + 1, t - 1
                if inside(m):
                    dve.wait_ge(scores_done, m + 1)
                    after(dve, sub_done, m)
                    sc = scores_ps[:, :].rearrange("p (h k) -> p h k", k=KV)
                    nc.vector.tensor_reduce(row_max[:, :], sc, AX_X, ALU.max).then_inc(max_done, 1)
                    dve.wait_ge(max_done, m + 1)
                    after(dve, pT_done, 2 * m - 2)
                    nc.vector.tensor_tensor(prob[1 - q][:, :].rearrange("p (h k) -> p h k", k=KV), sc,
                                            row_max[:, :].unsqueeze(2).to_broadcast([P, H, KV]),
                                            ALU.subtract).then_inc(sub_done, 1)
                if inside(u):
                    dve.wait_ge(xT_hi_done, u + 1)
                    nc.vector.tensor_tensor(xnT_lo[q][:, :, :], xT_ps[:, 0:D].rearrange("p (k s) -> p k s", k=KC),
                                            xnT_hi[q][:, :, :].bitcast(F32), ALU.subtract).then_inc(xT_lo_done, 1)
                if inside(t):
                    for h in range(2):
                        dve.wait_ge(pT_hi_done, 2 * t + h + 1)
                        nc.vector.tensor_tensor(pT_lo[:, 4 * h:4 * h + 4, :],
                                                pT_ps[h][:, :].rearrange("p (c s) -> p c s", c=4),
                                                pT_hi[:, 4 * h:4 * h + 4, :].bitcast(F32),
                                                ALU.subtract).then_inc(pT_lo_done, 1)
                if inside(m):
                    dve.wait_ge(exp_done, m + 1)
                    after(dve, inv_done, m)
                    nc.vector.tensor_reduce(row_sum[:, :], prob[1 - q][:, :].rearrange("p (h k) -> p h k", k=KV),
                                            AX_X, ALU.add).then_inc(sum_done, 1)
                    dve.wait_ge(sum_done, m + 1)
                    after(dve, norm_done, m)
                    nc.vector.reciprocal(row_inv[:, :], row_sum[:, :]).then_inc(inv_done, 1)
                if inside(v):
                    dve.wait_ge(tanh_done, v + 1)
                    after(dve, hid_done, v)
                    nc.vector.scalar_tensor_tensor(out=gate_act[:, :], in0=tanh_g[:, :], scalar=1.0, in1=h_ps[:, 0:F],
                                                   op0=ALU.add, op1=ALU.mult).then_inc(gact_done, 1)
                    dve.wait_ge(gact_done, v + 1)
                    after(dve, hT_done, v)
                    nc.vector.tensor_tensor(hid[:, :], gate_act[:, :], h_ps[:, F:2 * F], ALU.mult).then_inc(hid_done, 1)
                    dve.wait_ge(hT_hi_done, v + 1)
                    nc.vector.tensor_tensor(hT_lo[:, :, :], hy_ps[0:FH, 0:2 * P].rearrange("p (k s) -> p k s", k=2),
                                            hT_hi[:, :, :].bitcast(F32), ALU.subtract).then_inc(hT_lo_done, 1)
                if inside(w):
                    dve.wait_ge(x2T_hi_done, w + 1)
                    nc.vector.tensor_tensor(xn2T_lo[1 - q][:, :, :], xT_ps[:, 0:D].rearrange("p (k s) -> p k s", k=KC),
                                            xn2T_hi[1 - q][:, :, :].bitcast(F32), ALU.subtract).then_inc(x2T_lo_done, 1)
                if inside(t):
                    dve.wait_ge(att_done, t + 1)
                    dve.wait_ge(xb_done, t + 1)
                    nc.vector.tensor_tensor(x_sb[:, bass.ds(t, 1), :], att_ps[:, 0:D], x_sb[:, bass.ds(t, 1), :],
                                            ALU.add).then_inc(x2_done, 1)
                    dve.wait_ge(x2_done, t + 1)
                    after(dve, mv2_done, t)
                    carry_waits()
                    nc.vector.bn_stats(stats2[:, :], x_sb[:, bass.ds(t, 1), :]).then_inc(stats2_done, 1)
                    dve.wait_ge(stats2_done, t + 1)
                    after(dve, ln2_step, 4 * t)
                    carry_waits()
                    nc.vector.bn_aggr(mv2[:, :], stats2[:, :]).then_inc(mv2_done, 1)
                if inside(v):
                    dve.wait_ge(y_done, v + 1)
                    dve.wait_ge(xn2_done, v + 1)
                    nc.vector.scalar_tensor_tensor(out=x_sb[:, bass.ds(v, 1), :], in0=hy_ps[:, 0:D],
                                                   scalar=half_tgf[:, 0:1], in1=x_sb[:, bass.ds(v, 1), :],
                                                   op0=ALU.mult, op1=ALU.add).then_inc(yadd_done, 1)

            def carry_waits():
                nc.vector.tensor_copy(carrier[:, :], ident[:, 0:1])

            dve.wait_ge(gates_done, 3)
            dve.wait_ge(const_step, 5)
            token_loop(dve, step)

            steps = [0]

            def chain(ins):
                steps[0] += 1
                ins.then_inc(route_step, 1)
                dve.wait_ge(route_step, steps[0])

            def over_t(ap):
                return ap.unsqueeze(1).to_broadcast([P, T, E])

            def over_e(ap):
                return ap.unsqueeze(2).to_broadcast([P, T, E])

            dve.wait_ge(logit_done, T)
            dve.wait_ge(const_route, 10)
            dve.wait_ge(ld_misc, 64)
            chain(nc.vector.tensor_scalar(score[:, :, :], exp_neg[:, :, :], 1.0, None, ALU.add))
            chain(nc.vector.reciprocal(score[:, :, :], score[:, :, :]))
            chain(nc.vector.tensor_tensor(choice[:, :, :], score[:, :, :], over_t(expert_b[:, :]), ALU.add))
            for k in range(TOPK):
                chain(nc.vector.tensor_reduce(best[:, :], choice[:, :, :], AX_X, ALU.max))
                chain(nc.vector.tensor_tensor(cand[:, :, :], choice[:, :, :], over_e(best[:, :]), ALU.is_equal))
                chain(nc.vector.scalar_tensor_tensor(out=cand[:, :, :], in0=cand[:, :, :], scalar=-float(E),
                                                     in1=over_t(iota_e[:, :]), op0=ALU.mult, op1=ALU.add))
                chain(nc.vector.tensor_reduce(first_e[:, :], cand[:, :, :], AX_X, ALU.min))
                chain(nc.vector.tensor_tensor(hot[k][:, :, :], over_t(iota_e8[:, :]), over_e(first_e[:, :]), ALU.is_equal))
                if k == 0:
                    chain(nc.vector.scalar_tensor_tensor(out=choice[:, :, :], in0=hot[0][:, :, :], scalar=-BIG,
                                                         in1=choice[:, :, :], op0=ALU.mult, op1=ALU.add))
            chain(nc.vector.tensor_tensor(mask[:, :, :], hot[0][:, :, :], hot[1][:, :, :], ALU.add))
            nc.vector.tensor_reduce(mask_sum[:, :], mask[:, :, :].bitcast(F32).rearrange("p t e -> p e t"),
                                    AX_X, ALU.add).then_inc(mask_done, 1)
            nc.vector.tensor_scalar(not_after[:, :, :], not_after[:, :, :], 0.0, None, ALU.is_le)
            for k in range(TOPK):
                chain(nc.vector.tensor_tensor(cand[:, :, :], score[:, :, :], hot[k][:, :, :], ALU.mult))
                chain(nc.vector.tensor_reduce(picked[k][:, :], cand[:, :, :], AX_X, ALU.add))
            chain(nc.vector.tensor_tensor(den[:, :], picked[0][:, :], picked[1][:, :], ALU.add))
            chain(nc.vector.tensor_scalar(den[:, :], den[:, :], ROUTE_EPS, None, ALU.add))
            chain(nc.vector.reciprocal(den[:, :], den[:, :]))
            chain(nc.vector.tensor_scalar(den[:, :], den[:, :], tgate[:, 1:2], None, ALU.mult))
            for k in range(TOPK):
                nc.vector.tensor_tensor(weight[k][:, :], picked[k][:, :], den[:, :], ALU.mult)
            dve.wait_ge(rank_ps_done, 1)
            chain(nc.vector.tensor_scalar(count_i[:, :], count_ps, float(P - 1), None, ALU.add))
            chain(nc.vector.tensor_scalar(count_i[:, :], count_i[:, :], P.bit_length() - 1, None, ALU.logical_shift_right))
            chain(nc.vector.tensor_copy(tiles_f[:, :], count_i[:, :]))
            chain(nc.vector.tensor_tensor(end_prod[:, :, :], not_after[:, :, :],
                                          tiles_f[:, :].unsqueeze(1).to_broadcast([P, E, E]), ALU.mult))
            chain(nc.vector.tensor_reduce(end_f[:, :], end_prod[:, :, :], AX_X, ALU.add))
            chain(nc.vector.tensor_tensor(start_f[:, :], end_f[:, :], tiles_f[:, :], ALU.subtract))
            chain(nc.vector.tensor_scalar(start_f[:, :], start_f[:, :], float(P), None, ALU.mult))
            chain(nc.vector.tensor_tensor(choice[:, :, :], rank_ps, over_t(start_f[:, :]), ALU.add))
            for k in range(TOPK):
                chain(nc.vector.tensor_tensor(cand[:, :, :], choice[:, :, :], hot[k][:, :, :], ALU.mult))
                chain(nc.vector.tensor_reduce(slot[:, k, :], cand[:, :, :], AX_X, ALU.add))
            chain(nc.vector.tensor_copy(slot_i[:, :], slot[:, :, :].rearrange("p k t -> p (k t)")))
            chain(nc.vector.tensor_scalar(part_i[:, :], slot_i[:, :], P - 1, None, ALU.bitwise_and))
            chain(nc.vector.tensor_copy(slot_p[:, :], part_i[:, :]))
            chain(nc.vector.tensor_scalar(part_i[:, :], slot_i[:, :], P.bit_length() - 1, None, ALU.logical_shift_right))
            chain(nc.vector.tensor_copy(slot_q[:, :], part_i[:, :]))
            dve.wait_ge(att_done, T)
            for n in range(TOPK * T):
                nc.vector.tensor_scalar(onehot_p[:, n, :], iota_p[:, :], slot_p[:, n:n + 1], None, ALU.is_equal)
                nc.vector.tensor_scalar(onehot_q[:, n, :], iota_q[:, :], slot_q[:, n:n + 1], pair_row[:, n:n + 1],
                                        ALU.is_equal, ALU.mult).then_inc(onehot_done, 1)
            chain(nc.vector.tensor_tensor(tile_cmp[:, :, :], iota_q[0:1, :].unsqueeze(2).to_broadcast([1, Q, E]),
                                          end_f[0:1, :].unsqueeze(1).to_broadcast([1, Q, E]), ALU.is_ge))
            chain(nc.vector.tensor_reduce(tile_e[:, :], tile_cmp[:, :, :], AX_X, ALU.add))
            nc.vector.tensor_scalar(tile_row[:, :], tile_e[:, :], float(E - 1), float(KC), ALU.min,
                                    ALU.mult).then_inc(tile_row_done, 1)
            dve.wait_ge(table_ps_done, 1)
            chain(nc.vector.tensor_copy(table[:, :], table_ps))
            chain(nc.vector.tensor_scalar(src_i[:, :], table[:, :], -1.0, 0.0, ALU.add, ALU.max))
            nc.vector.tensor_scalar(src_i[:, :], src_i[:, :], TOKENS - 1, None, ALU.bitwise_and).then_inc(src_done, 1)
            chain(nc.vector.tensor_scalar(pad_far[:, :], table[:, :], 0.0, FAR, ALU.is_equal, ALU.mult))
            nc.vector.scalar_tensor_tensor(out=dst_i[:, :], in0=table[:, :], scalar=-1.0, in1=pad_far[:, :],
                                           op0=ALU.add, op1=ALU.add).then_inc(dst_done, 1)
            dve.wait_ge(src_done, 1)
            dve.wait_ge(dst_done, 1)

            def expert_step(j, k, i):
                n, d, g = j + 1, j - 1, j + 3
                kd, kg, kx = (k - 1) % RING, (k + 3) % RING, (k + 1) % 2
                if in_tiles(g):
                    if i is None:
                        after(dve, gathered[kg], 16 * (g // RING))
                    else:
                        dve.wait_ge(gathered[kg], 16 * (i + (2 if k == 0 else 3)))
                    nc.vector.tensor_copy(gat_idx[kg][:, :], src_i[:, bass.ds(g, 1)]).then_inc(gat_idx_done, 1)
                if in_tiles(n):
                    dve.wait_ge(gT_hi_done, n + 1)
                    nc.vector.tensor_tensor(xnT_lo[kx][:, :, :], gT_ps[kx][:, 0:D].rearrange("p (k s) -> p k s", k=KC),
                                            xnT_hi[kx][:, :, :].bitcast(F32), ALU.subtract).then_inc(gT_lo_done, 1)
                if in_tiles(d):
                    dve.wait_ge(ehT_hi_done, d + 1)
                    nc.vector.tensor_tensor(hT_lo[:, :, :], ehT_ps[kx][0:FH, 0:2 * P].rearrange("p (k s) -> p k s", k=2),
                                            hT_hi[:, :, :].bitcast(F32), ALU.subtract).then_inc(ehT_lo_done, 1)
                if in_tiles(j):
                    dve.wait_ge(esilu_done, j + 1)
                    after(dve, ehT_done, j)
                    nc.vector.tensor_tensor(hid[:, :], gate_act[:, :], eh_ps[k % 2][:, F:2 * F], ALU.mult).then_inc(ehid_done, 1)
                if in_tiles(d):
                    scatter_wait(dve, d, kd, k, i)
                    nc.vector.tensor_copy(sct_idx[kd][:, :], dst_i[:, bass.ds(d, 1)]).then_inc(sct_idx_done, 1)
                    dve.wait_ge(ey_done, d + 1)
                    nc.vector.tensor_copy(y_sb[kd][:, :], ey_ps[kx][:, 0:D]).then_inc(ycopy_done, 1)

            expert_loop(dve, expert_step)

            for c in range(T // 2):
                dve.wait_ge(routed_loaded[c % 2], 32 * (c // 2 + 1))
                for k in range(TOPK):
                    for h in range(2):
                        t = 2 * c + h
                        if k:
                            dve.wait_ge(add_step, 4 * c + h + 1)
                        nc.vector.scalar_tensor_tensor(out=x_sb[:, t, :], in0=routed_in[c % 2][:, 2 * k + h, :],
                                                       scalar=weight[k][:, t:t + 1], in1=x_sb[:, t, :],
                                                       op0=ALU.mult, op1=ALU.add).then_inc(add_step, 1)

        @block.tensor
        def _(pe):
            pe.wait_ge(const_step, 5)
            pe.wait_ge(ld_kv, 16 * 5)
            for k in range(KC):
                nc.tensor.transpose(bank[0][:, k * P:(k + 1) * P], ctx_sb[:, k * P:(k + 1) * P], ident[:, :])
            nc.tensor.transpose(bank[0][:, 256:256 + 3 * HP], bias_rows[:, :], ident[0:3 * HP, 0:3 * HP]).then_inc(ctxT_ps, 1)
            pe.wait_ge(ctxT_done, 2)

            def project(W_sb):
                for g in range(NG):
                    for c in range(g * GC, (g + 1) * GC):
                        for k in range(KC):
                            mm = nc.tensor.matmul(bank[4 + g][:, (c % GC) * P:(c % GC + 1) * P],
                                                  W_sb[:, k, c * P:(c + 1) * P], ctxT[:, k, :],
                                                  start=(k == 0), stop=(k == KC - 1))
                    mm.then_inc(kv_ps, 1)

            project(Wk_sb)
            pe.wait_ge(ld_q, 16)
            for j in range(HP // 2):
                for c in (2 * j, 2 * j + 1):
                    for k in range(KC):
                        mm = nc.tensor.transpose(bank[j][:, (c % 2) * D + k * P:(c % 2) * D + (k + 1) * P],
                                                 Wq_sb[:, k, c * P:(c + 1) * P], ident[:, :])
                mm.then_inc(wqT_ps, 1)
            pe.wait_ge(wqT_done, HP // 2)
            pe.wait_ge(kv_done, HP)
            for kc in range(KC):
                for g in range(NG):
                    for c in range(g * GC, (g + 1) * GC):
                        for p in range(2):
                            j = (kc * NG + g) * 2 + p
                            rows = slice(64 * p, 64 * p + 64)
                            mm = nc.tensor.matmul(fold_bank(bank, scores_ps, j)[:, (c % GC) * P:(c % GC + 1) * P],
                                                  WqT[rows, c, kc * P:(kc + 1) * P], kT[rows, c, :],
                                                  start=True, stop=True)
                            if c == (g + 1) * GC - 1:
                                mm.then_inc(A_ps, 1)
            for g in range(NG):
                pe.wait_ge(A_done, 2 * g + 2)
                for c in range(g * GC, (g + 1) * GC):
                    for p in range(2):
                        rows = slice(64 * p, 64 * p + 64)
                        mm = nc.tensor.matmul(fold_bank(bank, scores_ps, 2 * g + p)[0:64, (c % GC) * P:(c % GC + 1) * P],
                                              bias_cols[rows, c:c + 1].to_broadcast([64, 64]), kT[rows, c, :],
                                              start=True, stop=True)
                        if c == (g + 1) * GC - 1:
                            mm.then_inc(sbias_ps, 1)
            pe.wait_ge(A_done, 2 * KC * NG)
            pe.wait_ge(ld_vo, 32)
            project(Wv_sb)
            pe.wait_ge(kv_done, 2 * HP)
            pe.wait_ge(sbias_done, 2 * NG)
            for j in range(2 * HP):
                c, p = j // 2, j % 2
                rows = slice(64 * p, 64 * p + 64)
                if j >= 8:
                    pe.wait_ge(B_done, j - 7)
                for b in range(B):
                    mm = nc.tensor.matmul(fold_bank(bank, scores_ps, j)[rows, b * D:(b + 1) * D],
                                          vT[rows, c, b * KV:(b + 1) * KV], Wo_sb[rows, c, :],
                                          start=True, stop=True)
                mm.then_inc(B_ps, 1)
            pe.wait_ge(B_done, 2 * HP)
            pe.wait_ge(wsh_done, 2)
            pe.wait_ge(const_pick, 4)

            def split_product(out_ap, a_hi, a_lo, b_hi, b_lo, first, last):
                nc.tensor.matmul(out_ap, a_hi, b_hi, start=first, stop=False)
                nc.tensor.matmul(out_ap, a_hi, b_lo, start=False, stop=False)
                return nc.tensor.matmul(out_ap, a_lo, b_hi, start=False, stop=last)

            def step(t, q, i):
                u, v, w = t + 2, t - 2, t - 1
                if inside(t):
                    pe.wait_ge(norm_done, t + 1)
                    for h in range(2):
                        after(pe, pT_lo_done, 2 * t - 1 + h)
                        for c in range(4):
                            mm = nc.tensor.transpose(pT_ps[h][:, c * P:(c + 1) * P],
                                                     prob[q][:, (4 * h + c) * P:(4 * h + c + 1) * P], ident[:, :])
                        mm.then_inc(pT_done, 1)
                if inside(u):
                    pe.wait_ge(xn_done, u + 1)
                    after(pe, xT_lo_done, u)
                    after(pe, x2T_lo_done, t - 1)
                    for k in range(KC):
                        mm = nc.tensor.transpose(xT_ps[:, k * P:(k + 1) * P], xn[q][:, k * P:(k + 1) * P], ident[:, :])
                    mm.then_inc(xT_done, 1)
                if inside(v):
                    pe.wait_ge(x2T_lo_done, v + 1)
                    after(pe, hid_done, v)
                    after(pe, logit_done, v)
                    for k in range(KC):
                        mm = split_product(h_ps[:, 0:2 * F + E], xn2T_hi[q][:, k, :], xn2T_lo[q][:, k, :],
                                           Wsh_hi[:, k, :], Wsh_lo[:, k, :], k == 0, k == KC - 1)
                    mm.then_inc(h_done, 1)
                if inside(u):
                    pe.wait_ge(xT_lo_done, u + 1)
                    after(pe, sub_done, u)
                    b = u // TB
                    for half in range(2):
                        cols = slice(half * 512, half * 512 + 512)
                        acc = scores_ps[:, cols]
                        nc.tensor.matmul(acc, pick_rows[:, :], score_bias[:, bass.ds(b, 1), cols], start=True, stop=False)
                        for k in range(KC):
                            mm = split_product(acc, xnT_hi[q][:, k, :], xnT_lo[q][:, k, :],
                                               A_hi[:, bass.ds(b, 1), k, cols], A_lo[:, bass.ds(b, 1), k, cols],
                                               False, k == KC - 1)
                    mm.then_inc(scores_done, 1)
                if inside(v):
                    pe.wait_ge(hid_done, v + 1)
                    after(pe, yadd_done, v)
                    for k in range(2):
                        mm = nc.tensor.transpose(hy_ps[0:FH, k * P:(k + 1) * P], hid[:, k * FH:(k + 1) * FH], ident[:, :])
                    mm.then_inc(hT_done, 1)
                if inside(w):
                    pe.wait_ge(xn2_done, w + 1)
                    if isinstance(t, int):
                        pe.wait_ge(xT_lo_done, min(t + 3, T))
                    else:
                        pe.wait_ge(xT_lo_done, t + 3)
                    for k in range(KC):
                        mm = nc.tensor.transpose(xT_ps[:, k * P:(k + 1) * P], xn2[1 - q][:, k * P:(k + 1) * P], ident[:, :])
                    mm.then_inc(x2T_done, 1)
                if inside(t):
                    after(pe, x2_done, t)
                    b = t // TB
                    for c in range(HP):
                        if c % 4 == 0:
                            pe.wait_ge(pT_lo_done, 2 * t + c // 4 + 1)
                        mm = split_product(att_ps[:, 0:D], pT_hi[:, c, :], pT_lo[:, c, :],
                                           B_hi[:, bass.ds(b, 1), c, :], B_lo[:, bass.ds(b, 1), c, :],
                                           c == 0, c == HP - 1)
                    mm.then_inc(att_done, 1)
                if inside(v):
                    pe.wait_ge(hT_lo_done, v + 1)
                    for k in range(2):
                        mm = split_product(hy_ps[:, 0:D], hT_hi[:, k, :], hT_lo[:, k, :],
                                           Wds_hi[:, k, :], Wds_lo[:, k, :], k == 0, k == 1)
                    mm.then_inc(y_done, 1)

            token_loop(pe, step)

            pe.wait_ge(mask_done, 2)
            pe.wait_ge(route_step, 14 + 1)
            pe.wait_ge(hid_done, T)
            pe.wait_ge(yadd_done, T)
            flat = mask[:, :, :].rearrange("p t e -> p (t e)")
            nc.tensor.matmul(count_ps, ones_r[:, :].bitcast(F32), mask_sum[:, :], start=True, stop=True)
            nc.tensor.matmul(bank[4][:, 0:T * E], upper[:, :], flat, start=True, stop=False, skip_group_check=True)
            for d in range(1, T):
                mm = nc.tensor.matmul(bank[4][:, d * E:T * E], ones_r[:, :], flat[:, 0:(T - d) * E],
                                      start=False, stop=(d == T - 1), skip_group_check=True)
            mm.then_inc(rank_ps_done, 1)
            pe.wait_ge(x2T_lo_done, T)
            for n in range(TOPK * T):
                pe.wait_ge(onehot_done, n + 1)
                mm = nc.tensor.matmul(table_ps, onehot_p[:, n, :], onehot_q[:, n, :],
                                      start=(n == 0), stop=(n == TOPK * T - 1))
            mm.then_inc(table_ps_done, 1)
            pe.wait_ge(tile_row_done, 1)
            pe.wait_ge(w_lo_done, E)
            pe.wait_ge(wd_lo_done, 4)
            pe.wait_ge(src_done, 1)

            def expert_step(j, k, i):
                n, d = j + 1, j - 1
                kn, kx = (k + 1) % RING, (k + 1) % 2
                if in_tiles(n):
                    if i is None:
                        pe.wait_ge(gathered[kn], 16 * (n // RING + 1))
                    else:
                        pe.wait_ge(gathered[kn], 16 * (i + (4 if k == RING - 1 else 3)))
                    after(pe, gT_lo_done, n - 1)
                    for c in range(KC):
                        mm = nc.tensor.transpose(gT_ps[kx][:, c * P:(c + 1) * P], xg[kn][:, c * P:(c + 1) * P], ident[:, :])
                    mm.then_inc(gT_done, 1)
                if in_tiles(d):
                    pe.wait_ge(ehid_done, d + 1)
                    after(pe, ehT_lo_done, d - 1)
                    for c in range(2):
                        mm = nc.tensor.transpose(ehT_ps[kx][0:FH, c * P:(c + 1) * P], hid[:, c * FH:(c + 1) * FH], ident[:, :])
                    mm.then_inc(ehT_done, 1)
                if in_tiles(j):
                    row = pe.value_load(tile_row[0:1, bass.ds(j, 1)], min_val=0, max_val=KC * (E - 1))
                    pe.wait_ge(gT_lo_done, j + 1)
                    after(pe, ehid_done, j - 1)
                    for c in range(KC):
                        mm = split_product(eh_ps[k % 2][:, 0:2 * F], xnT_hi[k % 2][:, c, :], xnT_lo[k % 2][:, c, :],
                                           W_hi[:, bass.ds(row + c, 1), :], W_lo[:, bass.ds(row + c, 1), :],
                                           c == 0, c == KC - 1)
                    mm.then_inc(eh_done, 1)
                if in_tiles(d):
                    row = pe.value_load(tile_row[0:1, bass.ds(d, 1)], min_val=0, max_val=KC * (E - 1))
                    pe.wait_ge(ehT_lo_done, d + 1)
                    after(pe, ycopy_done, d - 1)
                    for c in range(2):
                        mm = split_product(ey_ps[kx][:, 0:D], hT_hi[:, c, :], hT_lo[:, c, :],
                                           Wd_hi[:, bass.ds(row + c, 1), :], Wd_lo[:, bass.ds(row + c, 1), :],
                                           c == 0, c == 1)
                    mm.then_inc(ey_done, 1)

            expert_loop(pe, expert_step)


def fold_bank(bank, scores_ps, j):
    j = j % 8
    return bank[j][:, :] if j < 6 else scores_ps[:, (j - 6) * 512:(j - 5) * 512]


def A_out(A, kc, g, p):
    return A[:, :, kc, :].rearrange("q b (c p k) -> q b c p k", p=2, k=KV)[:, :, 4 * g:4 * g + 4, p, :]


def A_in(ps):
    return ps.rearrange("q (c b k) -> q b c k", c=4, b=B)


def S_out(R, g, p, row):
    rows = slice(row, 64)
    return R[rows, :, :].rearrange("q b (c p k) -> q b c p k", p=2, k=KV)[:, :, 4 * g:4 * g + 4, p, :]


def S_in(ps, row):
    return ps[row:64, :].rearrange("q (c b k) -> q b c k", c=4, b=B)


_INS = ['x', 'ctx_1024', 'g_xattn', 'g_ffn', 'L0_xattn_Wq', 'L0_xattn_bq', 'L0_xattn_Wk', 'L0_xattn_bk',
        'L0_xattn_Wv', 'L0_xattn_bv', 'L0_xattn_Wo', 'L0_xattn_bo', 'L0_ffn_W_gate_router', 'L0_ffn_expert_bias',
        'L0_ffn_Wg', 'L0_ffn_Wu', 'L0_ffn_Wd', 'L0_ffn_Wg_s', 'L0_ffn_Wu_s', 'L0_ffn_Wd_s']


def kernel(**inputs):
    import numpy as _np
    import concourse.bacc as _bacc
    from concourse import mybir as _mybir
    from concourse.bass_utils import run_bass_kernel_spmd as _run

    nc = _bacc.Bacc("TRN2", target_bir_lowering=False, num_devices=1)
    arrays, args = {}, []
    for name in _INS:
        a = _np.ascontiguousarray(inputs[name])
        arrays[f"in_{name}_dram"] = a
        args.append(nc.dram_tensor(f"in_{name}_dram", a.shape, _mybir.dt.from_np(a.dtype), kind="ExternalInput").ap())
    args.append(nc.dram_tensor("out_dram", (B, SEQ, D), F32, kind="ExternalOutput").ap())
    flamingo_layer(nc, *args)
    r = _run(nc, [arrays], core_ids=[0])
    return r.results[0]["out_dram"]
```

```python
from contextlib import ExitStack

import concourse.bass as bass
from concourse import mybir

F32 = mybir.dt.float32
F32R = mybir.dt.float32r
I32 = mybir.dt.int32
ALU = mybir.AluOpType
ACT = mybir.ActivationFunctionType
AX_X = mybir.AxisListType.X

P = 128
B, SEQ, D = 2, 1024, 256
KV = 64
H, DH = 16, 64
HP = H // 2
HK = H * KV
KC = D // P
E, F = 8, 192
FH = F // 2
TOKENS = B * SEQ
T = TOKENS // P
TB = SEQ // P
TOPK = 2
SLOT_TILES = (TOKENS * TOPK + E * (P - 1)) // P
Q = SLOT_TILES + 1
RING = 4
LN_EPS = 1e-5
ROUTE_EPS = 1e-20
FAR = 8192.0
BIG = 3.0e38


def flamingo_layer(nc, x, ctx_kv, g_xattn, g_ffn, Wq, bq, Wk, bk, Wv, bv, Wo, bo,
                   W_router, expert_bias, Wg, Wu, Wd, Wg_s, Wu_s, Wd_s, out):
    stack = ExitStack()
    with stack:
        def sb(name, shape, dt=F32):
            return stack.enter_context(nc.sbuf_tensor(name, shape, dt))

        def sem(name):
            return stack.enter_context(nc.semaphore(name))

        x_sb = sb("x_sb", [P, T, D])
        A_hi = sb("A_hi", [P, B, KC, HK], F32R)
        A_lo = sb("A_lo", [P, B, KC, HK], F32R)
        B_hi = sb("B_hi", [P, B, HP, D], F32R)
        B_lo = sb("B_lo", [P, B, HP, D], F32R)
        score_bias = sb("score_bias", [P, B, HK], F32R)
        pick_rows = sb("pick_rows", [P, P], F32R)
        Wsh_hi = sb("Wsh_hi", [P, KC, 2 * F + E], F32R)
        Wsh_lo = sb("Wsh_lo", [P, KC, 2 * F + E], F32R)
        Wds_hi = sb("Wds_hi", [FH, 2, D], F32R)
        Wds_lo = sb("Wds_lo", [FH, 2, D], F32R)

        ident = sb("ident", [P, P])
        bo_row = sb("bo_row", [P, D])
        gates = sb("gates", [P, 2])
        tgate = sb("tgate", [P, 2])
        half_tgf = sb("half_tgf", [P, 1])
        minus_half = sb("minus_half", [P, T])
        stats1 = sb("stats1", [P, T, 6])
        mv1 = sb("mv1", [P, T, 2])
        ve1 = sb("ve1", [P, T])
        rstd1 = sb("rstd1", [P, T])
        shift1 = sb("shift1", [P, T])
        xn = [sb(f"xn{q}", [P, D]) for q in range(2)]
        xnT_hi = [sb(f"xnT_hi{q}", [P, KC, P], F32R) for q in range(2)]
        xnT_lo = [sb(f"xnT_lo{q}", [P, KC, P], F32R) for q in range(2)]
        prob = [sb(f"prob{q}", [P, HK]) for q in range(2)]
        row_max = sb("row_max", [P, H])
        row_sum = sb("row_sum", [P, H])
        row_inv = sb("row_inv", [P, H])
        pT_hi = sb("pT_hi", [P, HP, P], F32R)
        pT_lo = sb("pT_lo", [P, HP, P], F32R)
        stats2 = sb("stats2", [P, 6])
        mv2 = sb("mv2", [P, 2])
        ve2 = sb("ve2", [P, 1])
        neg_mean2 = sb("neg_mean2", [P, 1])
        eps_col = sb("eps_col", [P, 1])
        minus_one = sb("minus_one", [P, 1])
        carrier = sb("carrier", [P, 1])
        silu_first = sb("silu_first", [P, 1])
        rstd2 = sb("rstd2", [P, 1])
        shift2 = sb("shift2", [P, 1])
        xn2 = [sb(f"xn2_{q}", [P, D]) for q in range(2)]
        xn2T_hi = [sb(f"xn2T_hi{q}", [P, KC, P], F32R) for q in range(2)]
        xn2T_lo = [sb(f"xn2T_lo{q}", [P, KC, P], F32R) for q in range(2)]
        tanh_g = sb("tanh_g", [P, F])
        gate_act = sb("gate_act", [P, F])
        hid = sb("hid", [P, F])
        hT_hi = sb("hT_hi", [FH, 2, P], F32R)
        hT_lo = sb("hT_lo", [FH, 2, P], F32R)
        iota_e = sb("iota_e", [P, E])
        iota_e8 = sb("iota_e8", [P, E])
        iota_q = sb("iota_q", [P, Q])
        iota_p = sb("iota_p", [P, P])
        pair_row = sb("pair_row", [P, TOPK * T])
        upper_f = sb("upper_f", [P, P])
        upper = sb("upper", [P, P], F32R)
        ones_r = sb("ones_r", [P, P], F32R)
        before = sb("before", [P, E, E])
        expert_b = sb("expert_b", [P, E])
        score = sb("score", [P, T, E])
        choice = sb("choice", [P, T, E])
        best = sb("best", [P, T])
        first_e = sb("first_e", [P, T])
        hot = sb("hot", [P, TOPK, T, E])
        upto = [pT_hi[:, k, 0:T * E].rearrange("p (t e) -> p t e", e=E) for k in range(2)]
        cand = prob[1][:, TOPK * T * E:(TOPK + 1) * T * E].rearrange("p (t e) -> p t e", e=E)
        hot_val = prob[1][:, 0:TOPK * T * E].rearrange("p (k t e) -> p k t e", k=TOPK, e=E)
        mask = sb("mask", [P, T, E], F32R)
        picked = sb("picked", [P, TOPK, T])
        weight = [sb(f"weight{k}", [P, T]) for k in range(TOPK)]
        den = sb("den", [P, T])
        count_i = sb("count_i", [P, E], I32)
        tiles_f = sb("tiles_f", [P, E])
        start_prod = sb("start_prod", [P, E, E])
        end_f = sb("end_f", [P, E])
        start_f = sb("start_f", [P, E])
        slot = sb("slot", [P, TOPK, T])
        slot_i = sb("slot_i", [P, TOPK * T], I32)
        slot_p = sb("slot_p", [P, TOPK * T])
        slot_q = sb("slot_q", [P, TOPK * T])
        place_i = sb("place_i", [P, TOPK * T], I32)
        tile_i = sb("tile_i", [P, TOPK * T], I32)
        table = sb("table", [P, Q])
        pad_far = sb("pad_far", [P, Q])
        src_i = sb("src_i", [P, Q], I32)
        dst_i = sb("dst_i", [P, Q], I32)
        zero_i = sb("zero_i", [P, 1], I32)
        tile_cmp = sb("tile_cmp", [1, Q, E])
        tile_e = sb("tile_e", [1, Q])
        tile_row = sb("tile_row", [1, RING + Q + RING], I32)
        gat_idx = [sb(f"gat_idx{k}", [P, 1], I32) for k in range(RING)]
        sct_idx = [sb(f"sct_idx{k}", [P, 1], I32) for k in range(RING)]
        xg = [sb(f"xg{k}", [P, D]) for k in range(RING)]
        y_sb = [sb(f"y_sb{k}", [P, D]) for k in range(RING)]
        exp_neg = sb("exp_neg", [P, T, E])

        fold = ExitStack()

        def fb(name, shape, dt=F32):
            return fold.enter_context(nc.sbuf_tensor(name, shape, dt))

        Wk_sb = fb("Wk_sb", [P, KC, H * DH])
        Wq_sb = fb("Wq_sb", [P, KC, H * DH])
        Wv_sb = fb("Wv_sb", [P, KC, H * DH])
        Wo_sb = fb("Wo_sb", [P, HP, D])
        WqT = fb("WqT", [P, HP, D])
        ctx_sb = fb("ctx_sb", [P, D])
        ctxT = fb("ctxT", [P, KC, P])
        bias_rows = fb("bias_rows", [3 * HP, P])
        bias_cols = fb("bias_cols", [P, 3 * HP])
        kT = fb("kT", [P, HP, P])
        vT = fb("vT", [P, HP, P])
        raw_sh = fb("raw_sh", [P, KC, 2 * F + E])
        raw_ds = fb("raw_ds", [FH, 2, D])
        fold.close()
        W_hi = sb("W_hi", [P, E * KC, 2 * F], F32R)
        W_lo = sb("W_lo", [P, E * KC, 2 * F], F32R)
        raw_buf = [sb(f"raw_buf{q}", [P, 4 * D]) for q in range(2)]
        raw_w = [r[:, 0:KC * 2 * F].rearrange("p (k f) -> p k f", k=KC) for r in raw_buf]
        raw_d = [r[0:FH, :].rearrange("p (n d) -> p n d", d=D) for r in raw_buf]
        Wd_hi = A_hi[0:FH, :, :, :].rearrange("p b k (c d) -> p (b k c) d", d=D)
        Wd_lo = A_lo[0:FH, :, :, :].rearrange("p b k (c d) -> p (b k c) d", d=D)

        plane = [W[:, :, :].rearrange("p k f -> p (k f)")[:, 0:T * D].rearrange("p (t d) -> p t d", d=D).bitcast(F32)
                 for W in (W_hi, W_lo)]
        onehot_p = B_hi[:, :, :, :].rearrange("p b c d -> p (b c d)").rearrange("p (n s) -> p n s", s=P)
        onehot_q = B_lo[:, :, :, :].rearrange("p b c d -> p (b c d)")[:, 0:TOPK * T * Q].rearrange("p (n s) -> p n s", s=Q)
        bank = [stack.enter_context(nc.psum_tensor(f"bank{i}", [P, 512], F32)) for i in range(2, 8)]
        scores_ps = stack.enter_context(nc.psum_tensor("scores_ps", [P, HK], F32))
        pT_ps = bank[0:2]
        att_ps, xT_ps, h_ps, hy_ps = bank[2], bank[3], bank[4], bank[5]

        rank_ps = bank[4][:, 0:T * E].rearrange("p (t e) -> p t e", e=E)
        count_ps = bank[5][:, 0:E]
        table_ps = bank[3][:, 0:Q]
        gT_ps = [bank[3], bank[2]]
        eh_ps = [bank[4], scores_ps[:, 0:512]]
        ehT_ps = [bank[5], scores_ps[:, 512:1024]]
        ey_ps = [bank[0], bank[1]]

        xn2_dram = nc.dram_tensor("xn2_dram", [TOKENS, D], F32, kind="Internal").ap()
        routed_dram = nc.dram_tensor("routed_dram", [TOPK * TOKENS, D], F32, kind="Internal").ap()

        ld_kv = sem("ld_kv")
        ld_q = sem("ld_q")
        ld_x = [sem("ld_x0"), sem("ld_x1")]
        ld_vo = sem("ld_vo")
        ld_misc = sem("ld_misc")
        ld_sh = sem("ld_sh")
        ld_d = [sem("ld_d0"), sem("ld_d1")]
        pool_held = sem("pool_held")
        const_route = sem("const_route")
        route_step = sem("route_step")
        mask_done = sem("mask_done")
        rank_ps_done = sem("rank_ps_done")
        place_step = sem("place_step")
        hot_place_done = sem("hot_place_done")
        hot_tile_done = sem("hot_tile_done")
        hot_row_done = sem("hot_row_done")
        table_ps_done = sem("table_ps_done")
        src_done = sem("src_done")
        dst_done = sem("dst_done")
        tile_row_done = sem("tile_row_done")
        wd_hi_done = sem("wd_hi_done")
        wd_lo_done = sem("wd_lo_done")
        gat_idx_done = sem("gat_idx_done")
        sct_idx_done = sem("sct_idx_done")
        gathered = [sem(f"gathered{k}") for k in range(RING)]
        scattered = [sem(f"scattered{k}") for k in range(RING)]
        gT_done = sem("gT_done")
        gT_hi_done = sem("gT_hi_done")
        gT_lo_done = sem("gT_lo_done")
        eh_done = sem("eh_done")
        esilu_done = sem("esilu_done")
        ehid_done = sem("ehid_done")
        ehT_done = sem("ehT_done")
        ehT_hi_done = sem("ehT_hi_done")
        ehT_lo_done = sem("ehT_lo_done")
        ey_done = sem("ey_done")
        ycopy_done = sem("ycopy_done")
        routed_loaded = [[sem(f"routed_loaded{k}_{c}") for c in range(T // 2)] for k in range(TOPK)]
        add_step = sem("add_step")
        const_step = sem("const_step")
        const_pick = sem("const_pick")
        gates_done = sem("gates_done")
        ctxT_ps = sem("ctxT_ps")
        ctxT_done = sem("ctxT_done")
        kv_ps = sem("kv_ps")
        kv_done = sem("kv_done")
        wqT_ps = sem("wqT_ps")
        wqT_done = sem("wqT_done")
        A_ps = sem("A_ps")
        A_hi_done = sem("A_hi_done")
        A_done = sem("A_done")
        sbias_ps = sem("sbias_ps")
        sbias_hi = sem("sbias_hi")
        sbias_done = sem("sbias_done")
        B_ps = sem("B_ps")
        B_hi_done = sem("B_hi_done")
        B_done = sem("B_done")
        wsh_hi_done = sem("wsh_hi_done")
        wsh_done = sem("wsh_done")
        stats1_done = sem("stats1_done")
        mv1_done = sem("mv1_done")
        ln1_step = sem("ln1_step")
        xn_done = sem("xn_done")
        xb_done = sem("xb_done")
        xT_done = sem("xT_done")
        xT_hi_done = sem("xT_hi_done")
        xT_lo_done = sem("xT_lo_done")
        scores_done = sem("scores_done")
        max_done = sem("max_done")
        sub_done = sem("sub_done")
        exp_done = sem("exp_done")
        sum_done = sem("sum_done")
        inv_done = sem("inv_done")
        norm_done = sem("norm_done")
        pT_done = sem("pT_done")
        pT_hi_done = sem("pT_hi_done")
        pT_lo_done = sem("pT_lo_done")
        att_done = sem("att_done")
        x2_done = sem("x2_done")
        stats2_done = sem("stats2_done")
        mv2_done = sem("mv2_done")
        ln2_step = sem("ln2_step")
        xn2_done = sem("xn2_done")
        xn2_stored = [sem("xn2_stored0"), sem("xn2_stored1")]
        x2T_done = sem("x2T_done")
        x2T_hi_done = sem("x2T_hi_done")
        x2T_lo_done = sem("x2T_lo_done")
        h_done = sem("h_done")
        logit_done = sem("logit_done")
        tanh_done = sem("tanh_done")
        gact_done = sem("gact_done")
        hid_done = sem("hid_done")
        hT_done = sem("hT_done")
        hT_hi_done = sem("hT_hi_done")
        hT_lo_done = sem("hT_lo_done")
        y_done = sem("y_done")
        yscale_done = sem("yscale_done")
        yadd_done = sem("yadd_done")
        raw_loaded = [sem("raw_loaded0"), sem("raw_loaded1")]
        w_hi_done = sem("w_hi_done")
        w_lo_done = sem("w_lo_done")
        out_stored = sem("out_stored")

        NG = 2
        GC = HP // NG

        def token_loop(eng, step):
            for t in range(-3, 4):
                step(t, t % 2, None)
            with eng.Fori(0, E // 2) as i:
                for k in range(2):
                    step(4 + 2 * i + k, k, i)
            for t in range(4 + E, T + 3):
                step(t, t % 2, None)

        def expert_loop(eng, step):
            turns = (SLOT_TILES - 4 - 2 * RING) // (2 * RING)
            for j in range(-4, 2 * RING):
                step(j, j % RING, None)
            with eng.Fori(0, turns) as i:
                for k in range(2 * RING):
                    step(RING * (2 * i + (2 + k // RING)) + k % RING, k % RING, 2 * i + k // RING)
            for j in range(RING * (2 * turns + 2), SLOT_TILES + 2):
                step(j, j % RING, None)

        def in_tiles(j):
            return not isinstance(j, int) or 0 <= j < SLOT_TILES

        def ring_turn(j, k, i, ahead):
            return (j + ahead) // RING if i is None else i + (2 + (k + ahead) // RING)

        def inside(t):
            return not isinstance(t, int) or 0 <= t < T

        def after(eng, s, n):
            if not isinstance(n, int) or n > 0:
                eng.wait_ge(s, n)

        def store(sp, c):
            b, t = c // (TB // 2), 2 * c % TB
            sp.dma_start(out[b, t * P:(t + 2) * P, :].rearrange("(t p) d -> p t d", p=P),
                         x_sb[:, 2 * c:2 * c + 2, :]).then_inc(out_stored, 16)

        GROUPS = 4
        NPG = TOPK * T // GROUPS

        def group(g):
            return slice(g * NPG, (g + 1) * NPG)

        def load_plane(eng, k):
            eng.wait_ge(ey_done, SLOT_TILES)
            for r in range(RING):
                eng.wait_ge(scattered[r], 16 * len(range(r, SLOT_TILES, RING)))
            for c in range(T // 2):
                row = k * TOKENS + c * 2 * P
                eng.dma_start(plane[k][:, 2 * c:2 * c + 2, :],
                              routed_dram[row:row + 2 * P, :].rearrange("(t p) d -> p t d", p=P)).then_inc(routed_loaded[k][c], 16)

        block = stack.enter_context(nc.Block())

        @block.sync
        def _(sp):
            sp.dma_start(ctx_sb[:, :], ctx_kv.rearrange("b s d -> (b s) d")).then_inc(ld_kv, 16)
            for j, b_in in enumerate((bq, bk, bv)):
                sp.dma_start(bias_rows[j * HP:(j + 1) * HP, :],
                             b_in.rearrange("(c p) f -> c (p f)", p=2)).then_inc(ld_kv, 16)
            sp.dma_start(Wk_sb[:, :, :], Wk.rearrange("(k p) h f -> p k (h f)", p=P)).then_inc(ld_kv, 16)
            sp.dma_start(Wq_sb[:, :, :], Wq.rearrange("(k p) h f -> p k (h f)", p=P)).then_inc(ld_q, 16)
            sp.dma_start(x_sb[:, 0:TB, :], x[0].rearrange("(t p) d -> p t d", p=P)).then_inc(ld_x[0], 16)
            sp.dma_start(Wv_sb[:, :, :], Wv.rearrange("(k p) h f -> p k (h f)", p=P)).then_inc(ld_vo, 16)
            sp.dma_start(Wo_sb[:, :, :], Wo.rearrange("(c p) f d -> (p f) c d", p=2)).then_inc(ld_vo, 16)
            sp.dma_start(raw_sh[:, :, 0:F], Wg_s.rearrange("(k p) f -> p k f", p=P)).then_inc(ld_sh, 16)
            sp.dma_start(raw_sh[:, :, F:2 * F], Wu_s.rearrange("(k p) f -> p k f", p=P)).then_inc(ld_sh, 16)
            sp.dma_start(raw_sh[:, :, 2 * F:], W_router.rearrange("(k p) e -> p k e", p=P)).then_inc(ld_sh, 16)
            sp.dma_start(raw_ds[:, :, :], Wd_s.rearrange("(k p) d -> p k d", p=FH)).then_inc(ld_sh, 16)
            sp.dma_start(x_sb[:, TB:T, :], x[1].rearrange("(t p) d -> p t d", p=P)).then_inc(ld_x[1], 16)

            sp.wait_ge(B_done, 2 * HP)
            sp.wait_ge(wsh_done, 2)

            def step(t, q, i):
                if i is not None:
                    e = 2 * i + q
                    sp.wait_ge(xb_done, t + 1)
                    for half, W in enumerate((Wg, Wu)):
                        sp.dma_start(raw_w[q][:, :, half * F:(half + 1) * F],
                                     W[bass.ds(e, 1), :, :].rearrange("o (k p) f -> p (o k) f", p=P)).then_inc(raw_loaded[q], 16)
                if isinstance(t, int) and T - 4 <= t < T:
                    n = t - (T - 4)
                    if n < 2:
                        sp.wait_ge(w_lo_done, E)
                    else:
                        sp.wait_ge(wd_lo_done, n - 1)
                    sp.dma_start(raw_d[n % 2][:, :, :],
                                 Wd[2 * n:2 * n + 2].rearrange("e (k p) d -> p (e k) d", p=FH)).then_inc(ld_d[n % 2], 16)
                w = t - 1
                if inside(w):
                    sp.wait_ge(xn2_done, w + 1)
                    sp.dma_start(xn2_dram[bass.ds(w * P, P), :], xn2[1 - q][:, :]).then_inc(xn2_stored[1 - q], 16)

            token_loop(sp, step)
            load_plane(sp, 0)
            for c in range(T // 2):
                sp.wait_ge(add_step, 4 * (c + 1))
                store(sp, c)
            sp.wait_ge(out_stored, 16 * (T // 2))

        @block.gpsimd
        def _(pool):
            pool.dma_start(gates[:, 0:1], g_xattn.partition_broadcast(P)).then_inc(ld_misc, 16)
            pool.dma_start(gates[:, 1:2], g_ffn.partition_broadcast(P)).then_inc(ld_misc, 16)
            pool.dma_start(bo_row[:, :], bo.partition_broadcast(P)).then_inc(ld_misc, 16)
            nc.gpsimd.memset(ident[:, :], 0.0).then_inc(const_step, 1)
            nc.gpsimd.memset(minus_half[:, :], -0.5).then_inc(const_step, 1)
            nc.gpsimd.memset(eps_col[:, :], LN_EPS).then_inc(const_step, 1)
            nc.gpsimd.memset(minus_one[:, :], -1.0).then_inc(const_step, 1)
            nc.gpsimd.memset(pick_rows[:, :].bitcast(F32), 0.0).then_inc(const_pick, 1)
            pool.wait_ge(const_step, 4)
            nc.gpsimd.affine_select(out=ident[:, :], in_=ident[:, :], compare_op=ALU.not_equal, fill=1.0,
                                    base=0, pattern=[[-1, P]], channel_multiplier=1).then_inc(const_step, 1)
            pool.wait_ge(const_step, 5)
            nc.gpsimd.memset(score_bias[64:P, :, :].bitcast(F32), 0.0).then_inc(const_pick, 1)
            pool.wait_ge(const_pick, 2)
            nc.gpsimd.memset(pick_rows[0:1, :].bitcast(F32), 1.0).then_inc(const_pick, 1)
            pool.wait_ge(const_pick, 3)
            nc.gpsimd.memset(pick_rows[32:33, :].bitcast(F32), 1.0).then_inc(const_pick, 1)

            pool.wait_ge(const_pick, 4)
            pool.dma_start(expert_b[:, :], expert_bias.partition_broadcast(P)).then_inc(ld_misc, 16)
            nc.gpsimd.iota(iota_e[:, :], [[1, E]], base=0, channel_multiplier=0,
                           allow_small_or_imprecise_dtypes=True).then_inc(const_route, 1)
            nc.gpsimd.iota(iota_e8[:, :], [[1, E]], base=-E, channel_multiplier=0,
                           allow_small_or_imprecise_dtypes=True).then_inc(const_route, 1)
            nc.gpsimd.iota(iota_q[:, :], [[1, Q]], base=0, channel_multiplier=0,
                           allow_small_or_imprecise_dtypes=True).then_inc(const_route, 1)
            nc.gpsimd.iota(iota_p[:, :], [[1, P]], base=0, channel_multiplier=0,
                           allow_small_or_imprecise_dtypes=True).then_inc(const_route, 1)
            nc.gpsimd.iota(pair_row[:, :], [[TOKENS, TOPK], [P, T]], base=1, channel_multiplier=1,
                           allow_small_or_imprecise_dtypes=True).then_inc(const_route, 1)
            nc.gpsimd.iota(before[:, :, :], [[-1, E], [1, E]], base=0, channel_multiplier=0,
                           allow_small_or_imprecise_dtypes=True).then_inc(const_route, 1)
            nc.gpsimd.memset(zero_i[:, :], 0).then_inc(const_route, 1)
            nc.gpsimd.memset(tile_row[:, :], 0).then_inc(const_route, 1)
            nc.gpsimd.memset(ones_r[:, :].bitcast(F32), 1.0).then_inc(const_route, 1)
            nc.gpsimd.memset(upper_f[:, :], 1.0).then_inc(const_route, 1)
            pool.wait_ge(const_route, 10)
            nc.gpsimd.affine_select(out=upper_f[:, :], in_=upper_f[:, :], compare_op=ALU.is_gt, fill=0.0,
                                    base=0, pattern=[[1, P]], channel_multiplier=-1).then_inc(const_route, 1)

            pool.wait_ge(mv1_done, T)
            nc.gpsimd.tensor_scalar(ve1[:, :], mv1[:, :, 1], LN_EPS, None, ALU.add).then_inc(ln1_step, 1)
            pool.wait_ge(ln1_step, 1)
            nc.gpsimd.tensor_tensor(rstd1[:, :], ve1[:, :], minus_half[:, :], ALU.pow).then_inc(ln1_step, 1)
            pool.wait_ge(ln1_step, 2)
            nc.gpsimd.tensor_tensor(shift1[:, :], mv1[:, :, 0], rstd1[:, :], ALU.mult).then_inc(ln1_step, 1)
            pool.wait_ge(ln1_step, 3)
            nc.gpsimd.tensor_scalar(shift1[:, :], shift1[:, :], -1.0, None, ALU.mult).then_inc(ln1_step, 1)
            pool.wait_ge(ln1_step, 4)
            pool.wait_ge(ld_misc, 64)

            def step(t, q, i):
                w, m, u, z = t - 1, t + 1, t + 2, t - 3
                if inside(u):
                    pool.wait_ge(xn_done, u + 1)
                    nc.gpsimd.tensor_tensor(x_sb[:, bass.ds(u, 1), :], x_sb[:, bass.ds(u, 1), :], bo_row[:, :],
                                            ALU.add).then_inc(xb_done, 1)
                if inside(w):
                    pool.wait_ge(mv2_done, w + 1)
                    after(pool, xn2_done, w)
                    nc.gpsimd.tensor_tensor(ve2[:, :], mv2[:, 1:2], eps_col[:, :], ALU.add).then_inc(ln2_step, 1)
                    nc.gpsimd.tensor_tensor(neg_mean2[:, :], mv2[:, 0:1], minus_one[:, :], ALU.mult).then_inc(ln2_step, 1)
                    pool.wait_ge(ln2_step, 4 * w + 1)
                    nc.gpsimd.tensor_tensor(rstd2[:, :], ve2[:, :], minus_half[:, 0:1], ALU.pow).then_inc(ln2_step, 1)
                    pool.wait_ge(ln2_step, 4 * w + 3)
                    nc.gpsimd.tensor_tensor(shift2[:, :], neg_mean2[:, :], rstd2[:, :], ALU.mult).then_inc(ln2_step, 1)
                if inside(m):
                    pool.wait_ge(inv_done, m + 1)
                    pr = prob[1 - q][:, :].rearrange("p (h k) -> p h k", k=KV)
                    nc.gpsimd.tensor_tensor(pr, pr, row_inv[:, :].unsqueeze(2).to_broadcast([P, H, KV]),
                                            ALU.mult).then_inc(norm_done, 1)
                if inside(z):
                    pool.wait_ge(yscale_done, z + 1)
                    pool.wait_ge(xn2_done, z + 1)
                    nc.gpsimd.tensor_tensor(x_sb[:, bass.ds(z, 1), :], y_sb[1 - q][:, :], x_sb[:, bass.ds(z, 1), :],
                                            ALU.add).then_inc(yadd_done, 1)
                if i is not None:
                    e = 2 * i + q
                    pool.wait_ge(w_hi_done, e + 1)
                    nc.gpsimd.tensor_tensor(W_lo[:, bass.ds(KC * e, KC), :], raw_w[q],
                                            W_hi[:, bass.ds(KC * e, KC), :].bitcast(F32), ALU.subtract).then_inc(w_lo_done, 1)
                if isinstance(t, int) and T - 2 <= t < T + 2:
                    n = t - (T - 2)
                    part = slice(4 * n, 4 * n + 4)
                    pool.wait_ge(wd_hi_done, n + 1)
                    nc.gpsimd.tensor_tensor(Wd_lo[:, part, :], raw_d[n % 2][:, :, :],
                                            Wd_hi[:, part, :].bitcast(F32), ALU.subtract).then_inc(wd_lo_done, 1)

            token_loop(pool, step)

            def hold():
                pool.sem_inc(pool_held, 1)

            for g in range(GROUPS):
                pool.wait_ge(hot_tile_done, g + 1)
                nc.gpsimd.tensor_tensor(onehot_q[:, group(g), :], onehot_q[:, group(g), :].bitcast(F32),
                                        pair_row[:, group(g)].unsqueeze(2).to_broadcast([P, NPG, Q]),
                                        ALU.mult).then_inc(hot_row_done, 1)

            for q in range(2):
                pool.wait_ge(xn2_stored[q], 16 * (T // 2))

            def expert_step(j, k, i):
                n, s = j + 4, j - 2
                kn, ks = (k + 4) % RING, (k - 2) % RING
                if in_tiles(n):
                    after(pool, gT_done, j + 1)
                    pool.wait_ge(gat_idx_done, n + 1)
                    hold()
                    nc.gpsimd.indirect_dma_start(xg[kn][:, :], None, xn2_dram[:, :],
                                                 bass.IndirectOffsetOnAxis(ap=gat_idx[kn][:, 0:1], axis=0)).then_inc(gathered[kn], 16)
                if in_tiles(s):
                    pool.wait_ge(sct_idx_done, s + 1)
                    pool.wait_ge(ycopy_done, s + 1)
                    hold()
                    nc.gpsimd.indirect_dma_start(routed_dram[:, :], bass.IndirectOffsetOnAxis(ap=sct_idx[ks][:, 0:1], axis=0),
                                                 y_sb[ks][:, :], None, bounds_check=TOPK * TOKENS - 1,
                                                 oob_is_err=False).then_inc(scattered[ks], 16)

            expert_loop(pool, expert_step)

        @block.scalar
        def _(act):
            act.wait_ge(ld_misc, 64)
            nc.scalar.activation(tgate[:, :], gates[:, :], ACT.Tanh).then_inc(gates_done, 1)
            act.wait_ge(gates_done, 1)
            nc.scalar.activation(bo_row[:, :], bo_row[:, :], ACT.Copy, scale=tgate[:, 0:1]).then_inc(gates_done, 1)
            nc.scalar.activation(half_tgf[:, :], tgate[:, 1:2], ACT.Copy, scale=0.5).then_inc(gates_done, 1)
            for j in range(HP // 2):
                act.wait_ge(wqT_ps, j + 1)
                nc.scalar.activation(WqT[:, 2 * j:2 * j + 2, :], bank[j][:, :].rearrange("p (c d) -> p c d", c=2),
                                     ACT.Copy).then_inc(wqT_done, 1)
            j = 0
            for kc in range(KC):
                for g in range(NG):
                    for p in range(2):
                        act.wait_ge(A_ps, j + 1)
                        nc.scalar.activation(A_out(A_hi, kc, g, p), A_in(fold_bank(bank, scores_ps, j)),
                                             ACT.Copy).then_inc(A_hi_done, 1)
                        j += 1
            j = 0
            for g in range(NG):
                for p in range(2):
                    act.wait_ge(sbias_ps, j + 1)
                    nc.scalar.activation(S_out(score_bias, g, p, 0), S_in(fold_bank(bank, scores_ps, j), 0),
                                         ACT.Copy).then_inc(sbias_hi, 1)
                    j += 1
            for j in range(2 * HP):
                c, p = j // 2, j % 2
                act.wait_ge(B_ps, j + 1)
                nc.scalar.activation(B_hi[64 * p:64 * p + 64, :, c, :],
                                     fold_bank(bank, scores_ps, j)[64 * p:64 * p + 64, :].rearrange("p (b d) -> p b d", b=B),
                                     ACT.Copy, scale=tgate[64 * p:64 * p + 64, 0:1]).then_inc(B_hi_done, 1)
            act.wait_ge(ld_sh, 64)
            nc.scalar.activation(Wsh_hi[:, :, :], raw_sh[:, :, :], ACT.Copy).then_inc(wsh_hi_done, 1)
            nc.scalar.activation(Wds_hi[:, :, :], raw_ds[:, :, :], ACT.Copy).then_inc(wsh_hi_done, 1)

            act.wait_ge(const_route, 11)
            nc.scalar.activation(upper[:, :], upper_f[:, :], ACT.Copy).then_inc(mask_done, 1)
            act.wait_ge(ln1_step, 4)

            def step(t, q, i):
                u, v, m, w, n, z = t + 2, t - 2, t + 1, t - 1, t + 3, t - 3
                if inside(m):
                    act.wait_ge(sub_done, m + 1)
                    nc.scalar.activation(prob[1 - q][:, :], prob[1 - q][:, :], ACT.Exp).then_inc(exp_done, 1)
                if inside(u):
                    act.wait_ge(xT_done, u + 1)
                    after(act, scores_done, u - 1)
                    nc.scalar.activation(xnT_hi[q][:, :, :], xT_ps[:, 0:D].rearrange("p (k s) -> p k s", k=KC),
                                         ACT.Copy).then_inc(xT_hi_done, 1)
                if inside(t):
                    for h in range(2):
                        act.wait_ge(pT_done, 2 * t + h + 1)
                        if h == 0:
                            after(act, att_done, t)
                        nc.scalar.activation(pT_hi[:, 4 * h:4 * h + 4, :],
                                             pT_ps[h][:, :].rearrange("p (c s) -> p c s", c=4),
                                             ACT.Copy).then_inc(pT_hi_done, 1)
                if inside(n):
                    after(act, xT_done, n - 1)
                    nc.scalar.activation(xn[1 - q][:, :], x_sb[:, bass.ds(n, 1), :], ACT.Identity,
                                         scale=rstd1[:, bass.ds(n, 1)], bias=shift1[:, bass.ds(n, 1)]).then_inc(xn_done, 1)
                if inside(z):
                    act.wait_ge(y_done, z + 1)
                    after(act, yadd_done, z - 1)
                    nc.scalar.activation(y_sb[1 - q][:, :], hy_ps[:, 0:D], ACT.Copy,
                                         scale=half_tgf[:, 0:1]).then_inc(yscale_done, 1)
                if inside(v):
                    act.wait_ge(h_done, v + 1)
                    nc.scalar.activation(exp_neg[:, bass.ds(v, 1), :], h_ps[:, 2 * F:2 * F + E], ACT.Exp,
                                         scale=-1.0).then_inc(logit_done, 1)
                    after(act, gact_done, v)
                    nc.scalar.activation(tanh_g[:, :], h_ps[:, 0:F], ACT.Tanh, scale=0.5).then_inc(tanh_done, 1)
                if inside(w):
                    after(act, x2T_done, w - 1)
                    if isinstance(w, int):
                        after(act, xn2_stored[1 - q], 16 * (w // 2))
                    else:
                        act.wait_ge(xn2_stored[1 - q], 8 * (w - (1 - q)))
                    act.wait_ge(ln2_step, 4 * w + 4)
                    nc.scalar.activation(xn2[1 - q][:, :], x_sb[:, bass.ds(w, 1), :], ACT.Identity,
                                         scale=rstd2[:, 0:1], bias=shift2[:, 0:1]).then_inc(xn2_done, 1)
                if inside(v):
                    act.wait_ge(hT_done, v + 1)
                    after(act, y_done, v)
                    nc.scalar.activation(hT_hi[:, :, :], hy_ps[0:FH, 0:2 * P].rearrange("p (k s) -> p k s", k=2),
                                         ACT.Copy).then_inc(hT_hi_done, 1)
                if inside(w):
                    act.wait_ge(x2T_done, w + 1)
                    after(act, h_done, w - 1)
                    nc.scalar.activation(xn2T_hi[1 - q][:, :, :], xT_ps[:, 0:D].rearrange("p (k s) -> p k s", k=KC),
                                         ACT.Copy).then_inc(x2T_hi_done, 1)
                if i is not None:
                    act.wait_ge(raw_loaded[q], 32 * (i + 1))
                    nc.scalar.activation(W_hi[:, bass.ds(KC * (2 * i + q), KC), :], raw_w[q], ACT.Copy).then_inc(w_hi_done, 1)
                if isinstance(t, int) and T - 2 <= t < T + 2:
                    n = t - (T - 2)
                    part = slice(4 * n, 4 * n + 4)
                    act.wait_ge(ld_d[n % 2], 16 * (n // 2 + 1))
                    act.wait_ge(scores_done, T)
                    nc.scalar.activation(Wd_hi[:, part, :], raw_d[n % 2][:, :, :], ACT.Copy).then_inc(wd_hi_done, 1)

            token_loop(act, step)

            def expert_step(j, k, i):
                n, d = j + 2, j - 1
                if in_tiles(d):
                    act.wait_ge(ehT_done, d + 1)
                    after(act, ey_done, d)
                    nc.scalar.activation(hT_hi[:, :, :], ehT_ps[(k + 1) % 2][0:FH, 0:2 * P].rearrange("p (k s) -> p k s", k=2),
                                         ACT.Copy).then_inc(ehT_hi_done, 1)
                if in_tiles(j):
                    act.wait_ge(eh_done, j + 1)
                    after(act, ehid_done, j)
                    nc.scalar.activation(gate_act[:, :], eh_ps[k % 2][:, 0:F], ACT.Silu).then_inc(esilu_done, 1)
                if in_tiles(n):
                    act.wait_ge(gT_done, n + 1)
                    after(act, eh_done, n - 1)
                    nc.scalar.activation(xnT_hi[k % 2][:, :, :], gT_ps[k % 2][:, 0:D].rearrange("p (k s) -> p k s", k=KC),
                                         ACT.Copy).then_inc(gT_hi_done, 1)

            nc.scalar.activation(silu_first[:, :], half_tgf[:, :], ACT.Silu)
            expert_loop(act, expert_step)
            load_plane(act, 1)

        @block.vector
        def _(dve):
            dve.wait_ge(ctxT_ps, 1)
            nc.vector.tensor_copy(ctxT[:, :, :], bank[0][:, 0:KC * P].rearrange("p (k s) -> p k s", k=KC)).then_inc(ctxT_done, 1)
            nc.vector.tensor_copy(bias_cols[:, :], bank[0][:, 256:256 + 3 * HP]).then_inc(ctxT_done, 1)
            dve.wait_ge(ctxT_done, 2)
            for c in range(HP):
                dve.wait_ge(kv_ps, c // GC + 1)
                nc.vector.tensor_scalar(kT[:, c, :], bank[4 + c // GC][:, (c % GC) * P:(c % GC + 1) * P],
                                        bias_cols[:, HP + c:HP + c + 1], DH ** -0.5, ALU.add, ALU.mult).then_inc(kv_done, 1)
            j = 0
            for kc in range(KC):
                for g in range(NG):
                    for p in range(2):
                        dve.wait_ge(A_hi_done, j + 1)
                        nc.vector.tensor_tensor(A_out(A_lo, kc, g, p), A_in(fold_bank(bank, scores_ps, j)),
                                                A_out(A_hi, kc, g, p).bitcast(F32), ALU.subtract).then_inc(A_done, 1)
                        j += 1
            j = 0
            for g in range(NG):
                for p in range(2):
                    dve.wait_ge(sbias_hi, j + 1)
                    nc.vector.tensor_tensor(S_out(score_bias, g, p, 32), S_in(fold_bank(bank, scores_ps, j), 32),
                                            S_out(score_bias, g, p, 32).bitcast(F32), ALU.subtract).then_inc(sbias_done, 1)
                    j += 1
            for t in range(T):
                if t % TB == 0:
                    dve.wait_ge(ld_x[t // TB], 16)
                nc.vector.bn_stats(stats1[:, t, :], x_sb[:, t, :]).then_inc(stats1_done, 1)
            for t in range(T):
                dve.wait_ge(stats1_done, t + 1)
                nc.vector.bn_aggr(mv1[:, t, :], stats1[:, t, :]).then_inc(mv1_done, 1)
            for c in range(HP):
                dve.wait_ge(kv_ps, NG + c // GC + 1)
                nc.vector.tensor_scalar(vT[:, c, :], bank[4 + c // GC][:, (c % GC) * P:(c % GC + 1) * P],
                                        bias_cols[:, 2 * HP + c:2 * HP + c + 1], None, ALU.add).then_inc(kv_done, 1)
            for j in range(2 * HP):
                c, p = j // 2, j % 2
                rows = slice(64 * p, 64 * p + 64)
                dve.wait_ge(B_hi_done, j + 1)
                nc.vector.scalar_tensor_tensor(out=B_lo[rows, :, c, :],
                                               in0=fold_bank(bank, scores_ps, j)[rows, :].rearrange("p (b d) -> p b d", b=B),
                                               scalar=tgate[rows, 0:1], in1=B_hi[rows, :, c, :].bitcast(F32),
                                               op0=ALU.mult, op1=ALU.subtract).then_inc(B_done, 1)
            dve.wait_ge(wsh_hi_done, 1)
            nc.vector.tensor_tensor(Wsh_lo[:, :, :], raw_sh[:, :, :], Wsh_hi[:, :, :].bitcast(F32),
                                    ALU.subtract).then_inc(wsh_done, 1)
            dve.wait_ge(wsh_hi_done, 2)
            nc.vector.tensor_tensor(Wds_lo[:, :, :], raw_ds[:, :, :], Wds_hi[:, :, :].bitcast(F32),
                                    ALU.subtract).then_inc(wsh_done, 1)

            def step(t, q, i):
                u, v, m, w = t + 2, t - 2, t + 1, t - 1
                sc = scores_ps[:, :].rearrange("p (h k) -> p h k", k=KV)

                def pT_low(h):
                    dve.wait_ge(pT_hi_done, 2 * t + h + 1)
                    nc.vector.tensor_tensor(pT_lo[:, 4 * h:4 * h + 4, :], pT_ps[h][:, :].rearrange("p (c s) -> p c s", c=4),
                                            pT_hi[:, 4 * h:4 * h + 4, :].bitcast(F32), ALU.subtract).then_inc(pT_lo_done, 1)

                if inside(u):
                    dve.wait_ge(xT_hi_done, u + 1)
                    nc.vector.tensor_tensor(xnT_lo[q][:, :, :], xT_ps[:, 0:D].rearrange("p (k s) -> p k s", k=KC),
                                            xnT_hi[q][:, :, :].bitcast(F32), ALU.subtract).then_inc(xT_lo_done, 1)
                if inside(t):
                    pT_low(0)
                    pT_low(1)
                if inside(m):
                    dve.wait_ge(exp_done, m + 1)
                    after(dve, inv_done, m)
                    nc.vector.tensor_reduce(row_sum[:, :], prob[1 - q][:, :].rearrange("p (h k) -> p h k", k=KV),
                                            AX_X, ALU.add).then_inc(sum_done, 1)
                    dve.wait_ge(sum_done, m + 1)
                    after(dve, norm_done, m)
                    nc.vector.reciprocal(row_inv[:, :], row_sum[:, :]).then_inc(inv_done, 1)
                if inside(v):
                    dve.wait_ge(tanh_done, v + 1)
                    after(dve, hid_done, v)
                    nc.vector.scalar_tensor_tensor(out=gate_act[:, :], in0=tanh_g[:, :], scalar=1.0, in1=h_ps[:, 0:F],
                                                   op0=ALU.add, op1=ALU.mult).then_inc(gact_done, 1)
                    dve.wait_ge(gact_done, v + 1)
                    after(dve, hT_done, v)
                    nc.vector.tensor_tensor(hid[:, :], gate_act[:, :], h_ps[:, F:2 * F], ALU.mult).then_inc(hid_done, 1)
                if inside(u):
                    dve.wait_ge(scores_done, u + 1)
                    after(dve, sub_done, u)
                    nc.vector.tensor_reduce(row_max[:, :], sc, AX_X, ALU.max).then_inc(max_done, 1)
                if inside(v):
                    dve.wait_ge(hT_hi_done, v + 1)
                    nc.vector.tensor_tensor(hT_lo[:, :, :], hy_ps[0:FH, 0:2 * P].rearrange("p (k s) -> p k s", k=2),
                                            hT_hi[:, :, :].bitcast(F32), ALU.subtract).then_inc(hT_lo_done, 1)
                if inside(w):
                    dve.wait_ge(x2T_hi_done, w + 1)
                    nc.vector.tensor_tensor(xn2T_lo[1 - q][:, :, :], xT_ps[:, 0:D].rearrange("p (k s) -> p k s", k=KC),
                                            xn2T_hi[1 - q][:, :, :].bitcast(F32), ALU.subtract).then_inc(x2T_lo_done, 1)
                if inside(u):
                    dve.wait_ge(max_done, u + 1)
                    after(dve, pT_done, 2 * t + 2)
                    nc.vector.tensor_tensor(prob[q][:, :].rearrange("p (h k) -> p h k", k=KV), sc,
                                            row_max[:, :].unsqueeze(2).to_broadcast([P, H, KV]),
                                            ALU.subtract).then_inc(sub_done, 1)
                if inside(t):
                    dve.wait_ge(att_done, t + 1)
                    dve.wait_ge(xb_done, t + 1)
                    nc.vector.tensor_tensor(x_sb[:, bass.ds(t, 1), :], att_ps[:, 0:D], x_sb[:, bass.ds(t, 1), :],
                                            ALU.add).then_inc(x2_done, 1)
                    dve.wait_ge(x2_done, t + 1)
                    after(dve, mv2_done, t)
                    carry_waits()
                    nc.vector.bn_stats(stats2[:, :], x_sb[:, bass.ds(t, 1), :]).then_inc(stats2_done, 1)
                    dve.wait_ge(stats2_done, t + 1)
                    after(dve, ln2_step, 4 * t)
                    carry_waits()
                    nc.vector.bn_aggr(mv2[:, :], stats2[:, :]).then_inc(mv2_done, 1)

            def carry_waits():
                nc.vector.tensor_copy(carrier[:, :], ident[:, 0:1])

            dve.wait_ge(gates_done, 3)
            dve.wait_ge(const_step, 5)
            token_loop(dve, step)

            steps = [0]

            def chain(ins):
                steps[0] += 1
                ins.then_inc(route_step, 1)
                dve.wait_ge(route_step, steps[0])

            def over_t(ap):
                return ap.unsqueeze(1).to_broadcast([P, T, E])

            def over_e(ap):
                return ap.unsqueeze(2).to_broadcast([P, T, E])

            def scores_and_choice(a, b):
                part = score[:, a:b, :]
                chain(nc.vector.tensor_scalar(part, exp_neg[:, a:b, :], 1.0, None, ALU.add))
                chain(nc.vector.reciprocal(part, part))
                chain(nc.vector.tensor_tensor(choice[:, a:b, :], part,
                                              expert_b[:, :].unsqueeze(1).to_broadcast([P, b - a, E]), ALU.add))

            dve.wait_ge(const_route, 11)
            dve.wait_ge(ld_misc, 64)
            dve.wait_ge(logit_done, T)
            scores_and_choice(0, T)
            nc.vector.tensor_scalar(before[:, :, :], before[:, :, :], 0.0, float(P), ALU.is_lt, ALU.mult)
            for k in range(TOPK):
                chain(nc.vector.tensor_reduce(best[:, :], choice[:, :, :], AX_X, ALU.max))
                chain(nc.vector.tensor_tensor(cand[:, :, :], choice[:, :, :], over_e(best[:, :]), ALU.is_equal))
                chain(nc.vector.scalar_tensor_tensor(out=cand[:, :, :], in0=cand[:, :, :], scalar=-float(E),
                                                     in1=over_t(iota_e[:, :]), op0=ALU.mult, op1=ALU.add))
                chain(nc.vector.tensor_reduce(first_e[:, :], cand[:, :, :], AX_X, ALU.min))
                chain(nc.vector.tensor_tensor(hot[:, k, :, :], over_t(iota_e8[:, :]), over_e(first_e[:, :]), ALU.is_equal))
                if k == 0:
                    chain(nc.vector.scalar_tensor_tensor(out=choice[:, :, :], in0=hot[:, 0, :, :], scalar=-BIG,
                                                         in1=choice[:, :, :], op0=ALU.mult, op1=ALU.add))
            chain(nc.vector.tensor_tensor(mask[:, :, :], hot[:, 0, :, :], hot[:, 1, :, :], ALU.add))
            src, reach, turn = mask, 1, 0
            while reach < T:
                dst = upto[turn % 2]
                nc.vector.tensor_copy(dst[:, 0:reach, :], src[:, 0:reach, :].bitcast(F32))
                chain(nc.vector.tensor_tensor(dst[:, reach:T, :], src[:, reach:T, :].bitcast(F32),
                                              src[:, 0:T - reach, :].bitcast(F32), ALU.add))
                src, reach, turn = dst, 2 * reach, turn + 1
            assert src is upto[1]
            nc.vector.tensor_copy(carrier[:, :], ident[:, 0:1]).then_inc(mask_done, 1)

            def of_both_choices(ap):
                chain(nc.vector.tensor_tensor(hot_val[:, :, :, :], hot[:, :, :, :],
                                              ap.unsqueeze(1).to_broadcast([P, TOPK, T, E]), ALU.mult))

            dve.wait_ge(rank_ps_done, 1)
            chain(nc.vector.tensor_scalar(count_i[:, :], count_ps, float(P - 1), None, ALU.add))
            chain(nc.vector.tensor_scalar(count_i[:, :], count_i[:, :], P.bit_length() - 1, None, ALU.logical_shift_right))
            chain(nc.vector.tensor_copy(tiles_f[:, :], count_i[:, :]))
            chain(nc.vector.tensor_tensor(start_prod[:, :, :], before[:, :, :],
                                          tiles_f[:, :].unsqueeze(1).to_broadcast([P, E, E]), ALU.mult))
            chain(nc.vector.tensor_reduce(start_f[:, :], start_prod[:, :, :], AX_X, ALU.add))
            chain(nc.vector.tensor_tensor(choice[:, :, :], rank_ps, over_t(start_f[:, :]), ALU.add))
            of_both_choices(choice[:, :, :])
            chain(nc.vector.tensor_reduce(slot[:, :, :], hot_val[:, :, :, :], AX_X, ALU.add))
            chain(nc.vector.tensor_copy(slot_i[:, :], slot[:, :, :].rearrange("p k t -> p (k t)")))
            nc.vector.tensor_scalar(tile_i[:, :], slot_i[:, :], P.bit_length() - 1, None, ALU.logical_shift_right).then_inc(place_step, 1)
            nc.vector.tensor_scalar(place_i[:, :], slot_i[:, :], P - 1, None, ALU.bitwise_and).then_inc(place_step, 1)
            dve.wait_ge(place_step, 1)
            chain(nc.vector.tensor_copy(slot_q[:, :], tile_i[:, :]))
            dve.wait_ge(place_step, 2)
            chain(nc.vector.tensor_copy(slot_p[:, :], place_i[:, :]))
            dve.wait_ge(att_done, T)

            for g in range(GROUPS):
                part = group(g)
                nc.vector.tensor_tensor(onehot_q[:, part, :], iota_q[:, :].unsqueeze(1).to_broadcast([P, NPG, Q]),
                                        slot_q[:, part].unsqueeze(2).to_broadcast([P, NPG, Q]),
                                        ALU.is_equal).then_inc(hot_tile_done, 1)
                nc.vector.tensor_tensor(onehot_p[:, part, :], iota_p[:, :].unsqueeze(1).to_broadcast([P, NPG, P]),
                                        slot_p[:, part].unsqueeze(2).to_broadcast([P, NPG, P]),
                                        ALU.is_equal).then_inc(hot_place_done, 1)
            chain(nc.vector.scalar_tensor_tensor(out=end_f[:, :], in0=start_f[:, :], scalar=1.0 / P, in1=tiles_f[:, :],
                                                 op0=ALU.mult, op1=ALU.add))
            chain(nc.vector.tensor_tensor(tile_cmp[:, :, :], iota_q[0:1, :].unsqueeze(2).to_broadcast([1, Q, E]),
                                          end_f[0:1, :].unsqueeze(1).to_broadcast([1, Q, E]), ALU.is_ge))
            chain(nc.vector.tensor_reduce(tile_e[:, :], tile_cmp[:, :, :], AX_X, ALU.add))
            nc.vector.tensor_scalar(tile_row[:, RING:RING + Q], tile_e[:, :], float(E - 1), float(KC), ALU.min,
                                    ALU.mult).then_inc(tile_row_done, 1)
            dve.wait_ge(table_ps_done, 1)
            chain(nc.vector.tensor_copy(table[:, :], table_ps))
            chain(nc.vector.tensor_scalar(src_i[:, :], table[:, :], -1.0, 0.0, ALU.add, ALU.max))
            nc.vector.tensor_scalar(src_i[:, :], src_i[:, :], TOKENS - 1, None, ALU.bitwise_and).then_inc(src_done, 1)
            chain(nc.vector.tensor_scalar(pad_far[:, :], table[:, :], 0.0, FAR, ALU.is_equal, ALU.mult))
            nc.vector.scalar_tensor_tensor(out=dst_i[:, :], in0=table[:, :], scalar=-1.0, in1=pad_far[:, :],
                                           op0=ALU.add, op1=ALU.add).then_inc(dst_done, 1)
            dve.wait_ge(src_done, 1)
            dve.wait_ge(dst_done, 1)
            dve.wait_ge(yadd_done, T)

            def weigh():
                of_both_choices(score[:, :, :])
                chain(nc.vector.tensor_reduce(picked[:, :, :], hot_val[:, :, :, :], AX_X, ALU.add))
                chain(nc.vector.tensor_tensor(den[:, :], picked[:, 0, :], picked[:, 1, :], ALU.add))
                chain(nc.vector.tensor_scalar(den[:, :], den[:, :], ROUTE_EPS, None, ALU.add))
                chain(nc.vector.reciprocal(den[:, :], den[:, :]))
                chain(nc.vector.tensor_scalar(den[:, :], den[:, :], tgate[:, 1:2], None, ALU.mult))
                for k in range(TOPK):
                    nc.vector.tensor_tensor(weight[k][:, :], picked[:, k, :], den[:, :], ALU.mult)

            def expert_step(j, k, i):
                n, d, g, c = j + 2, j - 1, j + 4, j - 2
                kc = (k - 2) % RING
                if isinstance(j, int) and j < 0:
                    if j == -RING:
                        for r in range(RING):
                            nc.vector.tensor_copy(gat_idx[r][:, :], src_i[:, r:r + 1]).then_inc(gat_idx_done, 1)
                        weigh()
                elif in_tiles(g):
                    after(dve, gathered[k], 16 * ring_turn(j, k, i, 4))
                    nc.vector.tensor_copy(gat_idx[k][:, :], src_i[:, bass.ds(g, 1)]).then_inc(gat_idx_done, 1)
                if in_tiles(c):
                    after(dve, scattered[kc], 16 * ring_turn(j, k, i, -2))
                    nc.vector.tensor_copy(sct_idx[kc][:, :], dst_i[:, bass.ds(c, 1)]).then_inc(sct_idx_done, 1)
                    dve.wait_ge(ey_done, c + 1)
                    nc.vector.tensor_copy(y_sb[kc][:, :], ey_ps[k % 2][:, 0:D]).then_inc(ycopy_done, 1)
                if in_tiles(d):
                    dve.wait_ge(ehT_hi_done, d + 1)
                    nc.vector.tensor_tensor(hT_lo[:, :, :], ehT_ps[(k + 1) % 2][0:FH, 0:2 * P].rearrange("p (k s) -> p k s", k=2),
                                            hT_hi[:, :, :].bitcast(F32), ALU.subtract).then_inc(ehT_lo_done, 1)
                if in_tiles(j):
                    dve.wait_ge(esilu_done, j + 1)
                    after(dve, ehT_done, j)
                    nc.vector.tensor_tensor(hid[:, :], gate_act[:, :], eh_ps[k % 2][:, F:2 * F], ALU.mult).then_inc(ehid_done, 1)
                if in_tiles(n):
                    dve.wait_ge(gT_hi_done, n + 1)
                    nc.vector.tensor_tensor(xnT_lo[k % 2][:, :, :], gT_ps[k % 2][:, 0:D].rearrange("p (k s) -> p k s", k=KC),
                                            xnT_hi[k % 2][:, :, :].bitcast(F32), ALU.subtract).then_inc(gT_lo_done, 1)

            expert_loop(dve, expert_step)

            for c in range(T // 2):
                for k in range(TOPK):
                    dve.wait_ge(routed_loaded[k][c], 16)
                    for h in range(2):
                        t = 2 * c + h
                        if k:
                            dve.wait_ge(add_step, 4 * c + h + 1)
                        nc.vector.scalar_tensor_tensor(out=x_sb[:, t, :], in0=plane[k][:, t, :],
                                                       scalar=weight[k][:, t:t + 1], in1=x_sb[:, t, :],
                                                       op0=ALU.mult, op1=ALU.add).then_inc(add_step, 1)

        @block.tensor
        def _(pe):
            pe.wait_ge(const_step, 5)
            pe.wait_ge(ld_kv, 16 * 5)
            for k in range(KC):
                nc.tensor.transpose(bank[0][:, k * P:(k + 1) * P], ctx_sb[:, k * P:(k + 1) * P], ident[:, :])
            nc.tensor.transpose(bank[0][:, 256:256 + 3 * HP], bias_rows[:, :], ident[0:3 * HP, 0:3 * HP]).then_inc(ctxT_ps, 1)
            pe.wait_ge(ctxT_done, 2)

            def project(W_sb):
                for g in range(NG):
                    for c in range(g * GC, (g + 1) * GC):
                        for k in range(KC):
                            mm = nc.tensor.matmul(bank[4 + g][:, (c % GC) * P:(c % GC + 1) * P],
                                                  W_sb[:, k, c * P:(c + 1) * P], ctxT[:, k, :],
                                                  start=(k == 0), stop=(k == KC - 1))
                    mm.then_inc(kv_ps, 1)

            project(Wk_sb)
            pe.wait_ge(ld_q, 16)
            for j in range(HP // 2):
                for c in (2 * j, 2 * j + 1):
                    for k in range(KC):
                        mm = nc.tensor.transpose(bank[j][:, (c % 2) * D + k * P:(c % 2) * D + (k + 1) * P],
                                                 Wq_sb[:, k, c * P:(c + 1) * P], ident[:, :])
                mm.then_inc(wqT_ps, 1)
            pe.wait_ge(wqT_done, HP // 2)
            pe.wait_ge(kv_done, HP)
            for kc in range(KC):
                for g in range(NG):
                    for c in range(g * GC, (g + 1) * GC):
                        for p in range(2):
                            j = (kc * NG + g) * 2 + p
                            rows = slice(64 * p, 64 * p + 64)
                            mm = nc.tensor.matmul(fold_bank(bank, scores_ps, j)[:, (c % GC) * P:(c % GC + 1) * P],
                                                  WqT[rows, c, kc * P:(kc + 1) * P], kT[rows, c, :],
                                                  start=True, stop=True)
                            if c == (g + 1) * GC - 1:
                                mm.then_inc(A_ps, 1)
            for g in range(NG):
                pe.wait_ge(A_done, 2 * g + 2)
                for c in range(g * GC, (g + 1) * GC):
                    for p in range(2):
                        rows = slice(64 * p, 64 * p + 64)
                        mm = nc.tensor.matmul(fold_bank(bank, scores_ps, 2 * g + p)[0:64, (c % GC) * P:(c % GC + 1) * P],
                                              bias_cols[rows, c:c + 1].to_broadcast([64, 64]), kT[rows, c, :],
                                              start=True, stop=True)
                        if c == (g + 1) * GC - 1:
                            mm.then_inc(sbias_ps, 1)
            pe.wait_ge(A_done, 2 * KC * NG)
            pe.wait_ge(ld_vo, 32)
            project(Wv_sb)
            pe.wait_ge(kv_done, 2 * HP)
            pe.wait_ge(sbias_done, 2 * NG)
            for j in range(2 * HP):
                c, p = j // 2, j % 2
                rows = slice(64 * p, 64 * p + 64)
                if j >= 8:
                    pe.wait_ge(B_done, j - 7)
                for b in range(B):
                    mm = nc.tensor.matmul(fold_bank(bank, scores_ps, j)[rows, b * D:(b + 1) * D],
                                          vT[rows, c, b * KV:(b + 1) * KV], Wo_sb[rows, c, :],
                                          start=True, stop=True)
                mm.then_inc(B_ps, 1)
            pe.wait_ge(B_done, 2 * HP)
            pe.wait_ge(wsh_done, 2)
            pe.wait_ge(const_pick, 4)

            def split_product(out_ap, a_hi, a_lo, b_hi, b_lo, first, last):
                nc.tensor.matmul(out_ap, a_hi, b_hi, start=first, stop=False)
                nc.tensor.matmul(out_ap, a_hi, b_lo, start=False, stop=False)
                return nc.tensor.matmul(out_ap, a_lo, b_hi, start=False, stop=last)

            def step(t, q, i):
                u, v, w = t + 2, t - 2, t - 1
                if inside(u):
                    pe.wait_ge(xn_done, u + 1)
                    after(pe, xT_lo_done, u)
                    after(pe, x2T_lo_done, t - 1)
                    for k in range(KC):
                        mm = nc.tensor.transpose(xT_ps[:, k * P:(k + 1) * P], xn[q][:, k * P:(k + 1) * P], ident[:, :])
                    mm.then_inc(xT_done, 1)
                if inside(t):
                    pe.wait_ge(norm_done, t + 1)
                    for h in range(2):
                        after(pe, pT_lo_done, 2 * t - 1 + h)
                        for c in range(4):
                            mm = nc.tensor.transpose(pT_ps[h][:, c * P:(c + 1) * P],
                                                     prob[q][:, (4 * h + c) * P:(4 * h + c + 1) * P], ident[:, :])
                        mm.then_inc(pT_done, 1)
                if inside(v):
                    pe.wait_ge(x2T_lo_done, v + 1)
                    after(pe, hid_done, v)
                    after(pe, logit_done, v)
                    for k in range(KC):
                        mm = split_product(h_ps[:, 0:2 * F + E], xn2T_hi[q][:, k, :], xn2T_lo[q][:, k, :],
                                           Wsh_hi[:, k, :], Wsh_lo[:, k, :], k == 0, k == KC - 1)
                    mm.then_inc(h_done, 1)
                if inside(u):
                    pe.wait_ge(xT_lo_done, u + 1)
                    after(pe, sub_done, u)
                    b = u // TB
                    for half in range(2):
                        cols = slice(half * 512, half * 512 + 512)
                        acc = scores_ps[:, cols]
                        nc.tensor.matmul(acc, pick_rows[:, :], score_bias[:, bass.ds(b, 1), cols], start=True, stop=False)
                        for k in range(KC):
                            mm = split_product(acc, xnT_hi[q][:, k, :], xnT_lo[q][:, k, :],
                                               A_hi[:, bass.ds(b, 1), k, cols], A_lo[:, bass.ds(b, 1), k, cols],
                                               False, k == KC - 1)
                    mm.then_inc(scores_done, 1)
                if inside(v):
                    pe.wait_ge(hid_done, v + 1)
                    after(pe, yscale_done, v)
                    for k in range(2):
                        mm = nc.tensor.transpose(hy_ps[0:FH, k * P:(k + 1) * P], hid[:, k * FH:(k + 1) * FH], ident[:, :])
                    mm.then_inc(hT_done, 1)
                if inside(w):
                    pe.wait_ge(xn2_done, w + 1)
                    if isinstance(t, int):
                        pe.wait_ge(xT_lo_done, min(t + 3, T))
                    else:
                        pe.wait_ge(xT_lo_done, t + 3)
                    for k in range(KC):
                        mm = nc.tensor.transpose(xT_ps[:, k * P:(k + 1) * P], xn2[1 - q][:, k * P:(k + 1) * P], ident[:, :])
                    mm.then_inc(x2T_done, 1)
                if inside(t):
                    after(pe, x2_done, t)
                    b = t // TB
                    for c in range(HP):
                        if c % 4 == 0:
                            pe.wait_ge(pT_lo_done, 2 * t + c // 4 + 1)
                        mm = split_product(att_ps[:, 0:D], pT_hi[:, c, :], pT_lo[:, c, :],
                                           B_hi[:, bass.ds(b, 1), c, :], B_lo[:, bass.ds(b, 1), c, :],
                                           c == 0, c == HP - 1)
                    mm.then_inc(att_done, 1)
                if inside(v):
                    pe.wait_ge(hT_lo_done, v + 1)
                    for k in range(2):
                        mm = split_product(hy_ps[:, 0:D], hT_hi[:, k, :], hT_lo[:, k, :],
                                           Wds_hi[:, k, :], Wds_lo[:, k, :], k == 0, k == 1)
                    mm.then_inc(y_done, 1)

            token_loop(pe, step)

            pe.wait_ge(mask_done, 2)
            pe.wait_ge(hid_done, T)
            pe.wait_ge(yscale_done, T)
            flat = mask[:, :, :].rearrange("p t e -> p (t e)")
            flat_upto = upto[1][:, :, :].rearrange("p t e -> p (t e)")
            nc.tensor.matmul(count_ps, ones_r[:, :], flat_upto[:, (T - 1) * E:T * E], start=True, stop=True)
            nc.tensor.matmul(bank[4][:, 0:T * E], upper[:, :], flat, start=True, stop=False, skip_group_check=True)
            nc.tensor.matmul(bank[4][:, E:T * E], ones_r[:, :], flat_upto[:, 0:(T - 1) * E],
                             start=False, stop=True, skip_group_check=True).then_inc(rank_ps_done, 1)
            pe.wait_ge(x2T_lo_done, T)
            for g in range(GROUPS):
                pe.wait_ge(hot_place_done, g + 1)
                pe.wait_ge(hot_row_done, g + 1)
                for n in range(g * NPG, (g + 1) * NPG):
                    mm = nc.tensor.matmul(table_ps, onehot_p[:, n, :], onehot_q[:, n, :],
                                          start=(n == 0), stop=(n == TOPK * T - 1))
            mm.then_inc(table_ps_done, 1)
            pe.wait_ge(tile_row_done, 1)
            pe.wait_ge(w_lo_done, E)
            pe.wait_ge(wd_lo_done, 4)
            pe.wait_ge(src_done, 1)

            row_regs = [pe.alloc_register(f"row{r}") for r in range(2 * RING)]
            rows = []

            def expert_step(j, k, i):
                n, y, d = j + 1, j - 2, j - 1
                kn = (k + 1) % RING
                if k == 0 and (i is not None or j >= 0):
                    pe.load(row_regs, tile_row[0:1, bass.ds(j, 2 * RING)])
                    rows[:] = [pe.snap(r, min_val=0, max_val=KC * (E - 1)) for r in row_regs]
                if in_tiles(y):
                    y_row = rows[RING + k - 2]
                if in_tiles(j):
                    h_row = rows[RING + k]
                if in_tiles(n):
                    after(pe, gathered[kn], 16 * (ring_turn(j, k, i, 1) + 1))
                    after(pe, gT_lo_done, n - 1)
                    for c in range(KC):
                        mm = nc.tensor.transpose(gT_ps[(k + 1) % 2][:, c * P:(c + 1) * P], xg[kn][:, c * P:(c + 1) * P], ident[:, :])
                    mm.then_inc(gT_done, 1)
                if in_tiles(y):
                    pe.wait_ge(ehT_lo_done, y + 1)
                    after(pe, ycopy_done, y - 1)
                    for c in range(2):
                        mm = split_product(ey_ps[k % 2][:, 0:D], hT_hi[:, c, :], hT_lo[:, c, :],
                                           Wd_hi[:, bass.ds(y_row + c, 1), :], Wd_lo[:, bass.ds(y_row + c, 1), :],
                                           c == 0, c == 1)
                    mm.then_inc(ey_done, 1)
                if in_tiles(d):
                    pe.wait_ge(ehid_done, d + 1)
                    after(pe, ehT_lo_done, d - 1)
                    for c in range(2):
                        mm = nc.tensor.transpose(ehT_ps[(k + 1) % 2][0:FH, c * P:(c + 1) * P], hid[:, c * FH:(c + 1) * FH], ident[:, :])
                    mm.then_inc(ehT_done, 1)
                if in_tiles(j):
                    pe.wait_ge(gT_lo_done, j + 1)
                    after(pe, ehid_done, j - 1)
                    for c in range(KC):
                        mm = split_product(eh_ps[k % 2][:, 0:2 * F], xnT_hi[k % 2][:, c, :], xnT_lo[k % 2][:, c, :],
                                           W_hi[:, bass.ds(h_row + c, 1), :], W_lo[:, bass.ds(h_row + c, 1), :],
                                           c == 0, c == KC - 1)
                    mm.then_inc(eh_done, 1)

            expert_loop(pe, expert_step)


def fold_bank(bank, scores_ps, j):
    j = j % 8
    return bank[j][:, :] if j < 6 else scores_ps[:, (j - 6) * 512:(j - 5) * 512]


def A_out(A, kc, g, p):
    return A[:, :, kc, :].rearrange("q b (c p k) -> q b c p k", p=2, k=KV)[:, :, 4 * g:4 * g + 4, p, :]


def A_in(ps):
    return ps.rearrange("q (c b k) -> q b c k", c=4, b=B)


def S_out(R, g, p, row):
    rows = slice(row, 64)
    return R[rows, :, :].rearrange("q b (c p k) -> q b c p k", p=2, k=KV)[:, :, 4 * g:4 * g + 4, p, :]


def S_in(ps, row):
    return ps[row:64, :].rearrange("q (c b k) -> q b c k", c=4, b=B)


_INS = ['x', 'ctx_1024', 'g_xattn', 'g_ffn', 'L0_xattn_Wq', 'L0_xattn_bq', 'L0_xattn_Wk', 'L0_xattn_bk',
        'L0_xattn_Wv', 'L0_xattn_bv', 'L0_xattn_Wo', 'L0_xattn_bo', 'L0_ffn_W_gate_router', 'L0_ffn_expert_bias',
        'L0_ffn_Wg', 'L0_ffn_Wu', 'L0_ffn_Wd', 'L0_ffn_Wg_s', 'L0_ffn_Wu_s', 'L0_ffn_Wd_s']


def kernel(**inputs):
    import numpy as _np
    import concourse.bacc as _bacc
    from concourse import mybir as _mybir
    from concourse.bass_utils import run_bass_kernel_spmd as _run

    nc = _bacc.Bacc("TRN2", target_bir_lowering=False, num_devices=1)
    arrays, args = {}, []
    for name in _INS:
        a = _np.ascontiguousarray(inputs[name])
        arrays[f"in_{name}_dram"] = a
        args.append(nc.dram_tensor(f"in_{name}_dram", a.shape, _mybir.dt.from_np(a.dtype), kind="ExternalInput").ap())
    args.append(nc.dram_tensor("out_dram", (B, SEQ, D), F32, kind="ExternalOutput").ap())
    flamingo_layer(nc, *args)
    r = _run(nc, [arrays], core_ids=[0])
    return r.results[0]["out_dram"]
```

```python
from contextlib import ExitStack

import concourse.bass as bass
from concourse import mybir

F32 = mybir.dt.float32
F32R = mybir.dt.float32r
I32 = mybir.dt.int32
ALU = mybir.AluOpType
ACT = mybir.ActivationFunctionType
AX_X = mybir.AxisListType.X

P = 128
B, SEQ, D = 2, 1024, 256
KV = 64
H, DH = 16, 64
HP = H // 2
HK = H * KV
KC = D // P
E, F = 8, 192
FH = F // 2
TOKENS = B * SEQ
T = TOKENS // P
TB = SEQ // P
TOPK = 2
SLOT_TILES = (TOKENS * TOPK + E * (P - 1)) // P
Q = SLOT_TILES + 1
RING = 4
TURNS = 2
LN_EPS = 1e-5
ROUTE_EPS = 1e-20
FAR = 8192.0
BIG = 3.0e38


def flamingo_layer(nc, x, ctx_kv, g_xattn, g_ffn, Wq, bq, Wk, bk, Wv, bv, Wo, bo,
                   W_router, expert_bias, Wg, Wu, Wd, Wg_s, Wu_s, Wd_s, out):
    stack = ExitStack()
    with stack:
        def sb(name, shape, dt=F32):
            return stack.enter_context(nc.sbuf_tensor(name, shape, dt))

        def sem(name):
            return stack.enter_context(nc.semaphore(name))

        x_sb = sb("x_sb", [P, T, D])
        A_hi = sb("A_hi", [P, B, KC, HK], F32R)
        A_lo = sb("A_lo", [P, B, KC, HK], F32R)
        B_hi = sb("B_hi", [P, B, HP, D], F32R)
        B_lo = sb("B_lo", [P, B, HP, D], F32R)
        score_bias = sb("score_bias", [P, B, HK], F32R)
        pick_rows = sb("pick_rows", [P, P], F32R)
        Wsh_hi = sb("Wsh_hi", [P, KC, 2 * F + E], F32R)
        Wsh_lo = sb("Wsh_lo", [P, KC, 2 * F + E], F32R)
        Wds_hi = sb("Wds_hi", [FH, 2, D], F32R)
        Wds_lo = sb("Wds_lo", [FH, 2, D], F32R)

        ident = sb("ident", [P, P])
        bo_row = sb("bo_row", [P, D])
        gates = sb("gates", [P, 2])
        tgate = sb("tgate", [P, 2])
        half_tgf = sb("half_tgf", [P, 1])
        minus_half = sb("minus_half", [P, T])
        stats1 = sb("stats1", [P, T, 6])
        mv1 = sb("mv1", [P, T, 2])
        ve1 = sb("ve1", [P, T])
        rstd1 = sb("rstd1", [P, T])
        shift1 = sb("shift1", [P, T])
        xn = [sb(f"xn{q}", [P, D]) for q in range(2)]
        xnT_hi = [sb(f"xnT_hi{q}", [P, KC, P], F32R) for q in range(2)]
        xnT_lo = [sb(f"xnT_lo{q}", [P, KC, P], F32R) for q in range(2)]
        prob = [sb(f"prob{q}", [P, HK]) for q in range(2)]
        kT = [pr[:, :].rearrange("p (c h s) -> p c h s", h=2, s=P) for pr in prob]
        row_max = sb("row_max", [P, H])
        row_sum = sb("row_sum", [P, H])
        row_inv = sb("row_inv", [P, H])
        pT_hi = sb("pT_hi", [P, HP, P], F32R)
        pT_lo = sb("pT_lo", [P, HP, P], F32R)
        stats2 = sb("stats2", [P, 6])
        mv2 = sb("mv2", [P, 2])
        ve2 = sb("ve2", [P, 1])
        neg_mean2 = sb("neg_mean2", [P, 1])
        eps_col = sb("eps_col", [P, 1])
        minus_one = sb("minus_one", [P, 1])
        carrier = sb("carrier", [P, 1])
        silu_first = sb("silu_first", [P, 1])
        rstd2 = sb("rstd2", [P, 1])
        shift2 = sb("shift2", [P, 1])
        xn2 = [sb(f"xn2_{q}", [P, D]) for q in range(2)]
        xn2T_hi = [sb(f"xn2T_hi{q}", [P, KC, P], F32R) for q in range(2)]
        xn2T_lo = [sb(f"xn2T_lo{q}", [P, KC, P], F32R) for q in range(2)]
        tanh_g = sb("tanh_g", [P, F])
        gate_act = sb("gate_act", [P, F])
        hid = sb("hid", [P, F])
        hT_hi = sb("hT_hi", [FH, 2, P], F32R)
        hT_lo = sb("hT_lo", [FH, 2, P], F32R)
        iota_e = sb("iota_e", [P, E])
        iota_e8 = sb("iota_e8", [P, E])
        iota_q = sb("iota_q", [P, Q])
        iota_p = sb("iota_p", [P, P])
        pair_row = sb("pair_row", [P, TOPK * T])
        upper_f = sb("upper_f", [P, P])
        upper = sb("upper", [P, P], F32R)
        ones_r = sb("ones_r", [P, P], F32R)
        before = sb("before", [P, E, E])
        expert_b = sb("expert_b", [P, E])
        score = sb("score", [P, T, E])
        choice = sb("choice", [P, T, E])
        best = sb("best", [P, T])
        first_e = sb("first_e", [P, T])
        hot = sb("hot", [P, TOPK, T, E])
        upto = [pT_hi[:, k, 0:T * E].rearrange("p (t e) -> p t e", e=E) for k in range(2)]
        cand = prob[1][:, TOPK * T * E:(TOPK + 1) * T * E].rearrange("p (t e) -> p t e", e=E)
        hot_val = prob[1][:, 0:TOPK * T * E].rearrange("p (k t e) -> p k t e", k=TOPK, e=E)
        mask = sb("mask", [P, T, E], F32R)
        picked = sb("picked", [P, TOPK, T])
        weight = [sb(f"weight{k}", [P, T]) for k in range(TOPK)]
        den = sb("den", [P, T])
        count_i = sb("count_i", [P, E], I32)
        tiles_f = sb("tiles_f", [P, E])
        start_prod = sb("start_prod", [P, E, E])
        end_f = sb("end_f", [P, E])
        start_f = sb("start_f", [P, E])
        slot = sb("slot", [P, TOPK, T])
        slot_i = sb("slot_i", [P, TOPK * T], I32)
        slot_p = sb("slot_p", [P, TOPK * T])
        slot_q = sb("slot_q", [P, TOPK * T])
        place_i = sb("place_i", [P, TOPK * T], I32)
        tile_i = sb("tile_i", [P, TOPK * T], I32)
        table = sb("table", [P, Q])
        pad_far = sb("pad_far", [P, Q])
        src_i = sb("src_i", [P, Q], I32)
        dst_i = sb("dst_i", [P, Q], I32)
        tile_cmp = sb("tile_cmp", [1, Q, E])
        tile_e = sb("tile_e", [1, Q])
        tile_row = sb("tile_row", [1, RING + Q + RING], I32)
        gat_idx = [sb(f"gat_idx{k}", [P, 1], I32) for k in range(RING)]
        sct_idx = [sb(f"sct_idx{k}", [P, 1], I32) for k in range(RING)]
        xg = [sb(f"xg{k}", [P, D]) for k in range(RING)]
        y_sb = [sb(f"y_sb{k}", [P, D]) for k in range(RING)]
        exp_neg = sb("exp_neg", [P, T, E])

        fold = ExitStack()

        def fb(name, shape, dt=F32):
            return fold.enter_context(nc.sbuf_tensor(name, shape, dt))

        Wk_sb = fb("Wk_sb", [P, KC, H * DH])
        Wq_sb = fb("Wq_sb", [P, KC, H * DH])
        Wv_sb = fb("Wv_sb", [P, KC, H * DH])
        Wo_sb = fb("Wo_sb", [P, HP, D])
        WqT = fb("WqT", [P, HP, D])
        ctx_sb = fb("ctx_sb", [P, D])
        ctxT = fb("ctxT", [P, KC, P])
        bias_rows = fb("bias_rows", [3 * HP, P])
        bias_cols = fb("bias_cols", [P, 3 * HP])
        vT = fb("vT", [P, HP, B, P])
        raw_sh = fb("raw_sh", [P, KC, 2 * F + E])
        raw_ds = fb("raw_ds", [FH, 2, D])
        fold.close()
        W_hi = sb("W_hi", [P, E * KC, 2 * F], F32R)
        W_lo = sb("W_lo", [P, E * KC, 2 * F], F32R)
        raw_buf = [sb(f"raw_buf{q}", [P, 4 * D]) for q in range(2)]
        raw_w = [r[:, 0:KC * 2 * F].rearrange("p (k f) -> p k f", k=KC) for r in raw_buf]
        raw_d = [r[0:FH, :].rearrange("p (n d) -> p n d", d=D) for r in raw_buf]
        Wd_hi = A_hi[0:FH, :, :, :].rearrange("p b k (c d) -> p (b k c) d", d=D)
        Wd_lo = A_lo[0:FH, :, :, :].rearrange("p b k (c d) -> p (b k c) d", d=D)

        plane = [W[:, :, :].rearrange("p k f -> p (k f)")[:, 0:T * D].rearrange("p (t d) -> p t d", d=D).bitcast(F32)
                 for W in (W_hi, W_lo)]
        onehot_p = B_hi[:, :, :, :].rearrange("p b c d -> p (b c d)").rearrange("p (n s) -> p n s", s=P)
        onehot_q = B_lo[:, :, :, :].rearrange("p b c d -> p (b c d)")[:, 0:TOPK * T * Q].rearrange("p (n s) -> p n s", s=Q)
        bank = [stack.enter_context(nc.psum_tensor(f"bank{i}", [P, 512], F32)) for i in range(2, 8)]
        scores_ps = stack.enter_context(nc.psum_tensor("scores_ps", [P, HK], F32))
        pT_ps = bank[0:2]
        att_ps, xT_ps, h_ps, hy_ps = bank[2], bank[3], bank[4], bank[5]

        rank_flat = bank[0][:, 0:T * E]
        rank_ps = rank_flat.rearrange("p (t e) -> p t e", e=E)
        count_ps = bank[1][:, 0:E]
        table_ps = bank[3][:, 0:Q]
        gT_ps = [bank[3], bank[2]]
        eh_ps = [bank[4], scores_ps[:, 0:512]]
        ehT_ps = [bank[5], scores_ps[:, 512:1024]]
        ey_ps = [bank[0], bank[1]]

        xn2_dram = nc.dram_tensor("xn2_dram", [TOKENS, D], F32, kind="Internal").ap()
        routed_dram = nc.dram_tensor("routed_dram", [TOPK * TOKENS, D], F32, kind="Internal").ap()

        ld_ctx = sem("ld_ctx")
        ld_k = [sem(f"ld_k{g}") for g in range(2)]
        ld_q = [sem(f"ld_q{g}") for g in range(2)]
        ld_x = [sem("ld_x0"), sem("ld_x1")]
        ld_vo = sem("ld_vo")
        ld_misc = sem("ld_misc")
        zeroed = sem("zeroed")
        ld_sh = sem("ld_sh")
        ld_d = [sem("ld_d0"), sem("ld_d1")]
        pool_held = sem("pool_held")
        const_route = sem("const_route")
        route_step = sem("route_step")
        mask_done = sem("mask_done")
        rank_ps_done = sem("rank_ps_done")
        place_step = sem("place_step")
        hot_place_done = sem("hot_place_done")
        hot_tile_done = sem("hot_tile_done")
        hot_row_done = sem("hot_row_done")
        table_ps_done = sem("table_ps_done")
        src_done = sem("src_done")
        dst_done = sem("dst_done")
        tile_row_done = sem("tile_row_done")
        wd_hi_done = sem("wd_hi_done")
        wd_lo_done = sem("wd_lo_done")
        gat_idx_done = sem("gat_idx_done")
        gathered = [sem(f"gathered{k}") for k in range(RING)]
        scattered = [sem(f"scattered{k}") for k in range(RING)]
        gT_done = sem("gT_done")
        gT_hi_done = sem("gT_hi_done")
        gT_lo_done = sem("gT_lo_done")
        eh_done = sem("eh_done")
        esilu_done = sem("esilu_done")
        ehid_done = sem("ehid_done")
        ehT_done = sem("ehT_done")
        ehT_hi_done = sem("ehT_hi_done")
        ehT_lo_done = sem("ehT_lo_done")
        ey_done = sem("ey_done")
        ycopy_done = sem("ycopy_done")
        routed_loaded = [[sem(f"routed_loaded{k}_{c}") for c in range(T // 2)] for k in range(TOPK)]
        add_step = sem("add_step")
        const_step = sem("const_step")
        const_pick = sem("const_pick")
        gates_done = sem("gates_done")
        ctxT_ps = sem("ctxT_ps")
        ctxT_done = sem("ctxT_done")
        kv_ps = sem("kv_ps")
        kv_done = sem("kv_done")
        wqT_ps = sem("wqT_ps")
        wqT_done = sem("wqT_done")
        A_ps = sem("A_ps")
        A_hi_done = sem("A_hi_done")
        A_done = sem("A_done")
        sbias_ps = sem("sbias_ps")
        sbias_hi = sem("sbias_hi")
        sbias_done = sem("sbias_done")
        B_ps = sem("B_ps")
        B_hi_done = sem("B_hi_done")
        B_done = sem("B_done")
        wsh_hi_done = sem("wsh_hi_done")
        wsh_done = sem("wsh_done")
        stats1_done = sem("stats1_done")
        mv1_done = sem("mv1_done")
        ln1_step = sem("ln1_step")
        xn_done = sem("xn_done")
        xb_done = sem("xb_done")
        xT_done = sem("xT_done")
        xT_hi_done = sem("xT_hi_done")
        xT_lo_done = sem("xT_lo_done")
        scores_done = sem("scores_done")
        max_done = sem("max_done")
        sub_done = sem("sub_done")
        exp_done = sem("exp_done")
        sum_done = sem("sum_done")
        inv_done = sem("inv_done")
        norm_done = sem("norm_done")
        pT_done = sem("pT_done")
        pT_hi_done = sem("pT_hi_done")
        pT_lo_done = sem("pT_lo_done")
        att_done = sem("att_done")
        x2_done = sem("x2_done")
        stats2_done = sem("stats2_done")
        mv2_done = sem("mv2_done")
        ln2_step = sem("ln2_step")
        xn2_done = sem("xn2_done")
        xn2_stored = [sem("xn2_stored0"), sem("xn2_stored1")]
        x2T_done = sem("x2T_done")
        x2T_hi_done = sem("x2T_hi_done")
        x2T_lo_done = sem("x2T_lo_done")
        h_done = sem("h_done")
        logit_done = sem("logit_done")
        tanh_done = sem("tanh_done")
        gact_done = sem("gact_done")
        hid_done = sem("hid_done")
        hT_done = sem("hT_done")
        hT_hi_done = sem("hT_hi_done")
        hT_lo_done = sem("hT_lo_done")
        y_done = sem("y_done")
        yscale_done = sem("yscale_done")
        yadd_done = sem("yadd_done")
        raw_loaded = [sem("raw_loaded0"), sem("raw_loaded1")]
        w_hi_done = sem("w_hi_done")
        w_lo_done = sem("w_lo_done")
        out_stored = sem("out_stored")

        NG = 2
        GC = HP // NG
        FOLD_JOBS = HP // 2
        B_BANKS = [bank[i] for i in (0, 1, 2, 4, 5)]

        def token_loop(eng, step, between=lambda t: None):
            for t in range(-3, 4):
                between(t)
                step(t, t % 2, None)
            with eng.Fori(0, E // 2) as i:
                for k in range(2):
                    step(4 + 2 * i + k, k, i)
            for t in range(4 + E, T + 3):
                step(t, t % 2, None)

        def expert_loop(eng, step):
            turns = (SLOT_TILES - 5 - 2 * RING) // (TURNS * RING)
            for j in range(-4, 2 * RING):
                step(j, j % RING, None)
            with eng.Fori(0, turns) as i:
                for k in range(TURNS * RING):
                    step(RING * (TURNS * i + (2 + k // RING)) + k % RING, k % RING, TURNS * i + k // RING)
            for j in range(RING * (TURNS * turns + 2), SLOT_TILES + 2):
                step(j, j % RING, None)

        def fold_bank(j):
            return bank[j][:, :] if j < 6 else scores_ps[:, (j - 6) * 512:(j - 5) * 512]

        def fold_ps(j):
            return fold_bank(j).rearrange("q (m b k) -> q b m k", b=B, k=KV)

        def fold_cols(ap, j):
            return ap[:, :, 4 * KV * j:4 * KV * (j + 1)].rearrange("q b (m k) -> q b m k", k=KV)

        def in_tiles(j):
            return not isinstance(j, int) or 0 <= j < SLOT_TILES

        def ring_turn(j, k, i, ahead):
            return (j + ahead) // RING if i is None else i + (2 + (k + ahead) // RING)

        def inside(t):
            return not isinstance(t, int) or 0 <= t < T

        def after(eng, s, n):
            if not isinstance(n, int) or n > 0:
                eng.wait_ge(s, n)

        def store(sp, c):
            b, t = c // (TB // 2), 2 * c % TB
            sp.dma_start(out[b, t * P:(t + 2) * P, :].rearrange("(t p) d -> p t d", p=P),
                         x_sb[:, 2 * c:2 * c + 2, :]).then_inc(out_stored, 16)

        GROUPS = 8
        NPG = TOPK * T // GROUPS

        def group(g):
            return slice(g * NPG, (g + 1) * NPG)

        def load_plane(eng, k):
            eng.wait_ge(ey_done, SLOT_TILES)
            for r in range(RING):
                eng.wait_ge(scattered[r], 16 * len(range(r, SLOT_TILES, RING)))
            for c in range(T // 2):
                row = k * TOKENS + c * 2 * P
                eng.dma_start(plane[k][:, 2 * c:2 * c + 2, :],
                              routed_dram[row:row + 2 * P, :].rearrange("(t p) d -> p t d", p=P)).then_inc(routed_loaded[k][c], 16)

        block = stack.enter_context(nc.Block())

        @block.sync
        def _(sp):
            sp.dma_start(ctx_sb[:, :], ctx_kv.rearrange("b s d -> (b s) d")).then_inc(ld_ctx, 16)
            for j, b_in in enumerate((bq, bk, bv)):
                sp.dma_start(bias_rows[j * HP:(j + 1) * HP, :],
                             b_in.rearrange("(c p) f -> c (p f)", p=2)).then_inc(ld_ctx, 16)
            for W_sb, W, loaded in ((Wq_sb, Wq, ld_q), (Wk_sb, Wk, ld_k)):
                for g in range(NG):
                    sp.dma_start(W_sb[:, :, g * GC * P:(g + 1) * GC * P],
                                 W[:, g * H // NG:(g + 1) * H // NG, :].rearrange("(k p) h f -> p k (h f)", p=P)).then_inc(loaded[g], 16)
            sp.dma_start(gates[:, 0:1], g_xattn.partition_broadcast(P)).then_inc(ld_misc, 16)
            sp.dma_start(gates[:, 1:2], g_ffn.partition_broadcast(P)).then_inc(ld_misc, 16)
            sp.dma_start(bo_row[:, :], bo.partition_broadcast(P)).then_inc(ld_misc, 16)
            sp.dma_start(expert_b[:, :], expert_bias.partition_broadcast(P)).then_inc(ld_misc, 16)
            sp.dma_start(x_sb[:, 0:TB, :], x[0].rearrange("(t p) d -> p t d", p=P)).then_inc(ld_x[0], 16)
            sp.dma_start(Wv_sb[:, :, :], Wv.rearrange("(k p) h f -> p k (h f)", p=P)).then_inc(ld_vo, 16)
            sp.dma_start(Wo_sb[:, :, :], Wo.rearrange("(c p) f d -> (p f) c d", p=2)).then_inc(ld_vo, 16)
            sp.dma_start(raw_sh[:, :, 0:F], Wg_s.rearrange("(k p) f -> p k f", p=P)).then_inc(ld_sh, 16)
            sp.dma_start(raw_sh[:, :, F:2 * F], Wu_s.rearrange("(k p) f -> p k f", p=P)).then_inc(ld_sh, 16)
            sp.dma_start(raw_sh[:, :, 2 * F:], W_router.rearrange("(k p) e -> p k e", p=P)).then_inc(ld_sh, 16)
            sp.dma_start(raw_ds[:, :, :], Wd_s.rearrange("(k p) d -> p k d", p=FH)).then_inc(ld_sh, 16)
            sp.dma_start(x_sb[:, TB:T, :], x[1].rearrange("(t p) d -> p t d", p=P)).then_inc(ld_x[1], 16)

            sp.wait_ge(B_done, HP)
            sp.wait_ge(wsh_done, 2)

            def step(t, q, i):
                if i is not None:
                    e = 2 * i + q
                    sp.wait_ge(xb_done, t + 1)
                    for half, W in enumerate((Wg, Wu)):
                        sp.dma_start(raw_w[q][:, :, half * F:(half + 1) * F],
                                     W[bass.ds(e, 1), :, :].rearrange("o (k p) f -> p (o k) f", p=P)).then_inc(raw_loaded[q], 16)
                w = t - 1
                if inside(w):
                    sp.wait_ge(xn2_done, w + 1)
                    sp.dma_start(xn2_dram[bass.ds(w * P, P), :], xn2[1 - q][:, :]).then_inc(xn2_stored[1 - q], 16)
                if isinstance(t, int) and T - 4 <= t < T:
                    n = t - (T - 4)
                    if n < 2:
                        sp.wait_ge(w_lo_done, E)
                    else:
                        sp.wait_ge(wd_lo_done, n - 1)
                    sp.dma_start(raw_d[n % 2][:, :, :],
                                 Wd[2 * n:2 * n + 2].rearrange("e (k p) d -> p (e k) d", p=FH)).then_inc(ld_d[n % 2], 16)

            token_loop(sp, step)
            load_plane(sp, 0)
            for c in range(T // 2):
                sp.wait_ge(add_step, 4 * (c + 1))
                store(sp, c)
            sp.wait_ge(out_stored, 16 * (T // 2))

        @block.gpsimd
        def _(pool):
            nc.gpsimd.memset(ident[:, :], 0.0).then_inc(const_step, 1)
            nc.gpsimd.memset(minus_half[:, :], -0.5).then_inc(const_step, 1)
            nc.gpsimd.memset(eps_col[:, :], LN_EPS).then_inc(const_step, 1)
            nc.gpsimd.memset(minus_one[:, :], -1.0).then_inc(const_step, 1)
            nc.gpsimd.memset(pick_rows[:, :].bitcast(F32), 0.0).then_inc(const_pick, 1)
            pool.wait_ge(const_step, 4)
            nc.gpsimd.affine_select(out=ident[:, :], in_=ident[:, :], compare_op=ALU.not_equal, fill=1.0,
                                    base=0, pattern=[[-1, P]], channel_multiplier=1).then_inc(const_step, 1)
            for c in range(2):
                nc.gpsimd.memset(prob[c][:, :], 0.0).then_inc(zeroed, 1)
            pool.wait_ge(const_step, 5)
            pool.wait_ge(zeroed, 2)
            nc.gpsimd.memset(score_bias[64:P, :, :].bitcast(F32), 0.0).then_inc(const_pick, 1)
            pool.wait_ge(const_pick, 2)
            nc.gpsimd.memset(pick_rows[0:1, :].bitcast(F32), 1.0).then_inc(const_pick, 1)
            pool.wait_ge(const_pick, 3)
            nc.gpsimd.memset(pick_rows[32:33, :].bitcast(F32), 1.0).then_inc(const_pick, 1)

            pool.wait_ge(const_pick, 4)
            nc.gpsimd.memset(vT[:, :, :, :], 0.0).then_inc(zeroed, 1)
            nc.gpsimd.iota(iota_e[:, :], [[1, E]], base=0, channel_multiplier=0,
                           allow_small_or_imprecise_dtypes=True).then_inc(const_route, 1)
            nc.gpsimd.iota(iota_e8[:, :], [[1, E]], base=-E, channel_multiplier=0,
                           allow_small_or_imprecise_dtypes=True).then_inc(const_route, 1)
            nc.gpsimd.iota(iota_q[:, :], [[1, Q]], base=0, channel_multiplier=0,
                           allow_small_or_imprecise_dtypes=True).then_inc(const_route, 1)
            nc.gpsimd.iota(iota_p[:, :], [[1, P]], base=0, channel_multiplier=0,
                           allow_small_or_imprecise_dtypes=True).then_inc(const_route, 1)
            nc.gpsimd.iota(pair_row[:, :], [[TOKENS, TOPK], [P, T]], base=1, channel_multiplier=1,
                           allow_small_or_imprecise_dtypes=True).then_inc(const_route, 1)
            nc.gpsimd.iota(before[:, :, :], [[-1, E], [1, E]], base=0, channel_multiplier=0,
                           allow_small_or_imprecise_dtypes=True).then_inc(const_route, 1)
            nc.gpsimd.memset(tile_row[:, :], 0).then_inc(const_route, 1)
            nc.gpsimd.memset(ones_r[:, :].bitcast(F32), 1.0).then_inc(const_route, 1)
            nc.gpsimd.memset(upper_f[:, :], 1.0).then_inc(const_route, 1)
            pool.wait_ge(const_route, 9)
            nc.gpsimd.affine_select(out=upper_f[:, :], in_=upper_f[:, :], compare_op=ALU.is_gt, fill=0.0,
                                    base=0, pattern=[[1, P]], channel_multiplier=-1).then_inc(const_route, 1)

            def norm_factors(b):
                ts = slice(b * TB, (b + 1) * TB)
                pool.wait_ge(mv1_done, (b + 1) * TB)
                nc.gpsimd.tensor_scalar(ve1[:, ts], mv1[:, ts, 1], LN_EPS, None, ALU.add).then_inc(ln1_step, 1)
                pool.wait_ge(ln1_step, 4 * b + 1)
                nc.gpsimd.tensor_tensor(rstd1[:, ts], ve1[:, ts], minus_half[:, ts], ALU.pow).then_inc(ln1_step, 1)
                pool.wait_ge(ln1_step, 4 * b + 2)
                nc.gpsimd.tensor_tensor(shift1[:, ts], mv1[:, ts, 0], rstd1[:, ts], ALU.mult).then_inc(ln1_step, 1)
                pool.wait_ge(ln1_step, 4 * b + 3)
                nc.gpsimd.tensor_scalar(shift1[:, ts], shift1[:, ts], -1.0, None, ALU.mult).then_inc(ln1_step, 1)
                pool.wait_ge(ln1_step, 4 * b + 4)

            norm_factors(0)
            pool.wait_ge(ld_misc, 64)
            pool.wait_ge(gates_done, 3)

            def between(t):
                if t == -1:
                    norm_factors(1)

            def add_shared(z, qz):
                pool.wait_ge(yscale_done, z + 1)
                pool.wait_ge(xn2_done, z + 1)
                nc.gpsimd.tensor_tensor(x_sb[:, bass.ds(z, 1), :], y_sb[qz][:, :], x_sb[:, bass.ds(z, 1), :],
                                        ALU.add).then_inc(yadd_done, 1)

            def step(t, q, i):
                w, m, u, z = t - 1, t + 1, t + 2, t - 3
                if inside(u):
                    pool.wait_ge(xn_done, u + 1)
                    nc.gpsimd.tensor_tensor(x_sb[:, bass.ds(u, 1), :], x_sb[:, bass.ds(u, 1), :], bo_row[:, :],
                                            ALU.add).then_inc(xb_done, 1)
                if inside(w):
                    pool.wait_ge(mv2_done, w + 1)
                    after(pool, xn2_done, w)
                    nc.gpsimd.tensor_tensor(ve2[:, :], mv2[:, 1:2], eps_col[:, :], ALU.add).then_inc(ln2_step, 1)
                    nc.gpsimd.tensor_tensor(neg_mean2[:, :], mv2[:, 0:1], minus_one[:, :], ALU.mult).then_inc(ln2_step, 1)
                    pool.wait_ge(ln2_step, 4 * w + 1)
                    nc.gpsimd.tensor_tensor(rstd2[:, :], ve2[:, :], minus_half[:, 0:1], ALU.pow).then_inc(ln2_step, 1)
                    pool.wait_ge(ln2_step, 4 * w + 3)
                    nc.gpsimd.tensor_tensor(shift2[:, :], neg_mean2[:, :], rstd2[:, :], ALU.mult).then_inc(ln2_step, 1)
                if inside(m):
                    pool.wait_ge(inv_done, m + 1)
                    pr = prob[1 - q][:, :].rearrange("p (h k) -> p h k", k=KV)
                    nc.gpsimd.tensor_tensor(pr, pr, row_inv[:, :].unsqueeze(2).to_broadcast([P, H, KV]),
                                            ALU.mult).then_inc(norm_done, 1)
                if inside(z) and not (isinstance(t, int) and z == T - 1):
                    add_shared(z, 1 - q)
                if i is not None:
                    e = 2 * i + q
                    pool.wait_ge(w_hi_done, e + 1)
                    nc.gpsimd.tensor_tensor(W_lo[:, bass.ds(KC * e, KC), :], raw_w[q],
                                            W_hi[:, bass.ds(KC * e, KC), :].bitcast(F32), ALU.subtract).then_inc(w_lo_done, 1)
                if isinstance(t, int) and t in (T - 2, T):
                    for n in (0,) if t == T - 2 else (1, 2, 3):
                        part = slice(4 * n, 4 * n + 4)
                        pool.wait_ge(wd_hi_done, n + 1)
                        nc.gpsimd.tensor_tensor(Wd_lo[:, part, :], raw_d[n % 2][:, :, :],
                                                Wd_hi[:, part, :].bitcast(F32), ALU.subtract).then_inc(wd_lo_done, 1)

            token_loop(pool, step, between)

            def hold():
                pool.sem_inc(pool_held, 1)

            for g in range(GROUPS):
                pool.wait_ge(hot_tile_done, g + 1)
                nc.gpsimd.tensor_tensor(onehot_q[:, group(g), :], onehot_q[:, group(g), :].bitcast(F32),
                                        pair_row[:, group(g)].unsqueeze(2).to_broadcast([P, NPG, Q]),
                                        ALU.mult).then_inc(hot_row_done, 1)
            for q in range(2):
                pool.wait_ge(xn2_stored[q], 16 * (T // 2))

            def expert_step(j, k, i):
                if isinstance(j, int) and j == 0:
                    add_shared(T - 1, (T - 1) % 2)
                n, s = j + 4, j - 2
                kn, ks = (k + 4) % RING, (k - 2) % RING
                if in_tiles(n):
                    pool.wait_ge(gat_idx_done, n + 1)
                    hold()
                    nc.gpsimd.indirect_dma_start(xg[kn][:, :], None, xn2_dram[:, :],
                                                 bass.IndirectOffsetOnAxis(ap=gat_idx[kn][:, 0:1], axis=0)).then_inc(gathered[kn], 16)
                if in_tiles(s):
                    pool.wait_ge(ycopy_done, s + 1)
                    hold()
                    nc.gpsimd.indirect_dma_start(routed_dram[:, :], bass.IndirectOffsetOnAxis(ap=sct_idx[ks][:, 0:1], axis=0),
                                                 y_sb[ks][:, :], None, bounds_check=TOPK * TOKENS - 1,
                                                 oob_is_err=False).then_inc(scattered[ks], 16)

            expert_loop(pool, expert_step)

        @block.scalar
        def _(act):
            act.wait_ge(ld_misc, 64)
            nc.scalar.activation(tgate[:, :], gates[:, :], ACT.Tanh).then_inc(gates_done, 1)
            act.wait_ge(gates_done, 1)
            nc.scalar.activation(bo_row[:, :], bo_row[:, :], ACT.Copy, scale=tgate[:, 0:1]).then_inc(gates_done, 1)
            nc.scalar.activation(half_tgf[:, :], tgate[:, 1:2], ACT.Copy, scale=0.5).then_inc(gates_done, 1)
            for j in range(HP // 2):
                act.wait_ge(wqT_ps, j + 1)
                nc.scalar.activation(WqT[:, 2 * j:2 * j + 2, :], bank[j][:, :].rearrange("p (c d) -> p c d", c=2),
                                     ACT.Copy, scale=DH ** -0.5).then_inc(wqT_done, 1)
            for kc in range(KC):
                for j in range(FOLD_JOBS):
                    n = kc * FOLD_JOBS + j
                    act.wait_ge(A_ps, n + 1)
                    nc.scalar.activation(fold_cols(A_hi[:, :, kc, :], j), fold_ps(n), ACT.Copy).then_inc(A_hi_done, 1)
            for j in range(FOLD_JOBS):
                act.wait_ge(sbias_ps, j + 1)
                nc.scalar.activation(fold_cols(score_bias[0:64, :, :], j), fold_ps(j)[0:64], ACT.Copy).then_inc(sbias_hi, 1)
            act.wait_ge(ln1_step, 4)

            def B_high(pairs):
                for c in pairs:
                    act.wait_ge(B_ps, c + 1)
                    nc.scalar.activation(B_hi[:, :, c, :], B_BANKS[c % 5][:, :].rearrange("p (b d) -> p b d", b=B),
                                         ACT.Copy, scale=tgate[:, 0:1]).then_inc(B_hi_done, 1)

            def between(t):
                if t == -2:
                    act.wait_ge(ld_sh, 64)
                    nc.scalar.activation(Wsh_hi[:, :, :], raw_sh[:, :, :], ACT.Copy).then_inc(wsh_hi_done, 1)
                    nc.scalar.activation(Wds_hi[:, :, :], raw_ds[:, :, :], ACT.Copy).then_inc(wsh_hi_done, 1)
                if t == 3:
                    act.wait_ge(const_route, 10)
                    nc.scalar.activation(upper[:, :], upper_f[:, :], ACT.Copy).then_inc(mask_done, 1)
                    act.wait_ge(ln1_step, 8)

            def down_high(n):
                part = slice(4 * n, 4 * n + 4)
                act.wait_ge(ld_d[n % 2], 16 * (n // 2 + 1))
                act.wait_ge(scores_done, T)
                nc.scalar.activation(Wd_hi[:, part, :], raw_d[n % 2][:, :, :], ACT.Copy).then_inc(wd_hi_done, 1)

            def step(t, q, i):
                u, v, m, w, n, z = t + 2, t - 2, t + 1, t - 1, t + 3, t - 3
                folding = isinstance(t, int) and t == -1
                scores_first = isinstance(t, int) and t < 2

                def exponentials():
                    act.wait_ge(sub_done, m + 1)
                    nc.scalar.activation(prob[1 - q][:, :], prob[1 - q][:, :], ACT.Exp).then_inc(exp_done, 1)

                if inside(m) and not scores_first:
                    exponentials()
                if inside(u):
                    act.wait_ge(xT_done, u + 1)
                    after(act, scores_done, u - 1)
                    nc.scalar.activation(xnT_hi[q][:, :, :], xT_ps[:, 0:D].rearrange("p (k s) -> p k s", k=KC),
                                         ACT.Copy).then_inc(xT_hi_done, 1)
                if folding:
                    B_high(range(0, HP // 2))
                    exponentials()
                    B_high(range(HP // 2, HP))
                elif inside(m) and scores_first:
                    exponentials()
                if inside(t):
                    for h in range(2):
                        act.wait_ge(pT_done, 2 * t + h + 1)
                        if h == 0:
                            after(act, att_done, t)
                        nc.scalar.activation(pT_hi[:, 4 * h:4 * h + 4, :],
                                             pT_ps[h][:, :].rearrange("p (c s) -> p c s", c=4),
                                             ACT.Copy).then_inc(pT_hi_done, 1)
                if inside(n):
                    after(act, xT_done, n - 1)
                    nc.scalar.activation(xn[1 - q][:, :], x_sb[:, bass.ds(n, 1), :], ACT.Identity,
                                         scale=rstd1[:, bass.ds(n, 1)], bias=shift1[:, bass.ds(n, 1)]).then_inc(xn_done, 1)
                def scale_shared():
                    if inside(z):
                        act.wait_ge(y_done, z + 1)
                        after(act, yadd_done, z - 1)
                        nc.scalar.activation(y_sb[1 - q][:, :], hy_ps[:, 0:D], ACT.Copy,
                                             scale=half_tgf[:, 0:1]).then_inc(yscale_done, 1)

                def gates_of_shared():
                    if inside(v):
                        act.wait_ge(h_done, v + 1)
                        nc.scalar.activation(exp_neg[:, bass.ds(v, 1), :], h_ps[:, 2 * F:2 * F + E], ACT.Exp,
                                             scale=-1.0).then_inc(logit_done, 1)
                        after(act, gact_done, v)
                        nc.scalar.activation(tanh_g[:, :], h_ps[:, 0:F], ACT.Tanh, scale=0.5).then_inc(tanh_done, 1)

                def second_norm():
                    if inside(w):
                        after(act, x2T_done, w - 1)
                        if isinstance(w, int):
                            after(act, xn2_stored[1 - q], 16 * (w // 2))
                        else:
                            act.wait_ge(xn2_stored[1 - q], 8 * (w - (1 - q)))
                        act.wait_ge(ln2_step, 4 * w + 4)
                        nc.scalar.activation(xn2[1 - q][:, :], x_sb[:, bass.ds(w, 1), :], ACT.Identity,
                                             scale=rstd2[:, 0:1], bias=shift2[:, 0:1]).then_inc(xn2_done, 1)

                def high_hidden():
                    if inside(v):
                        act.wait_ge(hT_done, v + 1)
                        after(act, y_done, v)
                        nc.scalar.activation(hT_hi[:, :, :], hy_ps[0:FH, 0:2 * P].rearrange("p (k s) -> p k s", k=2),
                                             ACT.Copy).then_inc(hT_hi_done, 1)

                def high_xn2():
                    if inside(w):
                        act.wait_ge(x2T_done, w + 1)
                        after(act, h_done, w - 1)
                        nc.scalar.activation(xn2T_hi[1 - q][:, :, :], xT_ps[:, 0:D].rearrange("p (k s) -> p k s", k=KC),
                                             ACT.Copy).then_inc(x2T_hi_done, 1)

                if isinstance(t, int) and t >= T:
                    if t == T:
                        scale_shared()
                        second_norm()
                        gates_of_shared()
                        high_xn2()
                        high_hidden()
                    if t == T + 1:
                        gates_of_shared()
                        scale_shared()
                        down_high(2)
                        down_high(3)
                        high_hidden()
                    if t == T + 2:
                        scale_shared()
                    return
                scale_shared()
                gates_of_shared()
                second_norm()
                high_hidden()
                high_xn2()
                if i is not None:
                    act.wait_ge(raw_loaded[q], 32 * (i + 1))
                    nc.scalar.activation(W_hi[:, bass.ds(KC * (2 * i + q), KC), :], raw_w[q], ACT.Copy).then_inc(w_hi_done, 1)
                if isinstance(t, int) and t >= T - 2:
                    down_high(t - (T - 2))

            token_loop(act, step, between)

            def expert_step(j, k, i):
                n, d = j + 1, j - 1
                if in_tiles(n):
                    act.wait_ge(gT_done, n + 1)
                    after(act, eh_done, n - 1)
                    nc.scalar.activation(xnT_hi[(k + 1) % 2][:, :, :], gT_ps[(k + 1) % 2][:, 0:D].rearrange("p (k s) -> p k s", k=KC),
                                         ACT.Copy).then_inc(gT_hi_done, 1)
                if in_tiles(j):
                    act.wait_ge(eh_done, j + 1)
                    after(act, ehid_done, j)
                    nc.scalar.activation(gate_act[:, :], eh_ps[k % 2][:, 0:F], ACT.Silu).then_inc(esilu_done, 1)
                if in_tiles(d):
                    act.wait_ge(ehT_done, d + 1)
                    after(act, ey_done, d)
                    nc.scalar.activation(hT_hi[:, :, :], ehT_ps[(k + 1) % 2][0:FH, 0:2 * P].rearrange("p (k s) -> p k s", k=2),
                                         ACT.Copy).then_inc(ehT_hi_done, 1)

            nc.scalar.activation(silu_first[:, :], half_tgf[:, :], ACT.Silu)
            expert_loop(act, expert_step)
            load_plane(act, 1)

        @block.vector
        def _(dve):
            dve.wait_ge(ctxT_ps, 1)
            nc.vector.tensor_copy(ctxT[:, :, :], bank[0][:, 0:KC * P].rearrange("p (k s) -> p k s", k=KC)).then_inc(ctxT_done, 1)
            nc.vector.tensor_scalar(bias_cols[:, 0:HP], bank[0][:, 256:256 + HP], DH ** -0.5, None, ALU.mult).then_inc(ctxT_done, 1)
            nc.vector.tensor_copy(bias_cols[:, HP:3 * HP], bank[0][:, 256 + HP:256 + 3 * HP]).then_inc(ctxT_done, 1)
            dve.wait_ge(ctxT_done, 3)
            dve.wait_ge(zeroed, 2)
            for g in range(NG):
                dve.wait_ge(kv_ps, g + 1)
                for p in range(2):
                    rows = slice(64 * p, 64 * p + 64)
                    nc.vector.tensor_tensor(kT[g][rows, :, p, :], bank[4 + g][rows, :].rearrange("q (c s) -> q c s", c=GC),
                                            bias_cols[rows, HP + g * GC:HP + (g + 1) * GC].unsqueeze(2).to_broadcast([64, GC, P]),
                                            ALU.add).then_inc(kv_done, 1)

            def norm_stats(b):
                dve.wait_ge(ld_x[b], 16)
                for t in range(b * TB, (b + 1) * TB):
                    nc.vector.bn_stats(stats1[:, t, :], x_sb[:, t, :]).then_inc(stats1_done, 1)
                for t in range(b * TB, (b + 1) * TB):
                    dve.wait_ge(stats1_done, t + 1)
                    nc.vector.bn_aggr(mv1[:, t, :], stats1[:, t, :]).then_inc(mv1_done, 1)

            norm_stats(0)
            for kc in range(KC):
                for j in range(FOLD_JOBS):
                    n = kc * FOLD_JOBS + j
                    dve.wait_ge(A_hi_done, n + 1)
                    nc.vector.tensor_tensor(fold_cols(A_lo[:, :, kc, :], j), fold_ps(n),
                                            fold_cols(A_hi[:, :, kc, :], j).bitcast(F32), ALU.subtract).then_inc(A_done, 1)
            for j in range(FOLD_JOBS):
                dve.wait_ge(sbias_hi, j + 1)
                nc.vector.tensor_tensor(fold_cols(score_bias[32:64, :, :], j), fold_ps(j)[32:64],
                                        fold_cols(score_bias[32:64, :, :], j).bitcast(F32), ALU.subtract).then_inc(sbias_done, 1)
            norm_stats(1)

            def finish_v():
                dve.wait_ge(zeroed, 3)
                for g in range(NG):
                    dve.wait_ge(kv_ps, NG + g + 1)
                    pairs = slice(g * GC, (g + 1) * GC)
                    for p in range(2):
                        rows = slice(64 * p, 64 * p + 64)
                        nc.vector.tensor_tensor(vT[rows, pairs, :, 64 * p:64 * p + 64],
                                                bank[4 + g][rows, :].rearrange("q (c b k) -> q c b k", b=B, k=KV),
                                                bias_cols[rows, 2 * HP + g * GC:2 * HP + (g + 1) * GC].unsqueeze(2).unsqueeze(3)
                                                .to_broadcast([64, GC, B, KV]), ALU.add).then_inc(kv_done, 1)

            def B_low(pairs):
                for c in pairs:
                    dve.wait_ge(B_hi_done, c + 1)
                    nc.vector.scalar_tensor_tensor(out=B_lo[:, :, c, :],
                                                   in0=B_BANKS[c % 5][:, :].rearrange("p (b d) -> p b d", b=B),
                                                   scalar=tgate[:, 0:1], in1=B_hi[:, :, c, :].bitcast(F32),
                                                   op0=ALU.mult, op1=ALU.subtract).then_inc(B_done, 1)

            def shared_low():
                dve.wait_ge(wsh_hi_done, 1)
                nc.vector.tensor_tensor(Wsh_lo[:, :, :], raw_sh[:, :, :], Wsh_hi[:, :, :].bitcast(F32),
                                        ALU.subtract).then_inc(wsh_done, 1)
                dve.wait_ge(wsh_hi_done, 2)
                nc.vector.tensor_tensor(Wds_lo[:, :, :], raw_ds[:, :, :], Wds_hi[:, :, :].bitcast(F32),
                                        ALU.subtract).then_inc(wsh_done, 1)

            dve.wait_ge(gates_done, 3)
            dve.wait_ge(const_step, 5)

            steps = [0]

            def chain(ins):
                steps[0] += 1
                ins.then_inc(route_step, 1)
                dve.wait_ge(route_step, steps[0])

            def scores_and_choice(a, b):
                part = score[:, a:b, :]
                chain(nc.vector.tensor_scalar(part, exp_neg[:, a:b, :], 1.0, None, ALU.add))
                chain(nc.vector.reciprocal(part, part))
                chain(nc.vector.tensor_tensor(choice[:, a:b, :], part,
                                              expert_b[:, :].unsqueeze(1).to_broadcast([P, b - a, E]), ALU.add))

            def shared_hidden(v):
                dve.wait_ge(tanh_done, v + 1)
                after(dve, hid_done, v)
                nc.vector.scalar_tensor_tensor(out=gate_act[:, :], in0=tanh_g[:, :], scalar=1.0, in1=h_ps[:, 0:F],
                                               op0=ALU.add, op1=ALU.mult).then_inc(gact_done, 1)
                dve.wait_ge(gact_done, v + 1)
                after(dve, hT_done, v)
                nc.vector.tensor_tensor(hid[:, :], gate_act[:, :], h_ps[:, F:2 * F], ALU.mult).then_inc(hid_done, 1)

            def shared_hidden_low(v):
                dve.wait_ge(hT_hi_done, v + 1)
                nc.vector.tensor_tensor(hT_lo[:, :, :], hy_ps[0:FH, 0:2 * P].rearrange("p (k s) -> p k s", k=2),
                                        hT_hi[:, :, :].bitcast(F32), ALU.subtract).then_inc(hT_lo_done, 1)

            def step(t, q, i):
                u, v, m, w = t + 2, t - 2, t + 1, t - 1
                sc = scores_ps[:, :].rearrange("p (h k) -> p h k", k=KV)

                def pT_low(h):
                    dve.wait_ge(pT_hi_done, 2 * t + h + 1)
                    nc.vector.tensor_tensor(pT_lo[:, 4 * h:4 * h + 4, :], pT_ps[h][:, :].rearrange("p (c s) -> p c s", c=4),
                                            pT_hi[:, 4 * h:4 * h + 4, :].bitcast(F32), ALU.subtract).then_inc(pT_lo_done, 1)

                if inside(u):
                    dve.wait_ge(xT_hi_done, u + 1)
                    nc.vector.tensor_tensor(xnT_lo[q][:, :, :], xT_ps[:, 0:D].rearrange("p (k s) -> p k s", k=KC),
                                            xnT_hi[q][:, :, :].bitcast(F32), ALU.subtract).then_inc(xT_lo_done, 1)
                if isinstance(t, int) and t == -2:
                    finish_v()
                if isinstance(t, int) and t == -1:
                    B_low(range(0, HP // 2))
                if isinstance(t, int) and t == 0:
                    shared_low()

                def low_probabilities():
                    if inside(t):
                        pT_low(0)
                        pT_low(1)

                def sums():
                    if inside(m):
                        dve.wait_ge(exp_done, m + 1)
                        after(dve, inv_done, m)
                        nc.vector.tensor_reduce(row_sum[:, :], prob[1 - q][:, :].rearrange("p (h k) -> p h k", k=KV),
                                                AX_X, ALU.add).then_inc(sum_done, 1)
                        dve.wait_ge(sum_done, m + 1)
                        after(dve, norm_done, m)
                        nc.vector.reciprocal(row_inv[:, :], row_sum[:, :]).then_inc(inv_done, 1)

                def hidden():
                    if inside(v):
                        shared_hidden(v)

                def low_hidden():
                    if inside(v):
                        shared_hidden_low(v)

                def low_xn2():
                    if inside(w):
                        dve.wait_ge(x2T_hi_done, w + 1)
                        nc.vector.tensor_tensor(xn2T_lo[1 - q][:, :, :], xT_ps[:, 0:D].rearrange("p (k s) -> p k s", k=KC),
                                                xn2T_hi[1 - q][:, :, :].bitcast(F32), ALU.subtract).then_inc(x2T_lo_done, 1)

                def second_norm():
                    if inside(t):
                        dve.wait_ge(att_done, t + 1)
                        dve.wait_ge(xb_done, t + 1)
                        nc.vector.tensor_tensor(x_sb[:, bass.ds(t, 1), :], att_ps[:, 0:D], x_sb[:, bass.ds(t, 1), :],
                                                ALU.add).then_inc(x2_done, 1)
                        dve.wait_ge(x2_done, t + 1)
                        after(dve, mv2_done, t)
                        carry_waits()
                        nc.vector.bn_stats(stats2[:, :], x_sb[:, bass.ds(t, 1), :]).then_inc(stats2_done, 1)
                        dve.wait_ge(stats2_done, t + 1)
                        after(dve, ln2_step, 4 * t)
                        carry_waits()
                        nc.vector.bn_aggr(mv2[:, :], stats2[:, :]).then_inc(mv2_done, 1)

                if isinstance(t, int) and t >= T - 2:
                    sums()
                    low_probabilities()
                    if t < T - 1:
                        hidden()
                        low_hidden()
                        low_xn2()
                        second_norm()
                    elif t == T - 1:
                        hidden()
                        dve.wait_ge(const_route, 10)
                        dve.wait_ge(ld_misc, 64)
                        dve.wait_ge(logit_done, T - 2)
                        scores_and_choice(0, T - 2)
                        second_norm()
                        low_hidden()
                        low_xn2()
                    elif t == T:
                        hidden()
                        low_xn2()
                        low_hidden()
                    return
                low_probabilities()
                sums()
                if isinstance(t, int) and t == -1:
                    B_low(range(HP // 2, HP))
                hidden()
                if inside(u):
                    dve.wait_ge(scores_done, u + 1)
                    after(dve, sub_done, u)
                    nc.vector.tensor_reduce(row_max[:, :], sc, AX_X, ALU.max).then_inc(max_done, 1)
                low_hidden()
                low_xn2()
                if inside(u):
                    dve.wait_ge(max_done, u + 1)
                    after(dve, pT_done, 2 * t + 2)
                    nc.vector.tensor_tensor(prob[q][:, :].rearrange("p (h k) -> p h k", k=KV), sc,
                                            row_max[:, :].unsqueeze(2).to_broadcast([P, H, KV]),
                                            ALU.subtract).then_inc(sub_done, 1)
                second_norm()

            def carry_waits():
                nc.vector.tensor_copy(carrier[:, :], ident[:, 0:1])

            token_loop(dve, step)

            def over_t(ap):
                return ap.unsqueeze(1).to_broadcast([P, T, E])

            def over_e(ap):
                return ap.unsqueeze(2).to_broadcast([P, T, E])

            dve.wait_ge(logit_done, T)
            scores_and_choice(T - 2, T)
            nc.vector.tensor_scalar(before[:, :, :], before[:, :, :], 0.0, float(P), ALU.is_lt, ALU.mult)
            for k in range(TOPK):
                chain(nc.vector.tensor_reduce(best[:, :], choice[:, :, :], AX_X, ALU.max))
                chain(nc.vector.tensor_tensor(cand[:, :, :], choice[:, :, :], over_e(best[:, :]), ALU.is_equal))
                chain(nc.vector.scalar_tensor_tensor(out=cand[:, :, :], in0=cand[:, :, :], scalar=-float(E),
                                                     in1=over_t(iota_e[:, :]), op0=ALU.mult, op1=ALU.add))
                chain(nc.vector.tensor_reduce(first_e[:, :], cand[:, :, :], AX_X, ALU.min))
                chain(nc.vector.tensor_tensor(hot[:, k, :, :], over_t(iota_e8[:, :]), over_e(first_e[:, :]), ALU.is_equal))
                if k == 0:
                    chain(nc.vector.scalar_tensor_tensor(out=choice[:, :, :], in0=hot[:, 0, :, :], scalar=-BIG,
                                                         in1=choice[:, :, :], op0=ALU.mult, op1=ALU.add))
            chain(nc.vector.tensor_tensor(mask[:, :, :], hot[:, 0, :, :], hot[:, 1, :, :], ALU.add))
            src, reach, turn = mask, 1, 0
            while reach < T:
                dst = upto[turn % 2]
                nc.vector.tensor_copy(dst[:, 0:reach, :], src[:, 0:reach, :].bitcast(F32))
                chain(nc.vector.tensor_tensor(dst[:, reach:T, :], src[:, reach:T, :].bitcast(F32),
                                              src[:, 0:T - reach, :].bitcast(F32), ALU.add))
                src, reach, turn = dst, 2 * reach, turn + 1
            assert src is upto[1]
            nc.vector.tensor_copy(carrier[:, :], ident[:, 0:1]).then_inc(mask_done, 1)
            shared_hidden(T - 1)

            def of_both_choices(ap):
                chain(nc.vector.tensor_tensor(hot_val[:, :, :, :], hot[:, :, :, :],
                                              ap.unsqueeze(1).to_broadcast([P, TOPK, T, E]), ALU.mult))

            dve.wait_ge(rank_ps_done, 1)
            chain(nc.vector.tensor_scalar(count_i[:, :], count_ps, float(P - 1), None, ALU.add))
            chain(nc.vector.tensor_scalar(count_i[:, :], count_i[:, :], P.bit_length() - 1, None, ALU.logical_shift_right))
            chain(nc.vector.tensor_copy(tiles_f[:, :], count_i[:, :]))
            chain(nc.vector.tensor_tensor(start_prod[:, :, :], before[:, :, :],
                                          tiles_f[:, :].unsqueeze(1).to_broadcast([P, E, E]), ALU.mult))
            chain(nc.vector.tensor_reduce(start_f[:, :], start_prod[:, :, :], AX_X, ALU.add))
            chain(nc.vector.tensor_tensor(choice[:, :, :], rank_ps, over_t(start_f[:, :]), ALU.add))
            of_both_choices(choice[:, :, :])
            chain(nc.vector.tensor_reduce(slot[:, :, :], hot_val[:, :, :, :], AX_X, ALU.add))
            chain(nc.vector.tensor_copy(slot_i[:, :], slot[:, :, :].rearrange("p k t -> p (k t)")))
            nc.vector.tensor_scalar(tile_i[:, :], slot_i[:, :], P.bit_length() - 1, None, ALU.logical_shift_right).then_inc(place_step, 1)
            nc.vector.tensor_scalar(place_i[:, :], slot_i[:, :], P - 1, None, ALU.bitwise_and).then_inc(place_step, 1)
            dve.wait_ge(place_step, 1)
            chain(nc.vector.tensor_copy(slot_q[:, :], tile_i[:, :]))
            dve.wait_ge(place_step, 2)
            chain(nc.vector.tensor_copy(slot_p[:, :], place_i[:, :]))
            dve.wait_ge(att_done, T)

            for g in range(GROUPS):
                part = group(g)
                nc.vector.tensor_tensor(onehot_q[:, part, :], iota_q[:, :].unsqueeze(1).to_broadcast([P, NPG, Q]),
                                        slot_q[:, part].unsqueeze(2).to_broadcast([P, NPG, Q]),
                                        ALU.is_equal).then_inc(hot_tile_done, 1)
                nc.vector.tensor_tensor(onehot_p[:, part, :], iota_p[:, :].unsqueeze(1).to_broadcast([P, NPG, P]),
                                        slot_p[:, part].unsqueeze(2).to_broadcast([P, NPG, P]),
                                        ALU.is_equal).then_inc(hot_place_done, 1)
            shared_hidden_low(T - 1)
            chain(nc.vector.scalar_tensor_tensor(out=end_f[:, :], in0=start_f[:, :], scalar=1.0 / P, in1=tiles_f[:, :],
                                                 op0=ALU.mult, op1=ALU.add))
            chain(nc.vector.tensor_tensor(tile_cmp[:, :, :], iota_q[0:1, :].unsqueeze(2).to_broadcast([1, Q, E]),
                                          end_f[0:1, :].unsqueeze(1).to_broadcast([1, Q, E]), ALU.is_ge))
            chain(nc.vector.tensor_reduce(tile_e[:, :], tile_cmp[:, :, :], AX_X, ALU.add))
            nc.vector.tensor_scalar(tile_row[:, RING:RING + Q], tile_e[:, :], float(E - 1), float(KC), ALU.min,
                                    ALU.mult).then_inc(tile_row_done, 1)
            dve.wait_ge(table_ps_done, 1)
            chain(nc.vector.tensor_copy(table[:, :], table_ps))
            chain(nc.vector.tensor_scalar(src_i[:, :], table[:, :], -1.0, 0.0, ALU.add, ALU.max))
            nc.vector.tensor_scalar(src_i[:, :], src_i[:, :], TOKENS - 1, None, ALU.bitwise_and).then_inc(src_done, 1)
            dve.wait_ge(src_done, 1)
            for r in range(RING):
                nc.vector.tensor_copy(gat_idx[r][:, :], src_i[:, r:r + 1]).then_inc(gat_idx_done, 1)
            chain(nc.vector.tensor_scalar(pad_far[:, :], table[:, :], 0.0, FAR, ALU.is_equal, ALU.mult))
            nc.vector.scalar_tensor_tensor(out=dst_i[:, :], in0=table[:, :], scalar=-1.0, in1=pad_far[:, :],
                                           op0=ALU.add, op1=ALU.add).then_inc(dst_done, 1)
            dve.wait_ge(dst_done, 1)
            def weigh():
                of_both_choices(score[:, :, :])
                chain(nc.vector.tensor_reduce(picked[:, :, :], hot_val[:, :, :, :], AX_X, ALU.add))
                chain(nc.vector.tensor_tensor(den[:, :], picked[:, 0, :], picked[:, 1, :], ALU.add))
                chain(nc.vector.tensor_scalar(den[:, :], den[:, :], ROUTE_EPS, None, ALU.add))
                chain(nc.vector.reciprocal(den[:, :], den[:, :]))
                chain(nc.vector.tensor_scalar(den[:, :], den[:, :], tgate[:, 1:2], None, ALU.mult))
                for k in range(TOPK):
                    nc.vector.tensor_tensor(weight[k][:, :], picked[:, k, :], den[:, :], ALU.mult)

            def expert_step(j, k, i):
                n, d, g, c = j + 1, j - 1, j + 5, j - 2
                kc, kd, kg, kx = (k - 2) % RING, (k - 1) % RING, (k + 5) % RING, (k + 1) % 2
                if isinstance(j, int) and j == -RING:
                    weigh()
                if isinstance(j, int) and j == 2:
                    dve.wait_ge(yadd_done, T)
                if in_tiles(n):
                    dve.wait_ge(gT_hi_done, n + 1)
                    nc.vector.tensor_tensor(xnT_lo[kx][:, :, :], gT_ps[kx][:, 0:D].rearrange("p (k s) -> p k s", k=KC),
                                            xnT_hi[kx][:, :, :].bitcast(F32), ALU.subtract).then_inc(gT_lo_done, 1)
                if in_tiles(j):
                    dve.wait_ge(esilu_done, j + 1)
                    after(dve, ehT_done, j)
                    nc.vector.tensor_tensor(hid[:, :], gate_act[:, :], eh_ps[k % 2][:, F:2 * F], ALU.mult).then_inc(ehid_done, 1)
                if in_tiles(g) and not (isinstance(j, int) and g < RING):
                    after(dve, gathered[kg], 16 * ring_turn(j, k, i, 5))
                    nc.vector.tensor_copy(gat_idx[kg][:, :], src_i[:, bass.ds(g, 1)]).then_inc(gat_idx_done, 1)
                if in_tiles(d):
                    after(dve, scattered[kd], 16 * ring_turn(j, k, i, -1))
                    nc.vector.tensor_copy(sct_idx[kd][:, :], dst_i[:, bass.ds(d, 1)])
                if in_tiles(c):
                    dve.wait_ge(ey_done, c + 1)
                    nc.vector.tensor_copy(y_sb[kc][:, :], ey_ps[k % 2][:, 0:D]).then_inc(ycopy_done, 1)
                if in_tiles(d):
                    dve.wait_ge(ehT_hi_done, d + 1)
                    nc.vector.tensor_tensor(hT_lo[:, :, :], ehT_ps[kx][0:FH, 0:2 * P].rearrange("p (k s) -> p k s", k=2),
                                            hT_hi[:, :, :].bitcast(F32), ALU.subtract).then_inc(ehT_lo_done, 1)

            expert_loop(dve, expert_step)

            for c in range(T // 2):
                for k in range(TOPK):
                    dve.wait_ge(routed_loaded[k][c], 16)
                    for h in range(2):
                        t = 2 * c + h
                        if k:
                            dve.wait_ge(add_step, 4 * c + h + 1)
                        nc.vector.scalar_tensor_tensor(out=x_sb[:, t, :], in0=plane[k][:, t, :],
                                                       scalar=weight[k][:, t:t + 1], in1=x_sb[:, t, :],
                                                       op0=ALU.mult, op1=ALU.add).then_inc(add_step, 1)

        @block.tensor
        def _(pe):
            pe.wait_ge(const_step, 5)
            pe.wait_ge(ld_ctx, 16 * 4)
            for k in range(KC):
                nc.tensor.transpose(bank[0][:, k * P:(k + 1) * P], ctx_sb[:, k * P:(k + 1) * P], ident[:, :])
            nc.tensor.transpose(bank[0][:, 256:256 + 3 * HP], bias_rows[:, :], ident[0:3 * HP, 0:3 * HP]).then_inc(ctxT_ps, 1)
            pe.wait_ge(ctxT_done, 3)

            def project(W_sb, loaded):
                for g in range(NG):
                    pe.wait_ge(*loaded[g])
                    for c in range(g * GC, (g + 1) * GC):
                        for k in range(KC):
                            mm = nc.tensor.matmul(bank[4 + g][:, (c % GC) * P:(c % GC + 1) * P],
                                                  W_sb[:, k, c * P:(c + 1) * P], ctxT[:, k, :],
                                                  start=(k == 0), stop=(k == KC - 1))
                    mm.then_inc(kv_ps, 1)

            for j in range(HP // 2):
                if j % NG == 0:
                    pe.wait_ge(ld_q[j // NG], 16)
                for c in (2 * j, 2 * j + 1):
                    for k in range(KC):
                        mm = nc.tensor.transpose(bank[j][:, (c % 2) * D + k * P:(c % 2) * D + (k + 1) * P],
                                                 Wq_sb[:, k, c * P:(c + 1) * P], ident[:, :])
                mm.then_inc(wqT_ps, 1)
            project(Wk_sb, [(s, 16) for s in ld_k])
            for kc in range(KC):
                for j in range(FOLD_JOBS):
                    n = kc * FOLD_JOBS + j
                    if kc == 0:
                        pe.wait_ge(wqT_done, j + 1)
                        pe.wait_ge(kv_done, 2 * (j // 2) + 2)
                    for c in (2 * j, 2 * j + 1):
                        mm = nc.tensor.matmul(fold_bank(n)[:, (c % 2) * 256:(c % 2) * 256 + 256],
                                              WqT[:, c, kc * P:(kc + 1) * P], kT[c // GC][:, c % GC, :, :],
                                              start=True, stop=True)
                    mm.then_inc(A_ps, 1)
            for j in range(FOLD_JOBS):
                pe.wait_ge(A_done, j + 1)
                for c in (2 * j, 2 * j + 1):
                    mm = nc.tensor.matmul(fold_bank(j)[0:64, (c % 2) * 256:(c % 2) * 256 + 256],
                                          bias_cols[:, c:c + 1].to_broadcast([P, 64]), kT[c // GC][:, c % GC, :, :],
                                          start=True, stop=True)
                mm.then_inc(sbias_ps, 1)
            pe.wait_ge(A_done, KC * FOLD_JOBS)
            project(Wv_sb, [(ld_vo, 32)] * NG)
            pe.wait_ge(sbias_done, FOLD_JOBS)
            pe.wait_ge(const_pick, 4)

            def fold_v():
                pe.wait_ge(kv_done, 4 * NG)
                for c in range(HP):
                    after(pe, B_done, c - 4)
                    for b in range(B):
                        mm = nc.tensor.matmul(B_BANKS[c % 5][:, b * D:(b + 1) * D], vT[:, c, b, :], Wo_sb[:, c, :],
                                              start=True, stop=True)
                    mm.then_inc(B_ps, 1)

            def between(t):
                if t == 0:
                    pe.wait_ge(B_done, HP)
                if t == 2:
                    pe.wait_ge(wsh_done, 2)

            def split_product(out_ap, a_hi, a_lo, b_hi, b_lo, first, last):
                nc.tensor.matmul(out_ap, a_hi, b_hi, start=first, stop=False)
                nc.tensor.matmul(out_ap, a_hi, b_lo, start=False, stop=False)
                return nc.tensor.matmul(out_ap, a_lo, b_hi, start=False, stop=last)

            def shared_up(v, q):
                pe.wait_ge(x2T_lo_done, v + 1)
                after(pe, hid_done, v)
                after(pe, logit_done, v)
                for k in range(KC):
                    mm = split_product(h_ps[:, 0:2 * F + E], xn2T_hi[q][:, k, :], xn2T_lo[q][:, k, :],
                                       Wsh_hi[:, k, :], Wsh_lo[:, k, :], k == 0, k == KC - 1)
                mm.then_inc(h_done, 1)

            def shared_transpose(v):
                pe.wait_ge(hid_done, v + 1)
                after(pe, yscale_done, v)
                for k in range(2):
                    mm = nc.tensor.transpose(hy_ps[0:FH, k * P:(k + 1) * P], hid[:, k * FH:(k + 1) * FH], ident[:, :])
                mm.then_inc(hT_done, 1)

            def attention(t):
                after(pe, x2_done, t)
                b = t // TB
                for c in range(HP):
                    if c % 4 == 0:
                        pe.wait_ge(pT_lo_done, 2 * t + c // 4 + 1)
                    mm = split_product(att_ps[:, 0:D], pT_hi[:, c, :], pT_lo[:, c, :],
                                       B_hi[:, bass.ds(b, 1), c, :], B_lo[:, bass.ds(b, 1), c, :],
                                       c == 0, c == HP - 1)
                mm.then_inc(att_done, 1)

            def shared_down(v):
                pe.wait_ge(hT_lo_done, v + 1)
                for k in range(2):
                    mm = split_product(hy_ps[:, 0:D], hT_hi[:, k, :], hT_lo[:, k, :],
                                       Wds_hi[:, k, :], Wds_lo[:, k, :], k == 0, k == 1)
                mm.then_inc(y_done, 1)

            def step(t, q, i):
                u, v, w = t + 2, t - 2, t - 1
                if inside(u):
                    pe.wait_ge(xn_done, u + 1)
                    after(pe, xT_lo_done, u)
                    after(pe, x2T_lo_done, t - 1)
                    for k in range(KC):
                        mm = nc.tensor.transpose(xT_ps[:, k * P:(k + 1) * P], xn[q][:, k * P:(k + 1) * P], ident[:, :])
                    mm.then_inc(xT_done, 1)
                if isinstance(t, int) and t == -1:
                    fold_v()
                if inside(t):
                    pe.wait_ge(norm_done, t + 1)
                    for h in range(2):
                        after(pe, pT_lo_done, 2 * t - 1 + h)
                        for c in range(4):
                            mm = nc.tensor.transpose(pT_ps[h][:, c * P:(c + 1) * P],
                                                     prob[q][:, (4 * h + c) * P:(4 * h + c + 1) * P], ident[:, :])
                        mm.then_inc(pT_done, 1)
                if inside(v) and not (isinstance(t, int) and t == T + 1):
                    shared_up(v, q)
                if inside(u):
                    pe.wait_ge(xT_lo_done, u + 1)
                    after(pe, sub_done, u)
                    b = u // TB
                    for half in range(2):
                        cols = slice(half * 512, half * 512 + 512)
                        acc = scores_ps[:, cols]
                        nc.tensor.matmul(acc, pick_rows[:, :], score_bias[:, bass.ds(b, 1), cols], start=True, stop=False)
                        for k in range(KC):
                            mm = split_product(acc, xnT_hi[q][:, k, :], xnT_lo[q][:, k, :],
                                               A_hi[:, bass.ds(b, 1), k, cols], A_lo[:, bass.ds(b, 1), k, cols],
                                               False, k == KC - 1)
                    mm.then_inc(scores_done, 1)
                def transpose_xn2():
                    if inside(w):
                        pe.wait_ge(xn2_done, w + 1)
                        if isinstance(t, int):
                            pe.wait_ge(xT_lo_done, min(t + 3, T))
                        else:
                            pe.wait_ge(xT_lo_done, t + 3)
                        for k in range(KC):
                            mm = nc.tensor.transpose(xT_ps[:, k * P:(k + 1) * P], xn2[1 - q][:, k * P:(k + 1) * P], ident[:, :])
                        mm.then_inc(x2T_done, 1)

                if isinstance(t, int) and t >= T - 1:
                    if t == T - 1:
                        attention(t)
                        shared_transpose(v)
                        transpose_xn2()
                        shared_down(v)
                    if t == T:
                        transpose_xn2()
                        shared_transpose(v)
                        shared_up(v + 1, 1 - q)
                        shared_down(v)
                    return
                if inside(v):
                    shared_transpose(v)
                transpose_xn2()
                if inside(t):
                    attention(t)
                if inside(v):
                    shared_down(v)

            token_loop(pe, step, between)

            pe.wait_ge(mask_done, 2)
            flat = mask[:, :, :].rearrange("p t e -> p (t e)")
            flat_upto = upto[1][:, :, :].rearrange("p t e -> p (t e)")
            nc.tensor.matmul(count_ps, ones_r[:, :], flat_upto[:, (T - 1) * E:T * E], start=True, stop=True)
            nc.tensor.matmul(rank_flat, upper[:, :], flat, start=True, stop=False, skip_group_check=True)
            nc.tensor.matmul(rank_flat[:, E:T * E], ones_r[:, :], flat_upto[:, 0:(T - 1) * E],
                             start=False, stop=True, skip_group_check=True).then_inc(rank_ps_done, 1)
            shared_transpose(T - 1)
            pe.wait_ge(x2T_lo_done, T)
            for g in range(GROUPS):
                pe.wait_ge(hot_place_done, g + 1)
                pe.wait_ge(hot_row_done, g + 1)
                for n in range(g * NPG, (g + 1) * NPG):
                    mm = nc.tensor.matmul(table_ps, onehot_p[:, n, :], onehot_q[:, n, :],
                                          start=(n == 0), stop=(n == TOPK * T - 1))
            mm.then_inc(table_ps_done, 1)
            shared_down(T - 1)
            pe.wait_ge(tile_row_done, 1)
            pe.wait_ge(w_lo_done, E)
            pe.wait_ge(wd_lo_done, 4)
            pe.wait_ge(src_done, 1)

            row_regs = [pe.alloc_register(f"row{r}") for r in range(2 * RING)]
            rows = []

            def expert_step(j, k, i):
                n, y, d = j + 1, j - 2, j - 1
                kn = (k + 1) % RING
                if k == 0 and (i is not None or j >= 0):
                    pe.load(row_regs, tile_row[0:1, bass.ds(j, 2 * RING)])
                    rows[:] = [pe.snap(r, min_val=0, max_val=KC * (E - 1)) for r in row_regs]
                if in_tiles(y):
                    y_row = rows[RING + k - 2]
                if in_tiles(j):
                    h_row = rows[RING + k]
                if in_tiles(n):
                    after(pe, gathered[kn], 16 * (ring_turn(j, k, i, 1) + 1))
                    after(pe, gT_lo_done, n - 1)
                    for c in range(KC):
                        mm = nc.tensor.transpose(gT_ps[(k + 1) % 2][:, c * P:(c + 1) * P], xg[kn][:, c * P:(c + 1) * P], ident[:, :])
                    mm.then_inc(gT_done, 1)
                if in_tiles(j):
                    pe.wait_ge(gT_lo_done, j + 1)
                    after(pe, ehid_done, j - 1)
                    for c in range(KC):
                        mm = split_product(eh_ps[k % 2][:, 0:2 * F], xnT_hi[k % 2][:, c, :], xnT_lo[k % 2][:, c, :],
                                           W_hi[:, bass.ds(h_row + c, 1), :], W_lo[:, bass.ds(h_row + c, 1), :],
                                           c == 0, c == KC - 1)
                    mm.then_inc(eh_done, 1)
                if isinstance(j, int) and d == 0:
                    pe.wait_ge(yscale_done, T)
                if in_tiles(d):
                    pe.wait_ge(ehid_done, d + 1)
                    after(pe, ehT_lo_done, d - 1)
                    for c in range(2):
                        mm = nc.tensor.transpose(ehT_ps[(k + 1) % 2][0:FH, c * P:(c + 1) * P], hid[:, c * FH:(c + 1) * FH], ident[:, :])
                    mm.then_inc(ehT_done, 1)
                if in_tiles(y):
                    pe.wait_ge(ehT_lo_done, y + 1)
                    after(pe, ycopy_done, y - 1)
                    for c in range(2):
                        mm = split_product(ey_ps[k % 2][:, 0:D], hT_hi[:, c, :], hT_lo[:, c, :],
                                           Wd_hi[:, bass.ds(y_row + c, 1), :], Wd_lo[:, bass.ds(y_row + c, 1), :],
                                           c == 0, c == 1)
                    mm.then_inc(ey_done, 1)

            expert_loop(pe, expert_step)


_INS = ['x', 'ctx_1024', 'g_xattn', 'g_ffn', 'L0_xattn_Wq', 'L0_xattn_bq', 'L0_xattn_Wk', 'L0_xattn_bk',
        'L0_xattn_Wv', 'L0_xattn_bv', 'L0_xattn_Wo', 'L0_xattn_bo', 'L0_ffn_W_gate_router', 'L0_ffn_expert_bias',
        'L0_ffn_Wg', 'L0_ffn_Wu', 'L0_ffn_Wd', 'L0_ffn_Wg_s', 'L0_ffn_Wu_s', 'L0_ffn_Wd_s']


def kernel(**inputs):
    import numpy as _np
    import concourse.bacc as _bacc
    from concourse import mybir as _mybir
    from concourse.bass_utils import run_bass_kernel_spmd as _run

    nc = _bacc.Bacc("TRN2", target_bir_lowering=False, num_devices=1)
    arrays, args = {}, []
    for name in _INS:
        a = _np.ascontiguousarray(inputs[name])
        arrays[f"in_{name}_dram"] = a
        args.append(nc.dram_tensor(f"in_{name}_dram", a.shape, _mybir.dt.from_np(a.dtype), kind="ExternalInput").ap())
    args.append(nc.dram_tensor("out_dram", (B, SEQ, D), F32, kind="ExternalOutput").ap())
    flamingo_layer(nc, *args)
    r = _run(nc, [arrays], core_ids=[0])
    return r.results[0]["out_dram"]
```
